# Optimizing a Trainium2 kernel written in Bass

```python
import numpy as np
import jax
import jax.numpy as jnp

def _softmax(x, axis=-1):
    return jax.nn.softmax(x, axis=axis)

def _gelu(x):
    return jax.nn.gelu(x, approximate=True)

def _silu(x):
    return jax.nn.silu(x)

def _sigmoid(x):
    return jax.nn.sigmoid(x)

def _layernorm(x, axis=-1, eps=1e-05):
    m = jnp.mean(x, axis=axis, keepdims=True)
    v = jnp.var(x, axis=axis, keepdims=True)
    return (x - m) / jnp.sqrt(v + eps)

def _scatter_add(tgt, idx, src, axis=0):
    return tgt.at[idx].add(src)

def _segment_sum(src, seg, n):
    return jax.ops.segment_sum(src, seg, n)
kernel_name = 'mk_perceiver_d4_seqx_r4_96a312'

def setup_inputs(seed: int=0):
    np.random.seed(seed)
    _w = jnp.asarray

    def _rec_inputs():
        import jax
        import jax.numpy as jnp
        _rk = jax.random.key(seed)
        x = -0.0002928 + 1 * jax.random.normal(jax.random.fold_in(_rk, 1), (8, 64, 256), jnp.float32)
        _lenS = 64 - jax.random.randint(jax.random.fold_in(_rk, 7), (8,), 0, max(1, 64 // 4) + 1, jnp.int32)
        _lenS2 = 1601 - jax.random.randint(jax.random.fold_in(_rk, 8), (8,), 0, max(1, 1601 // 4) + 1, jnp.int32)
        _ctx_512P = jax.random.normal(jax.random.fold_in(_rk, 11), (8, 16, 128), jnp.float32)
        _ctx_512c = jax.random.dirichlet(jax.random.fold_in(_rk, 511), 0.3 * jnp.ones((16,), jnp.float32), (8, 1601))
        _ctx_512t = jnp.einsum('bsk,bkd->bsd', _ctx_512c, _ctx_512P)
        _ctx_512t = _ctx_512t * jax.lax.rsqrt(jnp.mean(jnp.square(_ctx_512t)) + 1e-12) * 0.953939
        ctx_512 = 0.00222621 + 0.99962 * (_ctx_512t + 0.3 * jax.random.normal(jax.random.fold_in(_rk, 611), (8, 1601, 128), jnp.float32))
        return (x, ctx_512)
    x, ctx_512 = _rec_inputs()

    def _L0_xattn_setup():
        import jax, jax.numpy as jnp
        import numpy as np
        H, D, C1, C2, S, M, B, W = (16, 32, 256, 128, 512, 128, 2, 4)

        def _ln(x, g, b):
            m = jnp.mean(x, -1, keepdims=True)
            v = jnp.var(x, -1, keepdims=True)
            return (x - m) * jax.lax.rsqrt(v + 1e-05) * g + b

        def _mha(x, y, wq, wk, wv, li1_w, li1_b, lnx_g, lnx_b, lny_g, lny_b, ln3_g, ln3_b, li2_w, li2_b, li3_w, li3_b, causal):
            xn = _ln(x, lnx_g, lnx_b)
            yn = _ln(y, lny_g, lny_b)
            q = jnp.einsum('bsc,hcd->bhsd', xn, wq)
            k = jnp.einsum('btc,hcd->bhtd', yn, wk)
            v = jnp.einsum('btc,hcd->bhtd', yn, wv)
            a = jax.nn.softmax(jnp.einsum('bhsd,bhtd->bhst', q, k) * D ** (-0.5), axis=-1)
            if causal:
                s, t = (a.shape[-2], a.shape[-1])
                mask = (jnp.arange(t)[None, :] > jnp.arange(s)[:, None]).astype(a.dtype)
                a = a * mask
            o = jnp.einsum('bhst,bhtd->bhsd', a, v)
            o = o.transpose(0, 2, 1, 3).reshape(x.shape[0], x.shape[1], H * D)
            x_out = x + o @ li1_w + li1_b
            h = jax.nn.gelu(_ln(x_out, ln3_g, ln3_b) @ li2_w + li2_b, approximate=False)
            return x_out + h @ li3_w + li3_b
        key = jax.random.key(seed)
        ks = iter(jax.random.split(key, 64))

        def w(shape, scale=0.02):
            return jax.random.normal(next(ks), shape, jnp.float32) * scale
        inp = {'xx': jax.random.normal(next(ks), (B, S, C1), jnp.float32), 'ee': jax.random.normal(next(ks), (B, M, C2), jnp.float32), 'ln1_g': jnp.ones(C1, jnp.float32), 'ln1_b': jnp.zeros(C1, jnp.float32), 'ln2_g': jnp.ones(C1, jnp.float32), 'ln2_b': jnp.zeros(C1, jnp.float32)}
        for pfx, cy in (('a1', C1), ('a2', C2)):
            inp[pfx + '_wq'] = w((H, C1, D))
            inp[pfx + '_wk'] = w((H, cy, D))
            inp[pfx + '_wv'] = w((H, cy, D))
            inp[pfx + '_li1_w'] = w((H * D, C1))
            inp[pfx + '_li1_b'] = jnp.zeros(C1, jnp.float32)
            inp[pfx + '_lnx_g'] = jnp.ones(C1, jnp.float32)
            inp[pfx + '_lnx_b'] = jnp.zeros(C1, jnp.float32)
            inp[pfx + '_lny_g'] = jnp.ones(cy, jnp.float32)
            inp[pfx + '_lny_b'] = jnp.zeros(cy, jnp.float32)
            inp[pfx + '_ln3_g'] = jnp.ones(C1, jnp.float32)
            inp[pfx + '_ln3_b'] = jnp.zeros(C1, jnp.float32)
            inp[pfx + '_li2_w'] = w((C1, C1 * W))
            inp[pfx + '_li2_b'] = jnp.zeros(C1 * W, jnp.float32)
            inp[pfx + '_li3_w'] = w((C1 * W, C1))
            inp[pfx + '_li3_b'] = jnp.zeros(C1, jnp.float32)
        inp['training'] = 0
        return inp
    _L0_xattn_all = _L0_xattn_setup()
    _L0_xattn_in = {k: v for k, v in _L0_xattn_all.items() if k in ('ln1_g', 'ln1_b', 'ln2_g', 'ln2_b', 'a1_wq', 'a1_wk', 'a1_wv', 'a1_li1_w', 'a1_li1_b', 'a1_lnx_g', 'a1_lnx_b', 'a1_lny_g', 'a1_lny_b', 'a1_ln3_g', 'a1_ln3_b', 'a1_li2_w', 'a1_li2_b', 'a1_li3_w', 'a1_li3_b', 'a2_wq', 'a2_wk', 'a2_wv', 'a2_li1_w', 'a2_li1_b', 'a2_lnx_g', 'a2_lnx_b', 'a2_lny_g', 'a2_lny_b', 'a2_ln3_g', 'a2_ln3_b', 'a2_li2_w', 'a2_li2_b', 'a2_li3_w', 'a2_li3_b')}
    del _L0_xattn_all

    def _L0_attn_setup():
        import jax, jax.numpy as jnp
        import numpy as np
        EPS = 1e-05

        def _apply_rope(t, cos, sin):
            B, H, S, D = t.shape
            tr = t.reshape(B, H, S, D // 2, 2)
            x0, x1 = (tr[..., 0], tr[..., 1])
            r0 = x0 * cos - x1 * sin
            r1 = x0 * sin + x1 * cos
            return jnp.stack([r0, r1], axis=-1).reshape(B, H, S, D)
        key = jax.random.key(seed)
        ks = jax.random.split(key, 3)
        B, S, DM = (2, 512, 256)
        return {'x': jax.random.normal(ks[0], (B, S, DM), jnp.float32), 'Wqkv': jax.random.normal(ks[1], (DM, 3 * DM), jnp.float32) * 0.02, 'bqkv': jnp.zeros((3 * DM,), jnp.float32), 'Wo': jax.random.normal(ks[2], (DM, DM), jnp.float32) * 0.02, 'bo': jnp.zeros((DM,), jnp.float32), 'gamma': jnp.ones((DM,), jnp.float32), 'beta': jnp.zeros((DM,), jnp.float32)}
    _L0_attn_all = _L0_attn_setup()
    _L0_attn_in = {k: v for k, v in _L0_attn_all.items() if k in ('Wqkv', 'bqkv', 'Wo', 'bo', 'gamma', 'beta')}
    del _L0_attn_all

    def _L0_ffn_setup():
        import jax, jax.numpy as jnp
        import numpy as np
        B, T, C = (4, 512, 256)
        E = 8
        K = 2
        H = 352
        HS = 352 * 2
        key = jax.random.key(seed)
        k = jax.random.split(key, 8)
        s = 0.02
        return {'x': jax.random.normal(k[0], (B, T, C), jnp.float32), 'Wg': jax.random.normal(k[1], (C, E), jnp.float32) * s, 'W1': jax.random.normal(k[2], (E, C, H), jnp.float32) * s, 'W2': jax.random.normal(k[3], (E, C, H), jnp.float32) * s, 'W3': jax.random.normal(k[4], (E, H, C), jnp.float32) * s, 'Ws1': jax.random.normal(k[5], (C, HS), jnp.float32) * s, 'Ws2': jax.random.normal(k[6], (C, HS), jnp.float32) * s, 'Ws3': jax.random.normal(k[7], (HS, C), jnp.float32) * s}
    _L0_ffn_all = _L0_ffn_setup()
    _L0_ffn_in = {k: v for k, v in _L0_ffn_all.items() if k in ('Wg', 'W1', 'W2', 'W3', 'Ws1', 'Ws2', 'Ws3')}
    del _L0_ffn_all

    def _L1_xattn_setup():
        import jax, jax.numpy as jnp
        import numpy as np
        B, LQ, LK = (8, 512, 512)
        QD, KD, VD = (256, 128, 128)
        key = jax.random.key(seed)
        ks = jax.random.split(key, 9)
        s = 0.02
        return {'query': jax.random.normal(ks[0], (B, LQ, QD), jnp.float32), 'key': jax.random.normal(ks[1], (B, LK, KD), jnp.float32), 'value': jax.random.normal(ks[2], (B, LK, VD), jnp.float32), 'Wq': jax.random.normal(ks[3], (QD, QD), jnp.float32) * s, 'bq': jnp.zeros((QD,), jnp.float32), 'Wk': jax.random.normal(ks[4], (KD, QD), jnp.float32) * s, 'bk': jnp.zeros((QD,), jnp.float32), 'Wv': jax.random.normal(ks[5], (VD, QD), jnp.float32) * s, 'bv': jnp.zeros((QD,), jnp.float32)}
    _L1_xattn_all = _L1_xattn_setup()
    _L1_xattn_in = {k: v for k, v in _L1_xattn_all.items() if k in ('Wq', 'bq', 'Wk', 'bk', 'Wv', 'bv')}
    del _L1_xattn_all

    def _L1_attn_setup():
        import jax, jax.numpy as jnp
        import numpy as np
        import math
        N_EMBD = 256
        DIM_ATT = 256
        N_LAYER = 24
        LAYER_ID = 12
        B, T = (4, 1024)

        def _init_params():
            r01 = LAYER_ID / (N_LAYER - 1)
            r1a0 = 1.0 - LAYER_ID / N_LAYER
            ddd = np.arange(N_EMBD, dtype=np.float32) / N_EMBD
            h = np.arange(DIM_ATT, dtype=np.float32)
            decay_speed = -5.0 + 8.0 * (h / (DIM_ATT - 1)) ** (0.7 + 1.3 * r01)
            zigzag = ((np.arange(DIM_ATT) + 1) % 3 - 1).astype(np.float32) * 0.5
            time_first = np.float32(math.log(0.3)) + zigzag
            return {'time_decay': jnp.asarray(decay_speed, jnp.float32), 'time_first': jnp.asarray(time_first, jnp.float32), 'time_mix_k': jnp.asarray(ddd ** r1a0, jnp.float32), 'time_mix_v': jnp.asarray(ddd ** r1a0 + 0.3 * r01, jnp.float32), 'time_mix_r': jnp.asarray(ddd ** (0.5 * r1a0), jnp.float32)}

        def _wkv(w, u, k, v):

            def step(carry, kv):
                aa, bb, pp = carry
                kt, vt = kv
                ww = u + kt
                p = jnp.maximum(pp, ww)
                e1 = jnp.exp(pp - p)
                e2 = jnp.exp(ww - p)
                y = (e1 * aa + e2 * vt) / (e1 * bb + e2)
                ww2 = pp + w
                p2 = jnp.maximum(ww2, kt)
                e1b = jnp.exp(ww2 - p2)
                e2b = jnp.exp(kt - p2)
                return ((e1b * aa + e2b * vt, e1b * bb + e2b, p2), y)
            Bb, Tt, C = k.shape
            init = (jnp.zeros((Bb, C), k.dtype), jnp.zeros((Bb, C), k.dtype), jnp.full((Bb, C), -1e+38, k.dtype))
            _, ys = jax.lax.scan(step, init, (jnp.swapaxes(k, 0, 1), jnp.swapaxes(v, 0, 1)))
            return jnp.swapaxes(ys, 0, 1)
        key = jax.random.key(seed)
        ks = jax.random.split(key, 5)
        inp = {'x': jax.random.normal(ks[0], (B, T, N_EMBD), jnp.float32)}
        inp.update(_init_params())
        s = 1.0 / math.sqrt(N_EMBD)
        inp['Wk'] = jax.random.normal(ks[1], (DIM_ATT, N_EMBD), jnp.float32) * s
        inp['Wv'] = jax.random.normal(ks[2], (DIM_ATT, N_EMBD), jnp.float32) * s
        inp['Wr'] = jax.random.normal(ks[3], (DIM_ATT, N_EMBD), jnp.float32) * s
        inp['Wo'] = jax.random.normal(ks[4], (N_EMBD, DIM_ATT), jnp.float32) * (1.0 / math.sqrt(DIM_ATT))
        return inp
    _L1_attn_all = _L1_attn_setup()
    _L1_attn_in = {k: v for k, v in _L1_attn_all.items() if k in ('time_decay', 'time_first', 'time_mix_k', 'time_mix_v', 'time_mix_r', 'Wk', 'Wv', 'Wr', 'Wo')}
    del _L1_attn_all

    def _L1_ffn_setup():
        import jax, jax.numpy as jnp
        import numpy as np
        TOP_K = 2
        CAPACITY_FACTOR = 1.0
        key = jax.random.key(seed)
        ks = jax.random.split(key, 4)
        sl, bs, hs, ffn, E = (512, 8, 256, 1024, 8)
        x = jax.random.normal(ks[0], (sl, bs, hs), dtype=jnp.float32)
        w_router = jax.random.normal(ks[1], (hs, E), dtype=jnp.float32) * 0.02
        w1 = jax.random.normal(ks[2], (E, hs, ffn), dtype=jnp.float32) * 0.02
        w2 = jax.random.normal(ks[3], (E, ffn, hs), dtype=jnp.float32) * 0.02
        bias = jnp.zeros((1, 1, hs), dtype=jnp.float32)
        return {'x': x, 'w_router': w_router, 'w1': w1, 'w2': w2, 'bias': bias}
    _L1_ffn_all = _L1_ffn_setup()
    _L1_ffn_in = {k: v for k, v in _L1_ffn_all.items() if k in ('w_router', 'w1', 'w2', 'bias')}
    del _L1_ffn_all

    def _L2_xattn_setup():
        import jax, jax.numpy as jnp
        import numpy as np
        NUM_HEADS = 16
        HEAD_DIM = 64
        Q_DIM = 256
        KV_DIM = 128
        INNER = NUM_HEADS * HEAD_DIM
        key = jax.random.key(seed)
        ks = jax.random.split(key, 7)
        B, N, M = (32, 128, 512)
        q = jax.random.normal(ks[0], (B, N, Q_DIM), dtype=jnp.float32)
        kv = jax.random.normal(ks[1], (B, M, KV_DIM), dtype=jnp.float32)
        Wq = jax.random.normal(ks[2], (Q_DIM, INNER), dtype=jnp.float32) / np.sqrt(Q_DIM)
        Wk = jax.random.normal(ks[3], (KV_DIM, INNER), dtype=jnp.float32) / np.sqrt(KV_DIM)
        Wv = jax.random.normal(ks[4], (KV_DIM, INNER), dtype=jnp.float32) / np.sqrt(KV_DIM)
        Wo = jax.random.normal(ks[5], (INNER, Q_DIM), dtype=jnp.float32) / np.sqrt(INNER)
        bo = jax.random.normal(ks[6], (Q_DIM,), dtype=jnp.float32) * 0.01
        return {'q': q, 'kv': kv, 'Wq': Wq, 'Wk': Wk, 'Wv': Wv, 'Wo': Wo, 'bo': bo}
    _L2_xattn_all = _L2_xattn_setup()
    _L2_xattn_in = {k: v for k, v in _L2_xattn_all.items() if k in ('Wq', 'Wk', 'Wv', 'Wo', 'bo')}
    del _L2_xattn_all

    def _L2_attn_setup():
        import jax, jax.numpy as jnp
        import numpy as np
        SEQLEN, K, OLDK, HEADS = (512, 256, 256, 16)
        BASE = 10000.0

        def rope(x):
            t = x.shape[1]
            half = K // 2
            theta = 1.0 / BASE ** (jnp.arange(half, dtype=jnp.float32) / half)
            ang = jnp.arange(t, dtype=jnp.float32)[:, None] * theta[None, :]
            cos, sin = (jnp.cos(ang), jnp.sin(ang))
            xr = x.reshape(x.shape[0], t, half, 2)
            xe, xo = (xr[..., 0], xr[..., 1])
            re = xe * cos - xo * sin
            im = xe * sin + xo * cos
            return jnp.stack([re, im], axis=-1).reshape(x.shape)
        key = jax.random.key(seed)
        ks = jax.random.split(key, 5)
        b = 4
        x = jax.random.normal(ks[0], (b, SEQLEN, OLDK), jnp.float32)
        sc_in = 1.0 / np.sqrt(OLDK).astype(np.float32)
        Wq = jax.random.normal(ks[1], (K, OLDK), jnp.float32) * sc_in
        Wk = jax.random.normal(ks[2], (K, OLDK), jnp.float32) * sc_in
        Wv = jax.random.normal(ks[3], (K, OLDK), jnp.float32) * sc_in
        Wu = jax.random.normal(ks[4], (K, K), jnp.float32) * (1.0 / np.sqrt(K).astype(np.float32))
        bu = jnp.zeros((K,), jnp.float32)
        return {'x': x, 'Wq': Wq, 'Wk': Wk, 'Wv': Wv, 'Wu': Wu, 'bu': bu}
    _L2_attn_all = _L2_attn_setup()
    _L2_attn_in = {k: v for k, v in _L2_attn_all.items() if k in ('Wq', 'Wk', 'Wv', 'Wu', 'bu')}
    del _L2_attn_all

    def _L2_ffn_setup():
        import jax, jax.numpy as jnp
        import numpy as np
        from jax import lax
        D_MODEL = 256
        INTER = 256
        N_EXPERTS = 8
        TOP_K = 2
        ROUTE_SCALE = 1.0
        B, S = (2, 1024)
        key = jax.random.key(seed)
        ks = jax.random.split(key, 16)
        sc_d = 1.0 / np.sqrt(D_MODEL)
        sc_f = 1.0 / np.sqrt(INTER)
        inp = {'x': jax.random.normal(ks[0], (B, S, D_MODEL), dtype=jnp.float32), 'gate_w': jax.random.normal(ks[1], (N_EXPERTS, D_MODEL), dtype=jnp.float32) * sc_d, 'w1': jax.random.normal(ks[2], (N_EXPERTS, D_MODEL, INTER), dtype=jnp.float32) * sc_d, 'b1': jnp.zeros((N_EXPERTS, INTER), dtype=jnp.float32), 'w2': jax.random.normal(ks[3], (N_EXPERTS, INTER, D_MODEL), dtype=jnp.float32) * sc_f, 'b2': jnp.zeros((N_EXPERTS, D_MODEL), dtype=jnp.float32), 'w3': jax.random.normal(ks[4], (N_EXPERTS, D_MODEL, INTER), dtype=jnp.float32) * sc_d, 'b3': jnp.zeros((N_EXPERTS, INTER), dtype=jnp.float32), 'sw1': jax.random.normal(ks[5], (D_MODEL, INTER), dtype=jnp.float32) * sc_d, 'sb1': jnp.zeros((INTER,), dtype=jnp.float32), 'sw2': jax.random.normal(ks[6], (INTER, D_MODEL), dtype=jnp.float32) * sc_f, 'sb2': jnp.zeros((D_MODEL,), dtype=jnp.float32), 'sw3': jax.random.normal(ks[7], (D_MODEL, INTER), dtype=jnp.float32) * sc_d, 'sb3': jnp.zeros((INTER,), dtype=jnp.float32)}
        return inp
    _L2_ffn_all = _L2_ffn_setup()
    _L2_ffn_in = {k: v for k, v in _L2_ffn_all.items() if k in ('gate_w', 'w1', 'b1', 'w2', 'b2', 'w3', 'b3', 'sw1', 'sb1', 'sw2', 'sb2', 'sw3', 'sb3')}
    del _L2_ffn_all

    def _L3_xattn_setup():
        import jax, jax.numpy as jnp
        import numpy as np
        DIM = 256
        LATENT_DIM = 128
        NUM_HEADS = 16
        HEAD_DIM = DIM // NUM_HEADS
        SCALE = HEAD_DIM ** (-0.5)
        key = jax.random.key(seed)
        k1, k2, k3, k4, k5 = jax.random.split(key, 5)
        B, xN, zN = (2, 512, 512)
        x = jax.random.normal(k1, (B, xN, DIM), dtype=jnp.float32)
        z = jax.random.normal(k2, (B, zN, LATENT_DIM), dtype=jnp.float32)
        Wq = jax.random.normal(k3, (DIM, DIM), dtype=jnp.float32) * DIM ** (-0.5)
        Wkv = jax.random.normal(k4, (2 * DIM, LATENT_DIM), dtype=jnp.float32) * LATENT_DIM ** (-0.5)
        Wo = jax.random.normal(k5, (DIM, DIM), dtype=jnp.float32) * DIM ** (-0.5)
        return {'x': x, 'z': z, 'Wq': Wq, 'Wkv': Wkv, 'Wo': Wo}
    _L3_xattn_all = _L3_xattn_setup()
    _L3_xattn_in = {k: v for k, v in _L3_xattn_all.items() if k in ('Wq', 'Wkv', 'Wo')}
    del _L3_xattn_all

    def _L3_attn_setup():
        import jax, jax.numpy as jnp
        import numpy as np
        EMB = 256
        HEADS = 16
        DEPTH = EMB // HEADS
        WINDOW = 64
        B, S = (1, 1024)
        key = jax.random.key(seed)
        ks = jax.random.split(key, 9)
        sc = 1.0 / np.sqrt(EMB)
        return {'x': jax.random.normal(ks[0], (B, S, EMB), dtype=jnp.float32), 'Wq': jax.random.normal(ks[1], (EMB, EMB), dtype=jnp.float32) * sc, 'bq': jax.random.normal(ks[2], (EMB,), dtype=jnp.float32) * 0.01, 'Wk': jax.random.normal(ks[3], (EMB, EMB), dtype=jnp.float32) * sc, 'bk': jax.random.normal(ks[4], (EMB,), dtype=jnp.float32) * 0.01, 'Wv': jax.random.normal(ks[5], (EMB, EMB), dtype=jnp.float32) * sc, 'bv': jax.random.normal(ks[6], (EMB,), dtype=jnp.float32) * 0.01, 'Wd': jax.random.normal(ks[7], (EMB, EMB), dtype=jnp.float32) * sc, 'bd': jax.random.normal(ks[8], (EMB,), dtype=jnp.float32) * 0.01}
    _L3_attn_all = _L3_attn_setup()
    _L3_attn_in = {k: v for k, v in _L3_attn_all.items() if k in ('Wq', 'bq', 'Wk', 'bk', 'Wv', 'bv', 'Wd', 'bd')}
    del _L3_attn_all

    def _L3_ffn_setup():
        import jax, jax.numpy as jnp
        import numpy as np
        HIDDEN = 256
        MOE_FF = 128
        SHARED_FF = 704
        NUM_EXPERTS = 16
        TOP_K = 2
        NORM_TOPK = True
        key = jax.random.key(seed)
        ks = jax.random.split(key, 8)
        s = 0.02
        return {'layer_input': jax.random.normal(ks[0], (1, 512, HIDDEN), dtype=jnp.float32), 'gate_w': jax.random.normal(ks[1], (NUM_EXPERTS, HIDDEN), dtype=jnp.float32) * s, 'w_gate_up': jax.random.normal(ks[2], (NUM_EXPERTS, HIDDEN, 2 * MOE_FF), dtype=jnp.float32) * s, 'w_down': jax.random.normal(ks[3], (NUM_EXPERTS, MOE_FF, HIDDEN), dtype=jnp.float32) * s, 'shared_w_gate': jax.random.normal(ks[4], (SHARED_FF, HIDDEN), dtype=jnp.float32) * s, 'shared_w_up': jax.random.normal(ks[5], (SHARED_FF, HIDDEN), dtype=jnp.float32) * s, 'shared_w_down': jax.random.normal(ks[6], (HIDDEN, SHARED_FF), dtype=jnp.float32) * s, 'shared_gate_w': jax.random.normal(ks[7], (1, HIDDEN), dtype=jnp.float32) * s}
    _L3_ffn_all = _L3_ffn_setup()
    _L3_ffn_in = {k: v for k, v in _L3_ffn_all.items() if k in ('gate_w', 'w_gate_up', 'w_down', 'shared_w_gate', 'shared_w_up', 'shared_w_down', 'shared_gate_w')}
    del _L3_ffn_all
    return {'x': x, 'ctx_512': ctx_512, 'L0_xattn_ln1_g': _L0_xattn_in['ln1_g'], 'L0_xattn_ln1_b': _L0_xattn_in['ln1_b'], 'L0_xattn_ln2_g': _L0_xattn_in['ln2_g'], 'L0_xattn_ln2_b': _L0_xattn_in['ln2_b'], 'L0_xattn_a1_wq': _L0_xattn_in['a1_wq'], 'L0_xattn_a1_wk': _L0_xattn_in['a1_wk'], 'L0_xattn_a1_wv': _L0_xattn_in['a1_wv'], 'L0_xattn_a1_li1_w': _L0_xattn_in['a1_li1_w'], 'L0_xattn_a1_li1_b': _L0_xattn_in['a1_li1_b'], 'L0_xattn_a1_lnx_g': _L0_xattn_in['a1_lnx_g'], 'L0_xattn_a1_lnx_b': _L0_xattn_in['a1_lnx_b'], 'L0_xattn_a1_lny_g': _L0_xattn_in['a1_lny_g'], 'L0_xattn_a1_lny_b': _L0_xattn_in['a1_lny_b'], 'L0_xattn_a1_ln3_g': _L0_xattn_in['a1_ln3_g'], 'L0_xattn_a1_ln3_b': _L0_xattn_in['a1_ln3_b'], 'L0_xattn_a1_li2_w': _L0_xattn_in['a1_li2_w'], 'L0_xattn_a1_li2_b': _L0_xattn_in['a1_li2_b'], 'L0_xattn_a1_li3_w': _L0_xattn_in['a1_li3_w'], 'L0_xattn_a1_li3_b': _L0_xattn_in['a1_li3_b'], 'L0_xattn_a2_wq': _L0_xattn_in['a2_wq'], 'L0_xattn_a2_wk': _L0_xattn_in['a2_wk'], 'L0_xattn_a2_wv': _L0_xattn_in['a2_wv'], 'L0_xattn_a2_li1_w': _L0_xattn_in['a2_li1_w'], 'L0_xattn_a2_li1_b': _L0_xattn_in['a2_li1_b'], 'L0_xattn_a2_lnx_g': _L0_xattn_in['a2_lnx_g'], 'L0_xattn_a2_lnx_b': _L0_xattn_in['a2_lnx_b'], 'L0_xattn_a2_lny_g': _L0_xattn_in['a2_lny_g'], 'L0_xattn_a2_lny_b': _L0_xattn_in['a2_lny_b'], 'L0_xattn_a2_ln3_g': _L0_xattn_in['a2_ln3_g'], 'L0_xattn_a2_ln3_b': _L0_xattn_in['a2_ln3_b'], 'L0_xattn_a2_li2_w': _L0_xattn_in['a2_li2_w'], 'L0_xattn_a2_li2_b': _L0_xattn_in['a2_li2_b'], 'L0_xattn_a2_li3_w': _L0_xattn_in['a2_li3_w'], 'L0_xattn_a2_li3_b': _L0_xattn_in['a2_li3_b'], 'L0_attn_Wqkv': _L0_attn_in['Wqkv'], 'L0_attn_bqkv': _L0_attn_in['bqkv'], 'L0_attn_Wo': _L0_attn_in['Wo'], 'L0_attn_bo': _L0_attn_in['bo'], 'L0_attn_gamma': _L0_attn_in['gamma'], 'L0_attn_beta': _L0_attn_in['beta'], 'L0_ffn_Wg': _L0_ffn_in['Wg'], 'L0_ffn_W1': _L0_ffn_in['W1'], 'L0_ffn_W2': _L0_ffn_in['W2'], 'L0_ffn_W3': _L0_ffn_in['W3'], 'L0_ffn_Ws1': _L0_ffn_in['Ws1'], 'L0_ffn_Ws2': _L0_ffn_in['Ws2'], 'L0_ffn_Ws3': _L0_ffn_in['Ws3'], 'L1_xattn_Wq': _L1_xattn_in['Wq'], 'L1_xattn_bq': _L1_xattn_in['bq'], 'L1_xattn_Wk': _L1_xattn_in['Wk'], 'L1_xattn_bk': _L1_xattn_in['bk'], 'L1_xattn_Wv': _L1_xattn_in['Wv'], 'L1_xattn_bv': _L1_xattn_in['bv'], 'L1_attn_time_decay': _L1_attn_in['time_decay'], 'L1_attn_time_first': _L1_attn_in['time_first'], 'L1_attn_time_mix_k': _L1_attn_in['time_mix_k'], 'L1_attn_time_mix_v': _L1_attn_in['time_mix_v'], 'L1_attn_time_mix_r': _L1_attn_in['time_mix_r'], 'L1_attn_Wk': _L1_attn_in['Wk'], 'L1_attn_Wv': _L1_attn_in['Wv'], 'L1_attn_Wr': _L1_attn_in['Wr'], 'L1_attn_Wo': _L1_attn_in['Wo'], 'L1_ffn_w_router': _L1_ffn_in['w_router'], 'L1_ffn_w1': _L1_ffn_in['w1'], 'L1_ffn_w2': _L1_ffn_in['w2'], 'L1_ffn_bias': _L1_ffn_in['bias'], 'L2_xattn_Wq': _L2_xattn_in['Wq'], 'L2_xattn_Wk': _L2_xattn_in['Wk'], 'L2_xattn_Wv': _L2_xattn_in['Wv'], 'L2_xattn_Wo': _L2_xattn_in['Wo'], 'L2_xattn_bo': _L2_xattn_in['bo'], 'L2_attn_Wq': _L2_attn_in['Wq'], 'L2_attn_Wk': _L2_attn_in['Wk'], 'L2_attn_Wv': _L2_attn_in['Wv'], 'L2_attn_Wu': _L2_attn_in['Wu'], 'L2_attn_bu': _L2_attn_in['bu'], 'L2_ffn_gate_w': _L2_ffn_in['gate_w'], 'L2_ffn_w1': _L2_ffn_in['w1'], 'L2_ffn_b1': _L2_ffn_in['b1'], 'L2_ffn_w2': _L2_ffn_in['w2'], 'L2_ffn_b2': _L2_ffn_in['b2'], 'L2_ffn_w3': _L2_ffn_in['w3'], 'L2_ffn_b3': _L2_ffn_in['b3'], 'L2_ffn_sw1': _L2_ffn_in['sw1'], 'L2_ffn_sb1': _L2_ffn_in['sb1'], 'L2_ffn_sw2': _L2_ffn_in['sw2'], 'L2_ffn_sb2': _L2_ffn_in['sb2'], 'L2_ffn_sw3': _L2_ffn_in['sw3'], 'L2_ffn_sb3': _L2_ffn_in['sb3'], 'L3_xattn_Wq': _L3_xattn_in['Wq'], 'L3_xattn_Wkv': _L3_xattn_in['Wkv'], 'L3_xattn_Wo': _L3_xattn_in['Wo'], 'L3_attn_Wq': _L3_attn_in['Wq'], 'L3_attn_bq': _L3_attn_in['bq'], 'L3_attn_Wk': _L3_attn_in['Wk'], 'L3_attn_bk': _L3_attn_in['bk'], 'L3_attn_Wv': _L3_attn_in['Wv'], 'L3_attn_bv': _L3_attn_in['bv'], 'L3_attn_Wd': _L3_attn_in['Wd'], 'L3_attn_bd': _L3_attn_in['bd'], 'L3_ffn_gate_w': _L3_ffn_in['gate_w'], 'L3_ffn_w_gate_up': _L3_ffn_in['w_gate_up'], 'L3_ffn_w_down': _L3_ffn_in['w_down'], 'L3_ffn_shared_w_gate': _L3_ffn_in['shared_w_gate'], 'L3_ffn_shared_w_up': _L3_ffn_in['shared_w_up'], 'L3_ffn_shared_w_down': _L3_ffn_in['shared_w_down'], 'L3_ffn_shared_gate_w': _L3_ffn_in['shared_gate_w']}

def reference(x, ctx_512, L0_xattn_ln1_g, L0_xattn_ln1_b, L0_xattn_ln2_g, L0_xattn_ln2_b, L0_xattn_a1_wq, L0_xattn_a1_wk, L0_xattn_a1_wv, L0_xattn_a1_li1_w, L0_xattn_a1_li1_b, L0_xattn_a1_lnx_g, L0_xattn_a1_lnx_b, L0_xattn_a1_lny_g, L0_xattn_a1_lny_b, L0_xattn_a1_ln3_g, L0_xattn_a1_ln3_b, L0_xattn_a1_li2_w, L0_xattn_a1_li2_b, L0_xattn_a1_li3_w, L0_xattn_a1_li3_b, L0_xattn_a2_wq, L0_xattn_a2_wk, L0_xattn_a2_wv, L0_xattn_a2_li1_w, L0_xattn_a2_li1_b, L0_xattn_a2_lnx_g, L0_xattn_a2_lnx_b, L0_xattn_a2_lny_g, L0_xattn_a2_lny_b, L0_xattn_a2_ln3_g, L0_xattn_a2_ln3_b, L0_xattn_a2_li2_w, L0_xattn_a2_li2_b, L0_xattn_a2_li3_w, L0_xattn_a2_li3_b, L0_attn_Wqkv, L0_attn_bqkv, L0_attn_Wo, L0_attn_bo, L0_attn_gamma, L0_attn_beta, L0_ffn_Wg, L0_ffn_W1, L0_ffn_W2, L0_ffn_W3, L0_ffn_Ws1, L0_ffn_Ws2, L0_ffn_Ws3, L1_xattn_Wq, L1_xattn_bq, L1_xattn_Wk, L1_xattn_bk, L1_xattn_Wv, L1_xattn_bv, L1_attn_time_decay, L1_attn_time_first, L1_attn_time_mix_k, L1_attn_time_mix_v, L1_attn_time_mix_r, L1_attn_Wk, L1_attn_Wv, L1_attn_Wr, L1_attn_Wo, L1_ffn_w_router, L1_ffn_w1, L1_ffn_w2, L1_ffn_bias, L2_xattn_Wq, L2_xattn_Wk, L2_xattn_Wv, L2_xattn_Wo, L2_xattn_bo, L2_attn_Wq, L2_attn_Wk, L2_attn_Wv, L2_attn_Wu, L2_attn_bu, L2_ffn_gate_w, L2_ffn_w1, L2_ffn_b1, L2_ffn_w2, L2_ffn_b2, L2_ffn_w3, L2_ffn_b3, L2_ffn_sw1, L2_ffn_sb1, L2_ffn_sw2, L2_ffn_sb2, L2_ffn_sw3, L2_ffn_sb3, L3_xattn_Wq, L3_xattn_Wkv, L3_xattn_Wo, L3_attn_Wq, L3_attn_bq, L3_attn_Wk, L3_attn_bk, L3_attn_Wv, L3_attn_bv, L3_attn_Wd, L3_attn_bd, L3_ffn_gate_w, L3_ffn_w_gate_up, L3_ffn_w_down, L3_ffn_shared_w_gate, L3_ffn_shared_w_up, L3_ffn_shared_w_down, L3_ffn_shared_gate_w):
    import jax
    import jax.numpy as jnp

    def _L0_xattn_ref(xx, ee, ln1_g, ln1_b, ln2_g, ln2_b, a1_wq, a1_wk, a1_wv, a1_li1_w, a1_li1_b, a1_lnx_g, a1_lnx_b, a1_lny_g, a1_lny_b, a1_ln3_g, a1_ln3_b, a1_li2_w, a1_li2_b, a1_li3_w, a1_li3_b, a2_wq, a2_wk, a2_wv, a2_li1_w, a2_li1_b, a2_lnx_g, a2_lnx_b, a2_lny_g, a2_lny_b, a2_ln3_g, a2_ln3_b, a2_li2_w, a2_li2_b, a2_li3_w, a2_li3_b, training):
        import jax, jax.numpy as jnp
        import numpy as np
        H, D, C1, C2, S, M, B, W = (16, 32, 256, 128, 512, 128, 2, 4)

        def _ln(x, g, b):
            m = jnp.mean(x, -1, keepdims=True)
            v = jnp.var(x, -1, keepdims=True)
            return (x - m) * jax.lax.rsqrt(v + 1e-05) * g + b

        def _mha(x, y, wq, wk, wv, li1_w, li1_b, lnx_g, lnx_b, lny_g, lny_b, ln3_g, ln3_b, li2_w, li2_b, li3_w, li3_b, causal):
            xn = _ln(x, lnx_g, lnx_b)
            yn = _ln(y, lny_g, lny_b)
            q = jnp.einsum('bsc,hcd->bhsd', xn, wq)
            k = jnp.einsum('btc,hcd->bhtd', yn, wk)
            v = jnp.einsum('btc,hcd->bhtd', yn, wv)
            a = jax.nn.softmax(jnp.einsum('bhsd,bhtd->bhst', q, k) * D ** (-0.5), axis=-1)
            if causal:
                s, t = (a.shape[-2], a.shape[-1])
                mask = (jnp.arange(t)[None, :] > jnp.arange(s)[:, None]).astype(a.dtype)
                a = a * mask
            o = jnp.einsum('bhst,bhtd->bhsd', a, v)
            o = o.transpose(0, 2, 1, 3).reshape(x.shape[0], x.shape[1], H * D)
            x_out = x + o @ li1_w + li1_b
            h = jax.nn.gelu(_ln(x_out, ln3_g, ln3_b) @ li2_w + li2_b, approximate=False)
            return x_out + h @ li3_w + li3_b
        x = _ln(xx, ln1_g, ln1_b)
        x = x + _mha(x, x, a1_wq, a1_wk, a1_wv, a1_li1_w, a1_li1_b, a1_lnx_g, a1_lnx_b, a1_lny_g, a1_lny_b, a1_ln3_g, a1_ln3_b, a1_li2_w, a1_li2_b, a1_li3_w, a1_li3_b, causal=True)
        x = _ln(x, ln2_g, ln2_b)
        return x + _mha(x, ee, a2_wq, a2_wk, a2_wv, a2_li1_w, a2_li1_b, a2_lnx_g, a2_lnx_b, a2_lny_g, a2_lny_b, a2_ln3_g, a2_ln3_b, a2_li2_w, a2_li2_b, a2_li3_w, a2_li3_b, causal=False)

    def _L0_attn_ref(x, Wqkv, bqkv, Wo, bo, gamma, beta):
        import jax, jax.numpy as jnp
        import numpy as np
        EPS = 1e-05

        def _apply_rope(t, cos, sin):
            B, H, S, D = t.shape
            tr = t.reshape(B, H, S, D // 2, 2)
            x0, x1 = (tr[..., 0], tr[..., 1])
            r0 = x0 * cos - x1 * sin
            r1 = x0 * sin + x1 * cos
            return jnp.stack([r0, r1], axis=-1).reshape(B, H, S, D)
        B, S, DM = x.shape
        H = 16
        D = DM // H
        qkv = (x @ Wqkv + bqkv).reshape(B, S, 3, H, D)
        qkv = jnp.transpose(qkv, (2, 0, 3, 1, 4))
        q, k, v = (qkv[0], qkv[1], qkv[2])
        inv_freq = 1.0 / 10000.0 ** (jnp.arange(0, D, 2, dtype=jnp.float32) / D)
        pos = jnp.arange(S, dtype=jnp.float32)
        freqs = pos[:, None] * inv_freq[None, :]
        cos, sin = (jnp.cos(freqs), jnp.sin(freqs))
        q = _apply_rope(q, cos, sin)
        k = _apply_rope(k, cos, sin)
        scores = jnp.einsum('bhqd,bhkd->bhqk', q, k) / jnp.sqrt(jnp.float32(D))
        w = jax.nn.softmax(scores, axis=-1)
        attn = jnp.einsum('bhqk,bhkd->bhqd', w, v)
        attn = jnp.transpose(attn, (0, 2, 1, 3)).reshape(B, S, DM)
        out = attn @ Wo + bo
        h = x + out
        mu = jnp.mean(h, axis=-1, keepdims=True)
        var = jnp.mean((h - mu) ** 2, axis=-1, keepdims=True)
        return (h - mu) * jax.lax.rsqrt(var + EPS) * gamma + beta

    def _L0_ffn_ref(x, Wg, W1, W2, W3, Ws1, Ws2, Ws3):
        import jax, jax.numpy as jnp
        import numpy as np
        B, T, C = (4, 512, 256)
        E = 8
        K = 2
        H = 352
        HS = 352 * 2
        b, t, c = x.shape
        xf = x.reshape(-1, c)
        n = xf.shape[0]
        router = xf @ Wg
        top_logits, idx = jax.lax.top_k(router, K)
        probs = jax.nn.softmax(top_logits.astype(jnp.float32), axis=-1).astype(x.dtype)
        w = jnp.zeros((n, E), x.dtype).at[jnp.arange(n)[:, None], idx].add(probs)
        h = jax.nn.silu(jnp.einsum('tc,ech->eth', xf, W1)) * jnp.einsum('tc,ech->eth', xf, W2)
        y = jnp.einsum('eth,ehc,te->tc', h, W3, w)
        y = y.reshape(b, t, c)
        hs = jax.nn.silu(xf @ Ws1) * (xf @ Ws2)
        y = y + (hs @ Ws3).reshape(b, t, c)
        return y

    def _L1_xattn_ref(query, key, value, Wq, bq, Wk, bk, Wv, bv):
        import jax, jax.numpy as jnp
        import numpy as np
        B, LQ, LK = (8, 512, 512)
        QD, KD, VD = (256, 128, 128)
        q = jnp.einsum('bld,de->ble', query, Wq) + bq
        k = jnp.einsum('bld,de->ble', key, Wk) + bk
        v = jnp.einsum('bld,de->ble', value, Wv) + bv
        scores = jnp.einsum('bqe,bke->bqk', q, k)
        attn = jax.nn.softmax(scores, axis=-1)
        out = jnp.einsum('bqk,bke->bqe', attn, v)
        return out

    def _L1_attn_ref(x, time_decay, time_first, time_mix_k, time_mix_v, time_mix_r, Wk, Wv, Wr, Wo):
        import jax, jax.numpy as jnp
        import numpy as np
        import math
        N_EMBD = 256
        DIM_ATT = 256
        N_LAYER = 24
        LAYER_ID = 12
        B, T = (4, 1024)

        def _init_params():
            r01 = LAYER_ID / (N_LAYER - 1)
            r1a0 = 1.0 - LAYER_ID / N_LAYER
            ddd = np.arange(N_EMBD, dtype=np.float32) / N_EMBD
            h = np.arange(DIM_ATT, dtype=np.float32)
            decay_speed = -5.0 + 8.0 * (h / (DIM_ATT - 1)) ** (0.7 + 1.3 * r01)
            zigzag = ((np.arange(DIM_ATT) + 1) % 3 - 1).astype(np.float32) * 0.5
            time_first = np.float32(math.log(0.3)) + zigzag
            return {'time_decay': jnp.asarray(decay_speed, jnp.float32), 'time_first': jnp.asarray(time_first, jnp.float32), 'time_mix_k': jnp.asarray(ddd ** r1a0, jnp.float32), 'time_mix_v': jnp.asarray(ddd ** r1a0 + 0.3 * r01, jnp.float32), 'time_mix_r': jnp.asarray(ddd ** (0.5 * r1a0), jnp.float32)}

        def _wkv(w, u, k, v):

            def step(carry, kv):
                aa, bb, pp = carry
                kt, vt = kv
                ww = u + kt
                p = jnp.maximum(pp, ww)
                e1 = jnp.exp(pp - p)
                e2 = jnp.exp(ww - p)
                y = (e1 * aa + e2 * vt) / (e1 * bb + e2)
                ww2 = pp + w
                p2 = jnp.maximum(ww2, kt)
                e1b = jnp.exp(ww2 - p2)
                e2b = jnp.exp(kt - p2)
                return ((e1b * aa + e2b * vt, e1b * bb + e2b, p2), y)
            Bb, Tt, C = k.shape
            init = (jnp.zeros((Bb, C), k.dtype), jnp.zeros((Bb, C), k.dtype), jnp.full((Bb, C), -1e+38, k.dtype))
            _, ys = jax.lax.scan(step, init, (jnp.swapaxes(k, 0, 1), jnp.swapaxes(v, 0, 1)))
            return jnp.swapaxes(ys, 0, 1)
        xx = jnp.pad(x, ((0, 0), (1, 0), (0, 0)))[:, :-1]
        xk = x * time_mix_k + xx * (1.0 - time_mix_k)
        xv = x * time_mix_v + xx * (1.0 - time_mix_v)
        xr = x * time_mix_r + xx * (1.0 - time_mix_r)
        k = jnp.einsum('btc,dc->btd', xk, Wk)
        v = jnp.einsum('btc,dc->btd', xv, Wv)
        sr = jax.nn.sigmoid(jnp.einsum('btc,dc->btd', xr, Wr))
        w = -jnp.exp(time_decay)
        rwkv = sr * _wkv(w, time_first, k, v)
        return jnp.einsum('btd,cd->btc', rwkv, Wo)

    def _L1_ffn_ref(x, w_router, w1, w2, bias):
        import jax, jax.numpy as jnp
        import numpy as np
        TOP_K = 2
        CAPACITY_FACTOR = 1.0
        sl, bs, hs = x.shape
        E = w_router.shape[1]
        xf = x.reshape(-1, hs)
        T = xf.shape[0]
        capacity = int(CAPACITY_FACTOR * TOP_K * T / E)
        scores = jax.nn.softmax(xf @ w_router, axis=-1)
        expert_weights, top_experts = jax.lax.top_k(scores, TOP_K)
        flat_e = top_experts.reshape(-1)
        flat_w = expert_weights.reshape(-1)
        N = flat_e.shape[0]
        order = jnp.argsort(flat_e, stable=True)
        bin_ids = flat_e[order]
        tpe = jnp.zeros((E,), jnp.int32).at[flat_e].add(1)
        starts = jnp.cumsum(tpe) - tpe
        offsets = jnp.arange(N) - starts[bin_ids]
        valid = offsets < capacity
        slot = jnp.where(valid, bin_ids * capacity + offsets, E * capacity)
        src = order // TOP_K
        xb = jnp.zeros((E * capacity + 1, hs), x.dtype).at[slot].set(xf[src])
        xb = xb[:-1].reshape(E, capacity, hs)
        h = jax.nn.gelu(jnp.einsum('ech,ehf->ecf', xb, w1))
        y = jnp.einsum('ecf,efh->ech', h, w2).reshape(E * capacity, hs)
        yv = jnp.where(valid[:, None], y[jnp.minimum(slot, E * capacity - 1)], 0.0)
        out = jnp.zeros((T, hs), x.dtype).at[src].add(flat_w[order][:, None] * yv)
        return out.reshape(sl, bs, hs) + bias

    def _L2_xattn_ref(q, kv, Wq, Wk, Wv, Wo, bo):
        import jax, jax.numpy as jnp
        import numpy as np
        NUM_HEADS = 16
        HEAD_DIM = 64
        Q_DIM = 256
        KV_DIM = 128
        INNER = NUM_HEADS * HEAD_DIM
        B, N, _ = q.shape
        M = kv.shape[1]
        scale = HEAD_DIM ** (-0.5)
        qh = (q @ Wq).reshape(B, N, NUM_HEADS, HEAD_DIM).transpose(0, 2, 1, 3)
        kh = (kv @ Wk).reshape(B, M, NUM_HEADS, HEAD_DIM).transpose(0, 2, 1, 3)
        vh = (kv @ Wv).reshape(B, M, NUM_HEADS, HEAD_DIM).transpose(0, 2, 1, 3)
        scores = jnp.einsum('bhnd,bhmd->bhnm', qh, kh) * scale
        attn = jax.nn.softmax(scores, axis=-1)
        out = jnp.einsum('bhnm,bhmd->bhnd', attn, vh)
        out = out.transpose(0, 2, 1, 3).reshape(B, N, INNER)
        return out @ Wo + bo

    def _L2_attn_ref(x, Wq, Wk, Wv, Wu, bu):
        import jax, jax.numpy as jnp
        import numpy as np
        SEQLEN, K, OLDK, HEADS = (512, 256, 256, 16)
        BASE = 10000.0

        def rope(x):
            t = x.shape[1]
            half = K // 2
            theta = 1.0 / BASE ** (jnp.arange(half, dtype=jnp.float32) / half)
            ang = jnp.arange(t, dtype=jnp.float32)[:, None] * theta[None, :]
            cos, sin = (jnp.cos(ang), jnp.sin(ang))
            xr = x.reshape(x.shape[0], t, half, 2)
            xe, xo = (xr[..., 0], xr[..., 1])
            re = xe * cos - xo * sin
            im = xe * sin + xo * cos
            return jnp.stack([re, im], axis=-1).reshape(x.shape)
        b, t, _ = x.shape
        h = HEADS
        s = K // h
        q = rope(x @ Wq.T)
        k = rope(x @ Wk.T)
        v = x @ Wv.T
        q = q.reshape(b, t, h, s).transpose(0, 2, 1, 3)
        k = k.reshape(b, t, h, s).transpose(0, 2, 1, 3)
        v = v.reshape(b, t, h, s).transpose(0, 2, 1, 3)
        dot = jnp.einsum('bhqd,bhkd->bhqk', q, k) / jnp.sqrt(jnp.float32(s))
        att = jax.nn.softmax(dot, axis=-1)
        out = jnp.einsum('bhqk,bhkd->bhqd', att, v)
        out = out.transpose(0, 2, 1, 3).reshape(b, t, h * s)
        return out @ Wu.T + bu

    def _L2_ffn_ref(x, gate_w, w1, b1, w2, b2, w3, b3, sw1, sb1, sw2, sb2, sw3, sb3):
        import jax, jax.numpy as jnp
        import numpy as np
        from jax import lax
        D_MODEL = 256
        INTER = 256
        N_EXPERTS = 8
        TOP_K = 2
        ROUTE_SCALE = 1.0
        B, S = (2, 1024)
        Bx, Sx, D = x.shape
        xt = x.reshape(-1, D)
        scores = jax.nn.softmax((xt @ gate_w.T).astype(jnp.float32), axis=-1)
        top_vals, top_idx = lax.top_k(scores, TOP_K)
        weights = (top_vals * ROUTE_SCALE).astype(x.dtype)
        combine = jnp.sum(jax.nn.one_hot(top_idx, N_EXPERTS, dtype=x.dtype) * weights[..., None], axis=1)

        def body(acc, p):
            W1, B1, W2, B2, W3, B3, c = p
            h = jax.nn.silu(xt @ W1 + B1) * (xt @ W3 + B3)
            return (acc + c[:, None] * (h @ W2 + B2), None)
        y, _ = lax.scan(body, jnp.zeros_like(xt), (w1, b1, w2, b2, w3, b3, combine.T))
        z = jax.nn.silu(xt @ sw1 + sb1) * (xt @ sw3 + sb3) @ sw2 + sb2
        return (y + z).reshape(Bx, Sx, D)

    def _L3_xattn_ref(x, z, Wq, Wkv, Wo):
        import jax, jax.numpy as jnp
        import numpy as np
        DIM = 256
        LATENT_DIM = 128
        NUM_HEADS = 16
        HEAD_DIM = DIM // NUM_HEADS
        SCALE = HEAD_DIM ** (-0.5)
        B, xN, _ = x.shape
        _, zN, _ = z.shape
        Q = (x @ Wq.T).reshape(B, xN, NUM_HEADS, HEAD_DIM)
        KV = (z @ Wkv.T).reshape(B, zN, 2, NUM_HEADS, HEAD_DIM)
        K = KV[:, :, 0]
        V = KV[:, :, 1]
        attn = jnp.einsum('bqhd,bkhd->bhqk', Q, K) * SCALE
        attn = jax.nn.softmax(attn, axis=-1)
        O = jnp.einsum('bhqk,bkhd->bqhd', attn, V).reshape(B, xN, DIM)
        return O @ Wo.T

    def _L3_attn_ref(x, Wq, bq, Wk, bk, Wv, bv, Wd, bd):
        import jax, jax.numpy as jnp
        import numpy as np
        EMB = 256
        HEADS = 16
        DEPTH = EMB // HEADS
        WINDOW = 64
        B, S = (1, 1024)
        b, s, _ = x.shape

        def proj(W, bias):
            y = jnp.einsum('bse,ef->bsf', x, W) + bias
            return y.reshape(b, s, HEADS, DEPTH).transpose(0, 2, 1, 3)
        q = proj(Wq, bq)
        k = proj(Wk, bk)
        v = proj(Wv, bv)
        scores = jnp.einsum('bhsd,bhtd->bhst', q, k) / jnp.sqrt(jnp.asarray(DEPTH, dtype=x.dtype))
        i = jnp.arange(s)[:, None]
        j = jnp.arange(s)[None, :]
        mask = jnp.where(jnp.abs(i - j) <= WINDOW, 0.0, -jnp.inf).astype(x.dtype)
        scores = scores + mask
        attn = jax.nn.softmax(scores, axis=-1)
        out = jnp.einsum('bhst,bhtd->bhsd', attn, v)
        out = out.transpose(0, 2, 1, 3).reshape(b, s, EMB)
        return jnp.einsum('bse,ef->bsf', out, Wd) + bd

    def _L3_ffn_ref(layer_input, gate_w, w_gate_up, w_down, shared_w_gate, shared_w_up, shared_w_down, shared_gate_w):
        import jax, jax.numpy as jnp
        import numpy as np
        HIDDEN = 256
        MOE_FF = 128
        SHARED_FF = 704
        NUM_EXPERTS = 16
        TOP_K = 2
        NORM_TOPK = True
        B, S, D = layer_input.shape
        x = layer_input.reshape(-1, D)
        N = x.shape[0]
        shared = jax.nn.silu(x @ shared_w_gate.T) * (x @ shared_w_up.T) @ shared_w_down.T
        shared = shared * jax.nn.sigmoid(x @ shared_gate_w.T)
        logits = x @ gate_w.T
        probs = jax.nn.softmax(logits.astype(jnp.float32), axis=-1)
        rw, sel = jax.lax.top_k(probs, TOP_K)
        if NORM_TOPK:
            rw = rw / rw.sum(axis=-1, keepdims=True)
        rw = rw.astype(x.dtype)
        combine = jnp.zeros((N, NUM_EXPERTS), x.dtype).at[jnp.arange(N)[:, None], sel].set(rw)
        gu = jnp.einsum('nd,edf->nef', x, w_gate_up)
        g, h = jnp.split(gu, 2, axis=-1)
        h = jax.nn.silu(g) * h
        expert_out = jnp.einsum('nef,efd,ne->nd', h, w_down, combine)
        out = expert_out + shared
        return out.reshape(B, S, D)
    x = x + _L0_xattn_ref(_layernorm(x, axis=-1), ctx_512, L0_xattn_ln1_g, L0_xattn_ln1_b, L0_xattn_ln2_g, L0_xattn_ln2_b, L0_xattn_a1_wq, L0_xattn_a1_wk, L0_xattn_a1_wv, L0_xattn_a1_li1_w, L0_xattn_a1_li1_b, L0_xattn_a1_lnx_g, L0_xattn_a1_lnx_b, L0_xattn_a1_lny_g, L0_xattn_a1_lny_b, L0_xattn_a1_ln3_g, L0_xattn_a1_ln3_b, L0_xattn_a1_li2_w, L0_xattn_a1_li2_b, L0_xattn_a1_li3_w, L0_xattn_a1_li3_b, L0_xattn_a2_wq, L0_xattn_a2_wk, L0_xattn_a2_wv, L0_xattn_a2_li1_w, L0_xattn_a2_li1_b, L0_xattn_a2_lnx_g, L0_xattn_a2_lnx_b, L0_xattn_a2_lny_g, L0_xattn_a2_lny_b, L0_xattn_a2_ln3_g, L0_xattn_a2_ln3_b, L0_xattn_a2_li2_w, L0_xattn_a2_li2_b, L0_xattn_a2_li3_w, L0_xattn_a2_li3_b, 0)
    x = x + _L0_attn_ref(_layernorm(x, axis=-1), L0_attn_Wqkv, L0_attn_bqkv, L0_attn_Wo, L0_attn_bo, L0_attn_gamma, L0_attn_beta)
    x = x + _L0_ffn_ref(_layernorm(x, axis=-1), L0_ffn_Wg, L0_ffn_W1, L0_ffn_W2, L0_ffn_W3, L0_ffn_Ws1, L0_ffn_Ws2, L0_ffn_Ws3)
    x = x + _L1_xattn_ref(_layernorm(x, axis=-1), ctx_512, ctx_512, L1_xattn_Wq, L1_xattn_bq, L1_xattn_Wk, L1_xattn_bk, L1_xattn_Wv, L1_xattn_bv)
    x = x + _L1_attn_ref(_layernorm(x, axis=-1), L1_attn_time_decay, L1_attn_time_first, L1_attn_time_mix_k, L1_attn_time_mix_v, L1_attn_time_mix_r, L1_attn_Wk, L1_attn_Wv, L1_attn_Wr, L1_attn_Wo)
    x = x + _L1_ffn_ref(_layernorm(x, axis=-1), L1_ffn_w_router, L1_ffn_w1, L1_ffn_w2, L1_ffn_bias)
    x = x + _L2_xattn_ref(_layernorm(x, axis=-1), ctx_512, L2_xattn_Wq, L2_xattn_Wk, L2_xattn_Wv, L2_xattn_Wo, L2_xattn_bo)
    x = x + _L2_attn_ref(_layernorm(x, axis=-1), L2_attn_Wq, L2_attn_Wk, L2_attn_Wv, L2_attn_Wu, L2_attn_bu)
    x = x + _L2_ffn_ref(_layernorm(x, axis=-1), L2_ffn_gate_w, L2_ffn_w1, L2_ffn_b1, L2_ffn_w2, L2_ffn_b2, L2_ffn_w3, L2_ffn_b3, L2_ffn_sw1, L2_ffn_sb1, L2_ffn_sw2, L2_ffn_sb2, L2_ffn_sw3, L2_ffn_sb3)
    x = x + _L3_xattn_ref(_layernorm(x, axis=-1), ctx_512, L3_xattn_Wq, L3_xattn_Wkv, L3_xattn_Wo)
    x = x + _L3_attn_ref(_layernorm(x, axis=-1), L3_attn_Wq, L3_attn_bq, L3_attn_Wk, L3_attn_bk, L3_attn_Wv, L3_attn_bv, L3_attn_Wd, L3_attn_bd)
    x = x + _L3_ffn_ref(_layernorm(x, axis=-1), L3_ffn_gate_w, L3_ffn_w_gate_up, L3_ffn_w_down, L3_ffn_shared_w_gate, L3_ffn_shared_w_up, L3_ffn_shared_w_down, L3_ffn_shared_gate_w)
    return x

_drawn_inputs = setup_inputs


def setup_inputs(seed=0):
    import zlib

    import numpy as np

    out = dict(_drawn_inputs(seed))
    spreads = {'L0_xattn_ln1_g': (1.0, 0.2),
     'L0_xattn_ln1_b': (0.0, 0.1),
     'L0_xattn_ln2_g': (1.0, 0.2),
     'L0_xattn_ln2_b': (0.0, 0.1),
     'L0_xattn_a1_li1_b': (0.0, 0.1),
     'L0_xattn_a1_lnx_g': (1.0, 0.6),
     'L0_xattn_a1_lnx_b': (0.0, 0.8),
     'L0_xattn_a1_lny_g': (1.0, 0.6),
     'L0_xattn_a1_lny_b': (0.0, 0.8),
     'L0_xattn_a1_ln3_g': (1.0, 0.6),
     'L0_xattn_a1_ln3_b': (0.0, 0.8),
     'L0_xattn_a1_li2_b': (0.0, 0.652),
     'L0_xattn_a1_li3_b': (0.0, 0.1),
     'L0_xattn_a2_li1_b': (0.0, 0.1),
     'L0_xattn_a2_lnx_g': (1.0, 0.6),
     'L0_xattn_a2_lnx_b': (0.0, 0.8),
     'L0_xattn_a2_lny_g': (1.0, 0.6),
     'L0_xattn_a2_lny_b': (0.0, 0.8),
     'L0_xattn_a2_ln3_g': (1.0, 0.6),
     'L0_xattn_a2_ln3_b': (0.0, 0.8),
     'L0_xattn_a2_li2_b': (0.0, 0.65),
     'L0_xattn_a2_li3_b': (0.0, 0.1),
     'L0_attn_bqkv': (0.0, 0.8),
     'L0_attn_bo': (0.0, 0.318),
     'L0_attn_gamma': (1.0, 0.2),
     'L0_attn_beta': (0.0, 0.337),
     'L1_xattn_bq': (0.0, 0.8),
     'L1_xattn_bk': (0.0, 2.0),
     'L1_xattn_bv': (0.0, 0.3),
     'L1_ffn_bias': (0.0, 0.337),
     'L2_attn_bu': (0.0, 0.836),
     'L2_ffn_b1': (0.0, 2.0),
     'L2_ffn_b2': (0.0, 2.0),
     'L2_ffn_b3': (0.0, 2.0),
     'L2_ffn_sb1': (0.0, 0.552),
     'L2_ffn_sb2': (0.0, 0.878),
     'L2_ffn_sb3': (0.0, 1.426)}
    factors = {'L0_xattn_a1_wq': 8.0,
     'L0_xattn_a1_wk': 8.0,
     'L0_xattn_a1_wv': 8.0,
     'L0_xattn_a1_li1_w': 8.0,
     'L0_xattn_a2_wq': 8.0,
     'L0_xattn_a2_wk': 8.0,
     'L0_xattn_a2_wv': 2.94,
     'L0_xattn_a2_li1_w': 2.927,
     'L0_attn_Wqkv': 8.0,
     'L0_attn_Wo': 5.777,
     'L0_ffn_Wg': 8.0,
     'L0_ffn_W1': 8.0,
     'L0_ffn_W2': 8.0,
     'L0_ffn_W3': 8.0,
     'L0_ffn_Ws1': 8.0,
     'L0_ffn_Ws2': 7.802,
     'L0_ffn_Ws3': 7.697,
     'L1_xattn_Wq': 3.975,
     'L1_xattn_Wk': 3.787,
     'L1_attn_time_first': 200.0,
     'L1_attn_time_mix_k': 3.888,
     'L1_attn_time_mix_r': 7.06,
     'L1_ffn_w_router': 8.0,
     'L1_ffn_w1': 8.0,
     'L1_ffn_w2': 8.0,
     'L2_xattn_bo': 43.431,
     'L3_attn_bq': 64.0,
     'L3_attn_bk': 200.0,
     'L3_attn_bv': 30.062,
     'L3_attn_bd': 59.989,
     'L3_ffn_gate_w': 8.0,
     'L3_ffn_w_gate_up': 8.0,
     'L3_ffn_w_down': 8.0,
     'L3_ffn_shared_w_gate': 8.0,
     'L3_ffn_shared_w_up': 8.0,
     'L3_ffn_shared_w_down': 8.0,
     'L3_ffn_shared_gate_w': 8.0,
     'L2_xattn_Wk': 2.984,
     'L2_attn_Wq': 2.756,
     'L2_attn_Wk': 3.005,
     'L3_attn_Wq': 3.436,
     'L3_attn_Wk': 3.584,
     'L3_xattn_Wq': 2.764}
    for name, (base, spread) in spreads.items():
        noise = np.random.default_rng([zlib.crc32(name.encode()), seed]).standard_normal(out[name].shape)
        drawn = base * np.exp(spread * noise) if base else spread * noise
        out[name] = jnp.asarray(drawn.astype(out[name].dtype))
    for name, factor in factors.items():
        out[name] = (out[name] * factor).astype(out[name].dtype)
    return out
```

```python
from contextlib import ExitStack, contextmanager

import numpy as np

import concourse.bass as bass
from concourse import mybir

ACT = mybir.ActivationFunctionType
ALU = mybir.AluOpType
AX = mybir.AxisListType
F32 = mybir.dt.float32
U32 = mybir.dt.uint32

P = 128
B, S, D = 8, 64, 256
N = B * S
NT = N // P
KC = D // P
KEYS, CD = 1601, 128
KCH = -(-KEYS // P)
KPAD = KCH * P
KLAST = KEYS - (KCH - 1) * P
H = 16
HP = 32
BANK = 512
EPS = 1e-5
LAYERS = 12


@contextmanager
def signals(nc, *names):
    with ExitStack() as stack:
        sems = [stack.enter_context(nc.semaphore(n)) for n in names]
        yield sems
        for s in sems:
            nc.sync.sem_clear(s)
        nc.all_engine_barrier()


class Chain:

    def __init__(self, engine, sem):
        self.engine, self.sem, self.count = engine, sem, 0

    def __call__(self, instruction):
        self.count += 1
        instruction.then_inc(self.sem, 1)
        self.engine.wait_ge(self.sem, self.count)


class Weights:

    def __init__(self, region, fields):
        self.region, self.fields = region, fields

    def __call__(self, name, rows=P):
        at, width = self.fields[name]
        return self.region[0:rows, at:at + width]

    def chunks(self, name, n):
        return self(name).rearrange("p (k n) -> p k n", k=n)


def perceiver_kernel(nc, dram, packs, out):
    with ExitStack() as stack:
        made_so_far = {}

        def sb(name, shape, dt=F32, where=stack):
            made_so_far[name] = made_so_far.get(name, 0) + 1
            return where.enter_context(nc.sbuf_tensor(f"{name}_{made_so_far[name]}", shape, dt))

        x = sb("x", [P, NT, D])
        xn = sb("xn", [P, NT, D])
        xT = sb("xT", [P, KC, N])
        ident = sb("ident", [P, P])
        ones = sb("ones", [1, P])
        iota = sb("iota", [P, P])
        stat = sb("stat", [P, NT, 6])
        mv = sb("mv", [P, NT, 2])
        std = sb("std", [P, NT])
        rstd = sb("rstd", [P, NT])
        zero = sb("zero", [P, 1])
        widths = [max(packs[n][1] for n in names) for names in
                  (["a1", "l0a", "l1x", "l1f", "l2a", "l3x", "l3f"], ["a2", "l0f", "l1a", "l2x", "l2f", "l3a"])]
        regions = [sb(f"weights{i}", [P, w]) for i, w in enumerate(widths)]
        ps = stack.enter_context(nc.psum_tensor("ps", [P, 8, BANK], F32))
        loaded = [stack.enter_context(nc.semaphore(f"weights_loaded{i}")) for i in range(2)]
        loads = [0, 0]

        def weights(name):
            return Weights(regions[order.index(name) % 2], packs[name][0])

        order = ["a1", "a2", "l0a", "l0f", "l1x", "l1a", "l1f", "l2x", "l2a", "l2f", "l3x", "l3a", "l3f"]

        def load_weights(engine, name):
            i = order.index(name) % 2
            engine.dma_start(regions[i][:, 0:packs[name][1]], dram[name]).then_inc(loaded[i], 16)
            loads[i] += 1

        def weights_here(name):
            i = order.index(name) % 2
            k = order.index(name) + 1
            with nc.Block() as block:
                @block.sync
                def _(sp):
                    sp.wait_ge(loaded[i], 16 * loads[i])
                    if k < len(order):
                        load_weights(sp, order[k])

        with signals(nc, "x_landed", "filled", "made") as (x_landed, filled, made), nc.Block() as block:
            @block.sync
            def _(sp):
                sp.dma_start(x[:], dram["x"].rearrange("(t p) d -> p t d", p=P)).then_inc(x_landed, 16)
                load_weights(sp, "a1")
                sp.wait_ge(x_landed, 16)

            @block.gpsimd
            def _(pool):
                pool.memset(ident[:], 0.0).then_inc(filled, 1)
                pool.memset(ones[:], 1.0).then_inc(filled, 1)
                pool.memset(zero[:], 0.0).then_inc(filled, 1)
                pool.iota(iota[:], pattern=[[1, P]], base=0, channel_multiplier=0,
                          allow_small_or_imprecise_dtypes=True).then_inc(made, 1)
                pool.wait_ge(filled, 3)
                pool.affine_select(out=ident[:], in_=ident[:], compare_op=ALU.not_equal, fill=1.0, base=0,
                                   pattern=[[-1, P]], channel_multiplier=1).then_inc(made, 1)
                pool.wait_ge(made, 2)

        def normalise(src, z, turned=(), add=(), affine=None):
            with signals(nc, "chain", "var_ready", "std_ready", "z_ready", "turned_ready") as \
                    (chain, var_ready, std_ready, z_ready, turned_ready), nc.Block() as block:
                @block.vector
                def _(dve):
                    link = Chain(dve, chain)
                    for other in add:
                        link(dve.tensor_tensor(src[:], src[:], other[:], ALU.add))
                    for t in range(NT):
                        last = dve.bn_stats(stat[:, t, :], src[:, t, :])
                    link(last)
                    for t in range(NT):
                        last = dve.bn_aggr(mv[:, t, :], stat[:, t, :])
                    link(last)
                    link(dve.tensor_scalar(std[:], mv[:, :, 1], EPS, None, ALU.add))
                    dve.sem_inc(var_ready, 1)
                    dve.wait_ge(std_ready, 1)
                    link(dve.reciprocal(rstd[:], std[:]))
                    for t in range(NT):
                        last = dve.tensor_scalar(z[:, t, :], src[:, t, :], mv[:, t, 0:1], rstd[:, t:t + 1],
                                                 ALU.subtract, ALU.mult)
                        if affine is None:
                            last.then_inc(z_ready, 1)
                    if affine is not None:
                        link(last)
                        for t in range(NT):
                            last = dve.tensor_tensor(z[:, t, :], z[:, t, :], affine[0], ALU.mult)
                        link(last)
                        for t in range(NT):
                            dve.tensor_tensor(z[:, t, :], z[:, t, :], affine[1], ALU.add).then_inc(z_ready, 1)

                @block.scalar
                def _(act):
                    act.wait_ge(var_ready, 1)
                    nc.scalar.activation(std[:], std[:], ACT.Sqrt).then_inc(std_ready, 1)
                    act.wait_ge(std_ready, 1)
                    if turned:
                        act.wait_ge(turned_ready, NT)
                    for dst, scale, bias in turned:
                        for c in range(KC):
                            if scale is None:
                                nc.scalar.activation(dst[:, c, :], ps[:, c, :], ACT.Copy)
                            else:
                                nc.scalar.activation(dst[:, c, :], ps[:, c, :], ACT.Identity,
                                                     bias=bias[:, c:c + 1], scale=scale[:, c:c + 1])

                if turned:
                    @block.tensor
                    def _(pe):
                        for t in range(NT):
                            pe.wait_ge(z_ready, t + 1)
                            for c in range(KC):
                                last = pe.transpose(ps[:, c, t * P:(t + 1) * P], z[:, t, c * P:(c + 1) * P], ident[:])
                            last.then_inc(turned_ready, 1)

        def dense(products):
            def nth(n):
                return sum(p[3] == products[n][3] for p in products[:n + 1])

            with signals(nc, "product_ready", "taken_by_scalar", "taken_by_vector") as \
                    (product_ready, taken_by_scalar, taken_by_vector), nc.Block() as block:
                taken = {"act": taken_by_scalar, "dve": taken_by_vector}

                @block.tensor
                def _(pe):
                    for n, (terms, rows, cols, engine, take) in enumerate(products):
                        if n >= 8:
                            pe.wait_ge(taken[products[n - 8][3]], nth(n - 8))
                        bank = ps[0:rows, n % 8, 0:cols]
                        if terms[0] is None:
                            for i, block_in in enumerate(terms[1]):
                                last = pe.transpose(ps[0:rows, n % 8, i * P:(i + 1) * P], block_in, ident[:])
                        elif terms[0] == "rows":
                            for at, lhsT, rhs in terms[1]:
                                last = pe.matmul(ps[at:at + lhsT.shape[1], n % 8, 0:cols], lhsT, rhs,
                                                 start=True, stop=True)
                        else:
                            for i, (lhsT, rhs) in enumerate(terms):
                                last = pe.matmul(bank, lhsT, rhs, start=(i == 0), stop=(i == len(terms) - 1))
                        last.then_inc(product_ready, 1)

                @block.scalar
                def _(act):
                    for n, (terms, rows, cols, engine, take) in enumerate(products):
                        if engine == "act":
                            act.wait_ge(product_ready, n + 1)
                            take(nc.scalar, ps[0:rows, n % 8, 0:cols]).then_inc(taken_by_scalar, 1)

                @block.vector
                def _(dve):
                    for n, (terms, rows, cols, engine, take) in enumerate(products):
                        if engine == "dve":
                            dve.wait_ge(product_ready, n + 1)
                            take(nc.vector, ps[0:rows, n % 8, 0:cols]).then_inc(taken_by_vector, 1)

        def copy_to(dst):
            def take(engine, psum):
                if engine is nc.scalar:
                    return engine.activation(dst, psum, ACT.Copy)
                return engine.tensor_copy(dst, psum)
            return take

        def plus_column(dst, column):
            def take(engine, psum):
                if engine is nc.scalar:
                    return engine.activation(dst, psum, ACT.Identity, bias=column)
                return engine.tensor_scalar(dst, psum, column, None, ALU.add)
            return take

        def plus(dst, other):
            return lambda engine, psum: engine.tensor_tensor(dst, psum, other, ALU.add)

        def activated(dst, func, bias=0.0):
            return lambda engine, psum: engine.activation(dst, psum, func, bias=bias)

        def either(n):
            return "act" if n % 2 else "dve"

        def feature_rows(w, src, dst, column=None, chunks=None):
            k_chunks = w.shape[1]
            chunks = chunks or w.shape[2] // P
            return [([(w[:, k, m * P:(m + 1) * P], src[:, k, :]) for k in range(k_chunks)], P, N, either(m),
                     copy_to(dst[:, m, :]) if column is None else plus_column(dst[:, m, :], column[:, m:m + 1]))
                    for m in range(chunks)]

        def token_rows(src, w, take, row=None, width=D, engine="dve"):
            products = []
            for t in range(NT):
                terms = [(src[:, k, t * P:(t + 1) * P], w[:, k, :]) for k in range(w.shape[1])]
                if row is not None:
                    terms.append((ones[0:1, :], row))
                products.append((terms, P, width, engine if engine != "both" else either(t), take(t)))
            return products

        def self_attention(qT, kT, v, oT, scale, mask=None):
            names = ("chain", "cleared", "scores_ready", "shifted", "exp_ready", "probs_ready", "turned_ready",
                     "turned_kept", "out_ready", "out_kept")
            with ExitStack() as own, signals(nc, *names) as \
                    (chain, cleared, scores_ready, shifted, exp_ready, probs_ready, turned_ready,
                     turned_kept, out_ready, out_kept):
                less = sb("less", [P, 2, H, S], where=own)
                probs = sb("probs", [P, 2, H, P], where=own)
                probsT = sb("probsT", [P, 2, H, P], where=own)
                top = sb("top", [P, H], where=own)
                total = sb("total", [P, H], where=own)
                rtotal = sb("rtotal", [P, H], where=own)
                with nc.Block() as block:
                    @block.tensor
                    def _(pe):
                        def scores(t):
                            if t:
                                pe.wait_ge(shifted, t)
                            for i in range(4):
                                for j in range(4):
                                    for half in range(2):
                                        rows = slice(HP * j, HP * j + HP)
                                        at = (2 * t + half) * S
                                        last = pe.matmul(ps[half * S:half * S + S, j, i * S:(i + 1) * S],
                                                         qT[rows, i, at:at + S], kT[rows, i, at:at + S],
                                                         start=True, stop=True)
                            last.then_inc(scores_ready, 1)

                        scores(0)
                        for t in range(NT):
                            if t + 1 < NT:
                                scores(t + 1)
                            pe.wait_ge(probs_ready, 2 * (t + 1))
                            for g in range(4):
                                n = 4 * t + g
                                if n >= 2:
                                    pe.wait_ge(turned_kept, n - 1)
                                for i in range(4):
                                    last = pe.transpose(ps[:, 4 + n % 2, i * P:(i + 1) * P],
                                                        probs[:, t % 2, 4 * g + i, :], ident[:])
                                last.then_inc(turned_ready, 1)
                            if t >= 2:
                                pe.wait_ge(out_kept, t - 1)
                            for j in range(4):
                                pe.wait_ge(turned_kept, 4 * t + j + 1)
                                for i in range(4):
                                    last = pe.matmul(ps[HP * j:HP * j + HP, 6 + t % 2, i * P:(i + 1) * P],
                                                     v[:, t, (4 * i + j) * HP:(4 * i + j + 1) * HP],
                                                     probsT[:, t % 2, 4 * j + i, :], start=True, stop=True)
                            last.then_inc(out_ready, 1)

                    @block.gpsimd
                    def _(pool):
                        pool.memset(probs[:, 0], 0.0).then_inc(cleared, 1)
                        pool.memset(probs[:, 1], 0.0).then_inc(cleared, 1)

                    @block.scalar
                    def _(act):
                        def exponents(t):
                            act.wait_ge(shifted, t + 1)
                            nc.scalar.activation(less[:, t % 2], less[:, t % 2], ACT.Exp, scale=scale)\
                                .then_inc(exp_ready, 1)

                        exponents(0)
                        for t in range(NT):
                            if t >= 2:
                                act.wait_ge(out_ready, t - 1)
                            for g in range(4):
                                n = 4 * t + g
                                act.wait_ge(turned_ready, n + 1)
                                nc.scalar.activation(probsT[:, t % 2, 4 * g:4 * g + 4, :],
                                                     ps[:, 4 + n % 2, :].rearrange("p (i q) -> p i q", q=P),
                                                     ACT.Copy).then_inc(turned_kept, 1)
                            if t + 1 < NT:
                                exponents(t + 1)

                    @block.vector
                    def _(dve):
                        link = Chain(dve, chain)

                        def shift(t):
                            dve.wait_ge(scores_ready, t + 1)
                            if t >= 2:
                                dve.wait_ge(probs_ready, 2 * (t - 1))
                            s = ps[:, 0:4, 0:4 * S].rearrange("p j (i q) -> p j i q", q=S)
                            link(dve.tensor_reduce(top[:], s, AX.X, ALU.max))
                            dve.tensor_tensor(less[:, t % 2].rearrange("p (j i) q -> p j i q", j=4), s,
                                              top[:].rearrange("p (j i) -> p j i", j=4).unsqueeze(3)
                                              .broadcast_to([P, 4, 4, S]), ALU.subtract).then_inc(shifted, 1)
                            dve.wait_ge(shifted, t + 1)

                        def normal(t):
                            dve.wait_ge(exp_ready, t + 1)
                            link(dve.tensor_reduce(total[:], less[:, t % 2], AX.X, ALU.add))
                            link(dve.reciprocal(rtotal[:], total[:]))
                            if mask is not None:
                                link(dve.tensor_tensor(less[:, t % 2], less[:, t % 2],
                                                       mask.unsqueeze(1).broadcast_to([P, H, S]), ALU.mult))
                            dve.wait_ge(cleared, min(t + 1, 2))
                            if t >= 2:
                                dve.wait_ge(turned_ready, 4 * (t - 1))
                            for half in range(2):
                                rows = slice(half * S, half * S + S)
                                dve.tensor_tensor(probs[rows, t % 2, :, half * S:half * S + S], less[rows, t % 2],
                                                  rtotal[rows].unsqueeze(2).broadcast_to([S, H, S]),
                                                  ALU.mult).then_inc(probs_ready, 1)

                        shift(0)
                        normal(0)
                        for t in range(NT):
                            if t + 1 < NT:
                                shift(t + 1)
                                normal(t + 1)
                            dve.wait_ge(out_ready, t + 1)
                            dve.tensor_copy(oT[:, :, t * P:(t + 1) * P],
                                            ps[:, 6 + t % 2, :].rearrange("p (i q) -> p i q", q=P)).then_inc(out_kept, 1)

        def cross_attention(q, heads, scale, keysT, keys, shift=None, affine=None):
            per_batch = max(heads // 2, 1)
            rows = min(heads, 2) * S
            group = min(4, per_batch)
            groups = per_batch // group
            units = 2 * per_batch
            steps = B // 2
            names = ("landed0", "landed1", "chain", "staged", "scores_half", "scores_ready", "top_ready",
                     "probs_ready", "turned_ready", "turned_act", "turned_dve", "value_ready", "value_kept",
                     "value_turned", "value_stored")
            with ExitStack() as own, signals(nc, *names) as \
                    (landed0, landed1, chain, staged, scores_half, scores_ready, top_ready, probs_ready,
                     turned_ready, turned_act, turned_dve, value_ready, value_kept, value_turned, value_stored):
                landed = (landed0, landed1)
                cT = sb("cT", [P, 2, KEYS + 1], where=own)
                c = sb("c", [P, 2, KCH, CD], where=own)
                qs = sb("qs", [P, 2, group * rows], where=own)
                probs = sb("probs", [P, 2, KEYS + 1], where=own)
                probsT = sb("probsT", [P, KCH, P], where=own)
                value = sb("value", [P, per_batch, CD], where=own)
                top = sb("top", [P, 2, 2], where=own)
                ntop = sb("ntop", [P, 2, 2], where=own)
                total = sb("total", [P, 2], where=own)
                rtotal = sb("rtotal", [P, 2], where=own)
                parts = [range(0, 4), range(4, 8), range(8, 12), range(12, KCH)]

                def middle(engine, start, end, body):
                    if heads == 1:
                        for step in range(start, end):
                            body(step)
                    else:
                        with engine.Fori(start, end) as step:
                            body(step)

                def width(chunk):
                    return P if chunk < KCH - 1 else KLAST

                with nc.Block() as block:
                    @block.sync
                    def _(sp):
                        def fetch(i, step):
                            sp.dma_start(cT[:, i, 0:KEYS], keysT[bass.ds(2 * step + i, 1)].rearrange("b p k -> (b p) k"))\
                                .then_inc(landed[i], 16)
                            sp.dma_start(c[:, i], keys[bass.ds(2 * step + i, 1)]
                                         .rearrange("b p (k d) -> (b p) k d", d=CD)).then_inc(landed[i], 16)
                        fetch(0, 0)
                        fetch(1, 0)
                        with sp.Fori(0, steps - 1) as step:
                            for i in range(2):
                                sp.wait_ge(value_ready, step * units + (i + 1) * per_batch)
                                fetch(i, step + 1)

                    @block.gpsimd
                    def _(pool):
                        def stage(step):
                            for i in range(2):
                                for g in range(groups):
                                    n = i * groups + g
                                    slot = n % 2
                                    if isinstance(step, int) and step == 0 and n < 2:
                                        pass
                                    else:
                                        pool.wait_ge(scores_ready, step * units + (n - 1) * group)
                                    h = 2 * group if heads > 1 else 1
                                    pool.tensor_copy(
                                        qs[:, slot].rearrange("p (h s) -> p h s", s=S),
                                        q[:, g * h:(g + 1) * h, bass.ds((2 * step + i) * S, S)]).then_inc(staged, 1)
                        stage(0)
                        middle(pool, 1, steps, stage)

                    @block.tensor
                    def _(pe):
                        def scores(u, base, step):
                            i, at = (u // per_batch) % 2, u % units
                            nxt = u // units
                            if at % per_batch == 0:
                                pe.wait_ge(landed[i], 32 * (step + nxt) + 32)
                            if at % group == 0:
                                pe.wait_ge(staged, (step + nxt) * 2 * groups + at // group + 1)
                            slot = (at // group) % 2
                            lhsT = qs[:, slot, (at % group) * rows:(at % group + 1) * rows]
                            for n in range(4):
                                w = min(BANK, KEYS - n * BANK)
                                last = pe.matmul(ps[0:rows, n, 0:w], lhsT, cT[:, i, n * BANK:n * BANK + w],
                                                 start=True, stop=True)
                                if n == 1:
                                    last.then_inc(scores_half, 1)
                            last.then_inc(scores_ready, 1)

                        def turn_part(u, base, g):
                            if g >= 2:
                                pe.wait_ge(turned_act if g % 2 else turned_dve, (base + u) * 2 + g // 2)
                            for k, chunk in enumerate(parts[g]):
                                w = width(chunk)
                                last = pe.transpose(ps[0:w, 4 + g % 2, k * P:k * P + rows],
                                                    probs[0:rows, u % 2, chunk * P:chunk * P + w], ident[0:rows, 0:rows])
                            last.then_inc(turned_ready, 1)

                        def turn_values(u, base, step):
                            g = u // group
                            pe.wait_ge(value_kept, base + u + 1)
                            if isinstance(step, int) and step == 0 and g == 0:
                                pass
                            else:
                                pe.wait_ge(value_stored, step * 2 * groups + g)
                            for k in range(group):
                                last = pe.transpose(ps[:, 7, k * rows:(k + 1) * rows],
                                                    value[0:rows, (u % per_batch) - group + 1 + k, :],
                                                    ident[0:rows, 0:rows])
                            last.then_inc(value_turned, 1)

                        def body(step, first, final):
                            base = step * units
                            for u in range(units):
                                i = u // per_batch
                                pe.wait_ge(probs_ready, base + u + 1)
                                if not (first and u == 0):
                                    pe.wait_ge(turned_dve, (base + u) * 2)
                                    pe.wait_ge(turned_act, (base + u) * 2)
                                turn_part(u, base, 0)
                                turn_part(u, base, 1)
                                if not (final and u == units - 1):
                                    scores(u + 1, base, step)
                                turn_part(u, base, 2)
                                turn_part(u, base, 3)
                                if not (first and u < 2):
                                    pe.wait_ge(value_kept, base + u - 1)
                                for k in range(KCH):
                                    if k % 4 == 0:
                                        pe.wait_ge(turned_act if (k // 4) % 2 else turned_dve,
                                                   (base + u) * 2 + k // 8 + 1)
                                    w = width(k)
                                    last = pe.matmul(ps[0:rows, 6, (u % 2) * CD:(u % 2) * CD + CD],
                                                     probsT[0:w, k, 0:rows], c[0:w, i, k, :],
                                                     start=(k == 0), stop=(k == KCH - 1))
                                last.then_inc(value_ready, 1)
                                if u % group == group - 1:
                                    turn_values(u, base, step)

                        scores(0, 0, 0)
                        body(0, True, False)
                        middle(pe, 1, steps - 1, lambda step: body(step, False, False))
                        body(steps - 1, False, True)

                    @block.scalar
                    def _(act):
                        def exponents(u, base, early):
                            act.wait_ge(top_ready, base + u + 1)
                            if not early:
                                act.wait_ge(turned_ready, (base + u - 1) * 4)
                            nc.scalar.activation(
                                probs[0:rows, u % 2, 0:KEYS],
                                ps[0:rows, 0:4, :].rearrange("p n k -> p (n k)")[:, 0:KEYS], ACT.Exp,
                                bias=ntop[0:rows, u % 2, 0:1], scale=scale,
                                accum_out=total[0:rows, u % 2:u % 2 + 1]).then_inc(probs_ready, 1)

                        def copy_turned(u, base, g):
                            act.wait_ge(turned_ready, (base + u) * 4 + g + 1)
                            w = width(parts[g][-1])
                            nc.scalar.activation(
                                probsT[0:w, parts[g][0]:parts[g][-1] + 1, 0:rows],
                                ps[0:w, 5, 0:len(parts[g]) * P].rearrange("p (k r) -> p k r", r=P)[:, :, 0:rows],
                                ACT.Copy).then_inc(turned_act, 1)

                        def store(u, step):
                            g = u // group
                            act.wait_ge(value_turned, step * 2 * groups + g + 1)
                            h = 2 * group if heads > 1 else 1
                            dst = q[:, (g % groups) * h:(g % groups + 1) * h, bass.ds((2 * step + g // groups) * S, S)]
                            src = ps[:, 7, 0:group * rows].rearrange("p (h s) -> p h s", s=S)
                            if affine is None:
                                nc.scalar.activation(dst, src, ACT.Copy).then_inc(value_stored, 1)
                            else:
                                nc.scalar.activation(dst, src, ACT.Identity, bias=affine[1],
                                                     scale=affine[0]).then_inc(value_stored, 1)

                        def body(step, first, final):
                            base = step * units
                            for u in range(units):
                                if not (first and u == 0):
                                    act.wait_ge(value_ready, base + u)
                                copy_turned(u, base, 1)
                                copy_turned(u, base, 3)
                                if not (final and u == units - 1):
                                    exponents(u + 1, base, first and u == 0)
                                if u % group == group - 1:
                                    store(u, step)

                        exponents(0, 0, True)
                        body(0, True, False)
                        middle(act, 1, steps - 1, lambda step: body(step, False, False))
                        body(steps - 1, False, True)

                    @block.vector
                    def _(dve):
                        per_unit = 3 if shift is None else 5

                        def maximum(u, base, step, count, first):
                            def linked(instruction, n):
                                instruction.then_inc(chain, 1)
                                dve.wait_ge(chain, count + n)
                            dve.wait_ge(scores_half, base + u + 1)
                            if not first:
                                dve.wait_ge(probs_ready, base + u - 1)
                            flat = ps[0:rows, 0:4, :].rearrange("p n k -> p (n k)")
                            dve.tensor_reduce(top[0:rows, u % 2, 0:1], flat[:, 0:2 * BANK], AX.X, ALU.max)\
                                .then_inc(chain, 1)
                            dve.wait_ge(scores_ready, base + u + 1)
                            linked(dve.tensor_reduce(top[0:rows, u % 2, 1:2], flat[:, 2 * BANK:KEYS], AX.X, ALU.max), 2)
                            if shift is None:
                                dve.tensor_scalar(ntop[0:rows, u % 2, 0:1], top[0:rows, u % 2, 0:1],
                                                  top[0:rows, u % 2, 1:2], -scale, ALU.max, ALU.mult)\
                                    .then_inc(top_ready, 1)
                            else:
                                term = shift[0:rows, bass.ds(2 * (step + u // units) + (u % units) // per_batch, 1)]
                                linked(dve.tensor_scalar(top[0:rows, u % 2, 0:1], top[0:rows, u % 2, 0:1],
                                                         top[0:rows, u % 2, 1:2], None, ALU.max), 3)
                                linked(dve.tensor_tensor(top[0:rows, u % 2, 0:1], top[0:rows, u % 2, 0:1],
                                                         term, ALU.add), 4)
                                dve.tensor_tensor(ntop[0:rows, u % 2, 0:1], term, top[0:rows, u % 2, 0:1],
                                                  ALU.subtract).then_inc(top_ready, 1)

                        def copy_turned(u, base, g):
                            dve.wait_ge(turned_ready, (base + u) * 4 + g + 1)
                            dve.tensor_copy(probsT[:, parts[g][0]:parts[g][-1] + 1, 0:rows],
                                            ps[:, 4, :].rearrange("p (k r) -> p k r", r=P)[:, :, 0:rows])\
                                .then_inc(turned_dve, 1)

                        def body(step, first, final):
                            base = step * units
                            for u in range(units):
                                if not (first and u == 0):
                                    dve.wait_ge(value_ready, base + u)
                                copy_turned(u, base, 0)
                                if not (final and u == units - 1):
                                    maximum(u + 1, base, step, (base + u + 1) * per_unit - 1, first and u == 0)
                                copy_turned(u, base, 2)
                                count = (base + u + 1) * per_unit + per_unit - 2
                                if final and u == units - 1:
                                    count = (base + u + 1) * per_unit - 1
                                dve.wait_ge(probs_ready, base + u + 1)
                                dve.reciprocal(rtotal[0:rows, u % 2:u % 2 + 1], total[0:rows, u % 2:u % 2 + 1])\
                                    .then_inc(chain, 1)
                                dve.wait_ge(chain, count + 1)
                                dve.wait_ge(value_ready, base + u + 1)
                                if not (first and u < per_batch):
                                    dve.wait_ge(value_turned, step * 2 * groups + u // group - groups + 1)
                                dve.tensor_scalar(value[0:rows, u % per_batch, :],
                                                  ps[0:rows, 6, (u % 2) * CD:(u % 2) * CD + CD],
                                                  rtotal[0:rows, u % 2:u % 2 + 1], None, ALU.mult)\
                                    .then_inc(value_kept, 1)

                        maximum(0, 0, 0, 0, True)
                        body(0, True, False)
                        middle(dve, 1, steps - 1, lambda step: body(step, False, False))
                        body(steps - 1, False, True)

        def experts(guide, down, count, hidden, combine, bias=False):
            chunks = -(-hidden // P)
            gw, dw = guide.shape[2], down.shape[2]
            steps = (count - 1) // 2
            names = ("guide_landed0", "guide_landed1", "down_landed0", "down_landed1", "raw_ready", "silu_ready",
                     "hidden_ready", "down_ready", "added")
            with ExitStack() as own, signals(nc, *names) as \
                    (guide_landed0, guide_landed1, down_landed0, down_landed1, raw_ready, silu_ready,
                     hidden_ready, down_ready, added):
                guide_landed, down_landed = (guide_landed0, guide_landed1), (down_landed0, down_landed1)
                wg = sb("wg", [P, 2, gw], where=own)
                wd = sb("wd", [P, 2, dw], where=own)
                silu = sb("silu", [P, 2, N], where=own)
                hid = sb("hid", [P, 2, chunks, N], where=own)

                def width(c):
                    return min(P, hidden - c * P)

                with nc.Block() as block:
                    @block.sync
                    def _(sp):
                        def fetch(e, slot, first=False):
                            if not first:
                                sp.wait_ge(hidden_ready, (e - 1) * chunks)
                            sp.dma_start(wg[:, slot], guide[bass.ds(e, 1)].rearrange("e p n -> (e p) n"))\
                                .then_inc(guide_landed[slot], 16)
                            if not first:
                                sp.wait_ge(down_ready, (e - 1) * NT)
                            sp.dma_start(wd[:, slot], down[bass.ds(e, 1)].rearrange("e p n -> (e p) n"))\
                                .then_inc(down_landed[slot], 16)
                        fetch(0, 0, True)
                        fetch(1, 1, True)
                        with sp.Fori(1, count // 2) as i:
                            fetch(2 * i, 0)
                            fetch(2 * i + 1, 1)
                        if count % 2:
                            fetch(count - 1, (count - 1) % 2)

                    def in_order(first_product, second_product, loop):
                        first_product(0, 0, 0, True)
                        for at in (None, 1):
                            if at is None:
                                first_product(1, 1, 0, True)
                                second_product(0, 0, 0, True)
                                first_product(2, 0, 1, False)
                                second_product(1, 1, 0, False)
                            else:
                                with loop(1, steps) as i:
                                    first_product(2 * i + 1, 1, i, False)
                                    second_product(2 * i, 0, i, False)
                                    first_product(2 * i + 2, 0, i + 1, False)
                                    second_product(2 * i + 1, 1, i, False)
                        if count % 2 == 0:
                            first_product(count - 1, 1, steps, False)
                            second_product(count - 2, 0, steps, False)
                            second_product(count - 1, 1, steps, False)
                        else:
                            second_product(count - 1, 0, steps, False)

                    @block.tensor
                    def _(pe):
                        def first_product(e, slot, turn_, first):
                            pe.wait_ge(guide_landed[slot], 16 * turn_ + 16)
                            for c in range(chunks):
                                pair = 2 * (((slot * chunks) + c) % 2)
                                w = width(c)
                                if not (first and slot * chunks + c < 2):
                                    pe.wait_ge(hidden_ready, e * chunks + c - 1)
                                for half in range(2):
                                    for k in range(KC):
                                        at = (half * KC + k) * hidden + c * P
                                        last = pe.matmul(ps[0:w, pair + half, :], wg[:, slot, at:at + w], xT[:, k, :],
                                                         start=(k == 0), stop=(k == KC - 1))
                                last.then_inc(raw_ready, 1)

                        def second_product(e, slot, turn_, first):
                            pe.wait_ge(down_landed[slot], 16 * turn_ + 16)
                            pe.wait_ge(hidden_ready, (e + 1) * chunks)
                            for t in range(NT):
                                if not first:
                                    pe.wait_ge(added, (e - 1) * NT + t + 1)
                                for c in range(chunks):
                                    w = width(c)
                                    last = pe.matmul(ps[:, 4 + t, 0:D], hid[0:w, slot, c, t * P:(t + 1) * P],
                                                     wd[0:w, slot, c * D:(c + 1) * D], start=(c == 0),
                                                     stop=(not bias and c == chunks - 1))
                                if bias:
                                    last = pe.matmul(ps[:, 4 + t, 0:D], ones[0:1, :],
                                                     wd[0:1, slot, chunks * D:(chunks + 1) * D],
                                                     start=False, stop=True)
                                last.then_inc(down_ready, 1)
                        in_order(first_product, second_product, pe.Fori)

                    @block.scalar
                    def _(act):
                        def first_product(e, slot, turn_, first):
                            for c in range(chunks):
                                n2 = (slot * chunks + c) % 2
                                w = width(c)
                                act.wait_ge(raw_ready, e * chunks + c + 1)
                                if not (first and slot * chunks + c < 2):
                                    act.wait_ge(hidden_ready, e * chunks + c - 1)
                                at = 2 * KC * hidden + c
                                nc.scalar.activation(silu[0:w, n2, :], ps[0:w, 2 * n2, :], ACT.Silu,
                                                     bias=wg[0:w, slot, at:at + 1] if bias else 0.0)\
                                    .then_inc(silu_ready, 1)

                        def second_product(e, slot, turn_, first):
                            pass
                        in_order(first_product, second_product, act.Fori)

                    @block.vector
                    def _(dve):
                        def first_product(e, slot, turn_, first):
                            for c in range(chunks):
                                n2 = (slot * chunks + c) % 2
                                w = width(c)
                                dve.wait_ge(silu_ready, e * chunks + c + 1)
                                if not first:
                                    dve.wait_ge(down_ready, (e - 1) * NT)
                                at = 2 * KC * hidden + chunks + c
                                dve.scalar_tensor_tensor(
                                    out=hid[0:w, slot, c, :], in0=ps[0:w, 2 * n2 + 1, :],
                                    scalar=wg[0:w, slot, at:at + 1] if bias else zero[0:w, :],
                                    in1=silu[0:w, n2, :], op0=ALU.add, op1=ALU.mult).then_inc(hidden_ready, 1)

                        def second_product(e, slot, turn_, first):
                            for t in range(NT):
                                dve.wait_ge(down_ready, e * NT + t + 1)
                                if not first:
                                    dve.wait_ge(added, (e - 1) * NT + t + 1)
                                dve.scalar_tensor_tensor(
                                    out=x[:, t, :], in0=ps[:, 4 + t, 0:D], scalar=combine[:, bass.ds(e * NT + t, 1)],
                                    in1=x[:, t, :], op0=ALU.mult, op1=ALU.add).then_inc(added, 1)
                        in_order(first_product, second_product, dve.Fori)

        def route(logits, count, combine, kind, picked=None):
            with ExitStack() as own, signals(nc, "chain", "exp_wanted", "exp_done") as (chain, exp_wanted, exp_done):
                small = sb("small", [P, NT, count], where=own)
                eight = sb("eight", [P, NT, 8], where=own)
                index = sb("index", [P, NT, 8], U32, where=own)
                where_ = sb("where", [P, NT, 8], where=own)
                first = sb("first", [P, NT, count], where=own)
                second = sb("second", [P, NT, count], where=own)
                row = sb("row", [P, 4, NT], where=own)
                pair = sb("pair", [P, 2, NT], where=own)

                def spread(v):
                    return v.unsqueeze(2).broadcast_to([P, NT, count])

                with nc.Block() as block:
                    @block.scalar
                    def _(act):
                        act.wait_ge(exp_wanted, 1)
                        if kind == "pair":
                            nc.scalar.activation(row[:, 0, :], row[:, 0, :], ACT.Exp).then_inc(exp_done, 1)
                        else:
                            nc.scalar.activation(small[:], small[:], ACT.Exp).then_inc(exp_done, 1)
                        act.wait_ge(exp_done, 1)

                    @block.vector
                    def _(dve):
                        link = Chain(dve, chain)
                        if kind == "pair":
                            scores = logits
                        else:
                            link(dve.tensor_reduce(row[:, 1, :], logits, AX.X, ALU.max))
                            link(dve.tensor_tensor(small[:], logits, spread(row[:, 1, :]), ALU.subtract))
                            dve.sem_inc(exp_wanted, 1)
                            dve.wait_ge(exp_done, 1)
                            link(dve.tensor_reduce(row[:, 2, :], small[:], AX.X, ALU.add))
                            link(dve.reciprocal(row[:, 3, :], row[:, 2, :]))
                            link(dve.tensor_tensor(small[:], small[:], spread(row[:, 3, :]), ALU.mult))
                            scores = small[:]
                        for t in range(NT):
                            last = dve.max(eight[:, t, :], scores[:, t, :])
                        link(last)
                        for t in range(NT):
                            last = dve.max_index(index[:, t, :], eight[:, t, :], scores[:, t, :])
                        link(last)
                        link(dve.tensor_copy(where_[:], index[:]))
                        places = iota[:, 0:count].unsqueeze(1).broadcast_to([P, NT, count])
                        dve.tensor_tensor(first[:], places, spread(where_[:, :, 0]), ALU.is_equal).then_inc(chain, 1)
                        chained = dve.tensor_tensor(second[:], places, spread(where_[:, :, 1]), ALU.is_equal)
                        link.count += 1
                        link(chained)
                        if kind == "pair":
                            link(dve.tensor_tensor(row[:, 0, :], eight[:, :, 1], eight[:, :, 0], ALU.subtract))
                            dve.sem_inc(exp_wanted, 1)
                            dve.wait_ge(exp_done, 1)
                            link(dve.tensor_scalar(row[:, 1, :], row[:, 0, :], 1.0, None, ALU.add))
                            link(dve.reciprocal(pair[:, 0, :], row[:, 1, :]))
                            link(dve.tensor_tensor(pair[:, 1, :], pair[:, 0, :], row[:, 0, :], ALU.mult))
                            weight = pair[:, 0, :], pair[:, 1, :]
                        elif kind == "share":
                            link(dve.tensor_tensor(row[:, 0, :], eight[:, :, 0], eight[:, :, 1], ALU.add))
                            link(dve.reciprocal(row[:, 1, :], row[:, 0, :]))
                            link(dve.tensor_tensor(pair[:, 0, :], eight[:, :, 0], row[:, 1, :], ALU.mult))
                            link(dve.tensor_tensor(pair[:, 1, :], eight[:, :, 1], row[:, 1, :], ALU.mult))
                            weight = pair[:, 0, :], pair[:, 1, :]
                        else:
                            weight = eight[:, :, 0], eight[:, :, 1]
                        if picked is not None:
                            link(dve.tensor_tensor(picked, first[:], second[:], ALU.add))
                        link(dve.tensor_tensor(first[:], first[:], spread(weight[0]), ALU.mult))
                        link(dve.tensor_tensor(second[:], second[:], spread(weight[1]), ALU.mult))
                        link(dve.tensor_tensor(combine[:, 0:count * NT].rearrange("p (e t) -> p t e", t=NT),
                                               first[:], second[:], ALU.add))

        def vector_steps(steps):
            with signals(nc, "chain") as (chain,), nc.Block() as block:
                @block.vector
                def _(dve):
                    link = Chain(dve, chain)
                    for step in steps:
                        link(step(dve))

        def rotary_rows(w, name, dst, tmp, bias):
            products = []
            tables = w("cos"), w("sin")
            n_tab = tables[0].shape[1] // S
            for part, (suffix, to) in enumerate((("", dst), ("_swapped", tmp))):
                mat = w.chunks(name + suffix, KC)
                for m in range(4):
                    tab = tables[part][:, (m % n_tab) * S:(m % n_tab + 1) * S].unsqueeze(1).broadcast_to([P, B, S])
                    col = w("b" + name[1:] + suffix)[:, m:m + 1] if bias else zero[:, 0:1]

                    def take(engine, psum, to=to, m=m, tab=tab, col=col):
                        return engine.scalar_tensor_tensor(
                            out=to[:, m, :].rearrange("p (b s) -> p b s", s=S),
                            in0=psum.rearrange("p (b s) -> p b s", s=S), scalar=col, in1=tab,
                            op0=ALU.add, op1=ALU.mult)
                    products.append(([(mat[:, k, m * P:(m + 1) * P], xT[:, k, :]) for k in range(KC)],
                                     P, N, "dve", take))
            return products

        def add_to_x(t):
            return plus(x[:, t, :], x[:, t, :])

        def two_attentions():
            with ExitStack() as own:
                inner = sb("inner", [P, NT, D], where=own)
                mid = sb("mid", [P, NT, D], where=own)

                def tail(w, oT):
                    with ExitStack() as tmp:
                        hT = sb("hT", [P, 4 * KC, N], where=tmp)
                        dense(token_rows(oT, w.chunks("li1_w", 4), lambda t: plus(mid[:, t, :], inner[:, t, :]),
                                         row=w("li1_b", 1)))
                        normalise(mid, xn, [(xT, w("ln3_g"), w("ln3_b"))])
                        li2 = w.chunks("li2_w", KC)
                        dense([([(li2[:, k, m * P:(m + 1) * P], xT[:, k, :]) for k in range(KC)], P, N, "act",
                                activated(hT[:, m, :], ACT.Gelu, w("li2_b")[:, m:m + 1])) for m in range(4 * KC)])
                        dense(token_rows(hT, w.chunks("li3_w", 4 * KC), lambda t: plus(mid[:, t, :], mid[:, t, :]),
                                         row=w("li3_b", 1)))

                weights_here("a1")
                w = weights("a1")
                with ExitStack() as tmp:
                    yT = sb("yT", [P, KC, N], where=tmp)
                    qT = sb("qT", [P, 4, N], where=tmp)
                    kT = sb("kT", [P, 4, N], where=tmp)
                    v = sb("v", [P, NT, H * HP], where=tmp)
                    oT = sb("oT", [P, 4, N], where=tmp)
                    normalise(x, xn)
                    normalise(xn, inner, affine=(w("ln1_g"), w("ln1_b")))
                    normalise(inner, xn, [(xT, w("lnx_g"), w("lnx_b")), (yT, w("lny_g"), w("lny_b"))])
                    dense(feature_rows(w.chunks("wq", KC), xT, qT) + feature_rows(w.chunks("wk", KC), yT, kT)
                          + token_rows(yT, w.chunks("wv", KC), lambda t: copy_to(v[:, t, :]), width=H * HP, engine="both"))
                    self_attention(qT, kT, v, oT, HP ** -0.5, mask=w("later"))
                    tail(w, oT)

                weights_here("a2")
                w = weights("a2")
                normalise(mid, inner, add=[inner], affine=(w("ln2_g"), w("ln2_b")))
                normalise(inner, xn, [(xT, w("lnx_g"), w("lnx_b"))])
                context_norm(w("lny_g"), w("lny_b"))
                with ExitStack() as tmp:
                    q = sb("q", [P, H, N], where=tmp)
                    with ExitStack() as early:
                        qT = sb("qT", [P, 4, N], where=early)
                        dense(feature_rows(w.chunks("wq", KC), xT, qT))
                        dense(head_queries(w.chunks("wkT", 4), qT, q, HP))
                    cross_attention(q, H, HP ** -0.5, dram["zT"], dram["z"], affine=(w("lny_g"), w("lny_b")))
                    oT = sb("oT", [P, 4, N], where=tmp)
                    dense(head_values(w("wv"), q, oT, HP))
                    tail(w, oT)
                return own.pop_all(), inner, mid

        def head_queries(wkT, qT, q, dh):
            per = P // dh
            return [([(wkT[dh * (h % per):dh * (h % per + 1), h // per, :],
                       qT[dh * (h % per):dh * (h % per + 1), h // per, :])], P, N, either(h), copy_to(q[:, h, :]))
                    for h in range(H)]

        def head_values(wv, q, oT, dh):
            per = P // dh
            return [(("rows", [(dh * j, wv[:, (per * m + j) * dh:(per * m + j + 1) * dh], q[:, per * m + j, :])
                               for j in range(per)]), P, N, either(m), copy_to(oT[:, m, :]))
                    for m in range(H // per)]

        def context_norm(gamma, beta):
            names = ("landed0", "landed1", "chain", "var_ready", "std_ready", "z_ready", "turned_ready", "zT_ready",
                     "z_stored0", "z_stored1", "zT_stored0", "zT_stored1")
            with ExitStack() as own, signals(nc, *names) as \
                    (landed0, landed1, chain, var_ready, std_ready, z_ready, turned_ready, zT_ready,
                     z_stored0, z_stored1, zT_stored0, zT_stored1):
                landed, z_stored, zT_stored = (landed0, landed1), (z_stored0, z_stored1), (zT_stored0, zT_stored1)
                raw = sb("raw", [P, 2, KCH, CD], where=own)
                z = sb("z", [P, 2, KCH, CD], where=own)
                zT = sb("zT", [P, 2, KPAD], where=own)
                stats = sb("stats", [P, KCH, 6], where=own)
                means = sb("means", [P, KCH], where=own)
                apart = sb("apart", [P, KCH], where=own)
                dev = sb("dev", [P, KCH], where=own)
                rdev = sb("rdev", [P, KCH], where=own)
                steps = B // 2
                with nc.Block() as block:
                    @block.sync
                    def _(sp):
                        def fetch(step, i):
                            sp.dma_start(raw[:, i], dram["ctx"][bass.ds(2 * step + i, 1)]
                                         .rearrange("b p (k d) -> (b p) k d", d=CD)).then_inc(landed[i], 16)

                        def store(step, i):
                            b = 2 * step + i
                            sp.wait_ge(z_ready, b + 1)
                            sp.dma_start(dram["z"][bass.ds(b, 1)].rearrange("b p (k d) -> (b p) k d", d=CD), z[:, i])\
                                .then_inc(z_stored[i], 16)
                            sp.wait_ge(zT_ready, 4 * b + 4)
                            sp.dma_start(dram["zT"][bass.ds(b, 1)].rearrange("b p k -> (b p) k"), zT[:, i, 0:KEYS])\
                                .then_inc(zT_stored[i], 16)
                        fetch(0, 0)
                        fetch(0, 1)
                        with sp.Fori(0, steps - 1) as step:
                            for i in range(2):
                                store(step, i)
                                fetch(step + 1, i)
                        for i in range(2):
                            store(steps - 1, i)
                        for i in range(2):
                            sp.wait_ge(z_stored[i], 16 * steps)
                            sp.wait_ge(zT_stored[i], 16 * steps)

                    @block.vector
                    def _(dve):
                        def one(step, i, first):
                            b = 2 * step + i
                            dve.wait_ge(landed[i], 16 * step + 16)
                            for k in range(KCH):
                                last = dve.bn_stats(stats[:, k, :], raw[:, i, k, :])
                            last.then_inc(chain, 1)
                            dve.wait_ge(chain, 7 * b + 1)
                            dve.tensor_tensor(apart[:], stats[:, :, 1], stats[:, :, 4], ALU.subtract)
                            dve.tensor_tensor(means[:], stats[:, :, 1], stats[:, :, 4], ALU.add)
                            dve.tensor_tensor(dev[:], stats[:, :, 2], stats[:, :, 5], ALU.add).then_inc(chain, 1)
                            dve.wait_ge(chain, 7 * b + 2)
                            dve.tensor_scalar(means[:], means[:], 0.5, None, ALU.mult)
                            dve.tensor_scalar(dev[:], dev[:], 1.0 / CD, EPS, ALU.mult, ALU.add)
                            dve.scalar_tensor_tensor(out=apart[:], in0=apart[:], scalar=0.25, in1=apart[:],
                                                     op0=ALU.mult, op1=ALU.mult).then_inc(chain, 1)
                            dve.wait_ge(chain, 7 * b + 3)
                            dve.tensor_tensor(dev[:], dev[:], apart[:], ALU.add).then_inc(var_ready, 1)
                            dve.wait_ge(std_ready, b + 1)
                            dve.reciprocal(rdev[:], dev[:]).then_inc(chain, 4)
                            dve.wait_ge(chain, 7 * b + 7)
                            if not first:
                                dve.wait_ge(z_stored[i], 16 * step)
                                dve.wait_ge(turned_ready, 4 * b - 4)
                            for k in range(KCH):
                                last = dve.tensor_scalar(z[:, i, k, :], raw[:, i, k, :], means[:, k:k + 1],
                                                         rdev[:, k:k + 1], ALU.subtract, ALU.mult)
                            last.then_inc(z_ready, 1)
                        one(0, 0, True)
                        one(0, 1, True)
                        with dve.Fori(1, steps) as step:
                            one(step, 0, False)
                            one(step, 1, False)

                    @block.tensor
                    def _(pe):
                        def one(step, i, first):
                            b = 2 * step + i
                            pe.wait_ge(z_ready, b + 1)
                            for g in range(4):
                                if not first:
                                    pe.wait_ge(zT_ready, 4 * b - 8 + g + 1)
                                for k in range(4 * g, min(4 * g + 4, KCH)):
                                    rows = P if k < KCH - 1 else KLAST
                                    last = pe.transpose(ps[:, 4 * i + g, (k % 4) * P:(k % 4) * P + rows],
                                                        z[0:rows, i, k, :], ident[0:rows, 0:rows])
                                last.then_inc(turned_ready, 1)
                        one(0, 0, True)
                        one(0, 1, True)
                        with pe.Fori(1, steps) as step:
                            one(step, 0, False)
                            one(step, 1, False)

                    @block.scalar
                    def _(act):
                        def one(step, i, first):
                            b = 2 * step + i
                            act.wait_ge(var_ready, b + 1)
                            nc.scalar.activation(dev[:], dev[:], ACT.Sqrt).then_inc(std_ready, 1)
                            if not first:
                                act.wait_ge(zT_stored[i], 16 * step)
                            for g in range(4):
                                w = min(BANK, KEYS - g * BANK)
                                act.wait_ge(turned_ready, 4 * b + g + 1)
                                nc.scalar.activation(zT[:, i, g * BANK:g * BANK + w], ps[:, 4 * i + g, 0:w],
                                                     ACT.Identity, bias=beta, scale=gamma).then_inc(zT_ready, 1)
                        one(0, 0, True)
                        one(0, 1, True)
                        with act.Fori(1, steps) as step:
                            one(step, 0, False)
                            one(step, 1, False)

        def inner_attention(name, rotary, biases, out_row, finish):
            weights_here(name)
            w = weights(name)
            with ExitStack() as tmp:
                qT = sb("qT", [P, 4, N], where=tmp)
                kT = sb("kT", [P, 4, N], where=tmp)
                v = sb("v", [P, NT, H * HP], where=tmp)
                oT = sb("oT", [P, 4, N], where=tmp)
                values = token_rows(xT, w.chunks("wv", KC), lambda t: copy_to(v[:, t, :]),
                                    row=w("bv", 1) if biases else None, width=H * HP, engine="both")
                if rotary:
                    with ExitStack() as early:
                        qs = sb("qs", [P, 4, N], where=early)
                        ks = sb("ks", [P, 4, N], where=early)
                        dense(rotary_rows(w, "wq", qT, qs, biases) + rotary_rows(w, "wk", kT, ks, biases) + values)
                        vector_steps([lambda dve: dve.tensor_tensor(qT[:], qT[:], qs[:], ALU.add),
                                      lambda dve: dve.tensor_tensor(kT[:], kT[:], ks[:], ALU.add)])
                else:
                    dense(feature_rows(w.chunks("wq", KC), xT, qT, w("bq")) + feature_rows(w.chunks("wk", KC), xT, kT, w("bk"))
                          + values)
                self_attention(qT, kT, v, oT, (D // H) ** -0.5)
                dense(token_rows(oT, w.chunks("wo", 4), finish, row=w(out_row, 1)))

        def many_head_cross(name, dh, scale, row):
            weights_here(name)
            w = weights(name)
            per = H * dh // P
            with ExitStack() as tmp:
                q = sb("q", [P, H, N], where=tmp)
                with ExitStack() as early:
                    qT = sb("qT", [P, per, N], where=early)
                    dense(feature_rows(w.chunks("wq", KC), xT, qT))
                    dense(head_queries(w.chunks("wkT", per), qT, q, dh))
                cross_attention(q, H, scale, dram["ctxT"], dram["ctx"])
                oT = sb("oT", [P, per, N], where=tmp)
                dense(head_values(w("wv"), q, oT, dh))
                dense(token_rows(oT, w.chunks("wo", per), add_to_x, row=w("bo", 1) if row else None))

        def one_head_cross():
            weights_here("l1x")
            w = weights("l1x")
            with ExitStack() as tmp:
                q = sb("q", [P, 1, N], where=tmp)
                qT = sb("qT", [P, KC, N], where=tmp)
                term = sb("term", [S, B], where=tmp)
                dense(feature_rows(w.chunks("wq", KC), xT, qT, w("bq")))
                wkT = w.chunks("wkT", KC)
                bk = w("bk")
                dense([([(wkT[:, k, :], qT[:, k, :]) for k in range(KC)], P, N, "act", copy_to(q[:, 0, :]))] +
                      [([(qT[:, k, b * S:(b + 1) * S], bk[:, k:k + 1]) for k in range(KC)], S, 1, "dve",
                        copy_to(term[:, b:b + 1])) for b in range(B)])
                cross_attention(q, 1, 1.0, dram["ctxT"], dram["ctx"], shift=term)
                wv = w("wv").rearrange("p (k n) -> p k n", k=1)
                dense(token_rows(q, wv, add_to_x, row=w("bv", 1)))

        def recurrence():
            weights_here("l1a")
            w = weights("l1a")
            with ExitStack() as tmp:
                mixed = sb("mixed", [P, 3, KC, N], where=tmp)
                rest = sb("rest", [P, 3, KC], where=tmp)
                decay = sb("decay", [P, KC], where=tmp)
                ndecay = sb("ndecay", [P, KC], where=tmp)
                k = sb("k", [P, KC, N], where=tmp)
                v = sb("v", [P, KC, N], where=tmp)
                r = sb("r", [P, KC, N], where=tmp)
                mix = w("mix").rearrange("p (m k) -> p m k", k=KC)
                with signals(nc, "chain", "decay_ready", "part_ready") as (chain, decay_ready, part_ready), \
                        nc.Block() as block:
                    @block.vector
                    def _(dve):
                        link = Chain(dve, chain)
                        link(dve.tensor_scalar(rest[:], mix, -1.0, 1.0, ALU.mult, ALU.add))
                        for m in range(3):
                            for c in range(KC):
                                last = dve.tensor_scalar(mixed[:, m, c, :], xT[:, c, :], mix[:, m, c:c + 1], None,
                                                         ALU.mult)
                        link(last)
                        for m in range(3):
                            for c in range(KC):
                                here = mixed[:, m, c, :].rearrange("p (b s) -> p b s", s=S)
                                before = xT[:, c, :].rearrange("p (b s) -> p b s", s=S)
                                last = dve.scalar_tensor_tensor(
                                    out=here[:, :, 1:S], in0=before[:, :, 0:S - 1], scalar=rest[:, m, c:c + 1],
                                    in1=here[:, :, 1:S], op0=ALU.mult, op1=ALU.add)
                        link(last)
                        dve.wait_ge(decay_ready, 1)
                        link(dve.tensor_scalar(ndecay[:], decay[:], -1.0, None, ALU.mult))

                    @block.scalar
                    def _(act):
                        nc.scalar.activation(decay[:], w("decay"), ACT.Exp).then_inc(decay_ready, 1)
                dense(feature_rows(w.chunks("wk", KC), mixed[:, 0], k) + feature_rows(w.chunks("wv", KC), mixed[:, 1], v)
                      + [(terms, rows, cols, "act", activated(r[:, m, :], ACT.Sigmoid)) for m, (terms, rows, cols, _, _)
                         in enumerate(feature_rows(w.chunks("wr", KC), mixed[:, 2], r))])

                fall = sb("fall", [P, KC, N], where=tmp)
                top = sb("top", [P, KC, N + 1], where=tmp)
                keep = sb("keep", [P, KC, N], where=tmp)
                new = sb("new", [P, KC, N], where=tmp)
                num = sb("num", [P, KC, N + 1], where=tmp)
                den = sb("den", [P, KC, N + 1], where=tmp)
                peak = mixed[:, 0]
                boost = mixed[:, 1]
                e_old = mixed[:, 2]

                def split(t):
                    return t.rearrange("p k (b s) -> p k b s", s=S)

                with signals(nc, "chain", "arguments", "exponents") as (chain, arguments, exponents), nc.Block() as block:
                    @block.scalar
                    def _(act):
                        act.wait_ge(arguments, 1)
                        nc.scalar.activation(keep[:], keep[:], ACT.Exp).then_inc(exponents, 1)
                        nc.scalar.activation(new[:], new[:], ACT.Exp).then_inc(exponents, 1)
                        act.wait_ge(arguments, 2)
                        nc.scalar.activation(e_old, e_old, ACT.Exp).then_inc(exponents, 1)
                        nc.scalar.activation(boost, boost, ACT.Exp).then_inc(exponents, 1)

                    @block.vector
                    def _(dve):
                        link = Chain(dve, chain)
                        link(dve.memset(fall[:], 0.0))
                        for c in range(KC):
                            last = dve.tensor_scalar(fall[:, c, :], fall[:, c, :], ndecay[:, c:c + 1], None, ALU.add)
                        link(last)
                        link(dve.memset(split(fall[:])[:, :, :, 0:1], -1e38))
                        for c in range(KC):
                            last = dve.tensor_tensor_scan(top[:, c, 1:N + 1], fall[:, c, :], k[:, c, :], 0.0,
                                                          ALU.add, ALU.max)
                        link(last)
                        link(dve.tensor_tensor(new[:], k[:], top[:, :, 1:N + 1], ALU.subtract))
                        link(dve.memset(top[:, :, 0:1], -1e38))
                        link(dve.tensor_tensor(keep[:], fall[:], top[:, :, 0:N], ALU.add))
                        link(dve.memset(split(keep[:])[:, :, :, 0:1], -1e38))
                        link(dve.tensor_tensor(keep[:], keep[:], top[:, :, 1:N + 1], ALU.subtract))
                        dve.sem_inc(arguments, 1)
                        dve.wait_ge(exponents, 2)
                        for c in range(KC):
                            last = dve.tensor_tensor_scan(den[:, c, 1:N + 1], keep[:, c, :], new[:, c, :], 0.0,
                                                          ALU.mult, ALU.add)
                        link(last)
                        link(dve.tensor_tensor(new[:], new[:], v[:], ALU.mult))
                        for c in range(KC):
                            last = dve.tensor_tensor_scan(num[:, c, 1:N + 1], keep[:, c, :], new[:, c, :], 0.0,
                                                          ALU.mult, ALU.add)
                        link(last)
                        link(dve.memset(top[:, :, 0:N:S], -1e38))
                        link(dve.memset(num[:, :, 0:N:S], 0.0))
                        link(dve.memset(den[:, :, 0:N:S], 0.0))
                        for c in range(KC):
                            last = dve.tensor_scalar(boost[:, c, :], k[:, c, :], w("first")[:, c:c + 1], None, ALU.add)
                        link(last)
                        link(dve.tensor_tensor(peak, boost, top[:, :, 0:N], ALU.max))
                        link(dve.tensor_tensor(e_old, top[:, :, 0:N], peak, ALU.subtract))
                        link(dve.tensor_tensor(boost, boost, peak, ALU.subtract))
                        dve.sem_inc(arguments, 1)
                        dve.wait_ge(exponents, 4)
                        link(dve.tensor_tensor(num[:, :, 0:N], num[:, :, 0:N], e_old, ALU.mult))
                        link(dve.tensor_tensor(den[:, :, 0:N], den[:, :, 0:N], e_old, ALU.mult))
                        link(dve.tensor_tensor(den[:, :, 0:N], den[:, :, 0:N], boost, ALU.add))
                        link(dve.tensor_tensor(boost, boost, v[:], ALU.mult))
                        link(dve.tensor_tensor(num[:, :, 0:N], num[:, :, 0:N], boost, ALU.add))
                        link(dve.reciprocal(keep[:], den[:, :, 0:N]))
                        link(dve.tensor_tensor(keep[:], keep[:], r[:], ALU.mult))
                        link(dve.tensor_tensor(keep[:], keep[:], num[:, :, 0:N], ALU.mult))
                dense(token_rows(keep, w.chunks("wo", KC), add_to_x))

        def capacity_experts():
            weights_here("l1f")
            w = weights("l1f")
            E, F, CAP = 8, 1024, 2 * N // 8
            FCH = F // P
            assert CAP == P
            with ExitStack() as own:
                logits = sb("logits", [P, NT, E], where=own)
                combine = sb("combine", [P, E * NT], where=own)
                picked = sb("picked", [P, NT, E], where=own)
                rank = sb("rank", [P, NT, E], where=own)
                place = sb("place", [P, NT, E, P], where=own)
                shareT = sb("shareT", [P, E, N], where=own)
                taken = sb("taken", [P, KC, E * P], where=own)
                y = sb("y", [P, E, D], where=own)
                dense(token_rows(xT, w.chunks("router", KC), lambda t: copy_to(logits[:, t, :]), width=E))
                route(logits[:], E, combine, "all", picked=picked[:])
                dense([([(w("ones"), picked[:, u, :]) for u in range(t)] + [(w("earlier"), picked[:, t, :])],
                        P, E, "dve", copy_to(rank[:, t, :])) for t in range(NT)])

                def one_hot(scalar):
                    steps = []
                    for t in range(NT):
                        for e in range(E):
                            steps.append((t, e, scalar(t, e)))
                    with signals(nc, "placed") as (placed,), nc.Block() as block:
                        @block.vector
                        def _(dve):
                            for t, e, s in steps:
                                dve.tensor_scalar(place[:, t, e, :], iota[:], rank[:, t, e:e + 1], s,
                                                  ALU.is_equal, ALU.mult).then_inc(placed, 1)
                            dve.wait_ge(placed, len(steps))
                one_hot(lambda t, e: picked[:, t, e:e + 1])
                dense([([(xn[:, t, c * P:(c + 1) * P],
                          place[:, t, 4 * g:4 * g + 4, :].rearrange("p e s -> p (e s)")) for t in range(NT)],
                        P, BANK, either(g), copy_to(taken[:, c, g * BANK:(g + 1) * BANK]))
                       for c in range(KC) for g in range(2)])
                one_hot(lambda t, e: combine[:, e * NT + t:e * NT + t + 1])
                dense([((None, [place[:, t, e, :] for t in range(NT)]), P, N, either(e), copy_to(shareT[:, e, :]))
                       for e in range(E)])

                names = ("w1_landed0", "w1_landed1", "w2_landed0", "w2_landed1", "raw_ready", "hidden_ready",
                         "y_ready", "y_kept")
                with ExitStack() as inner, signals(nc, *names) as \
                        (w1_landed0, w1_landed1, w2_landed0, w2_landed1, raw_ready, hidden_ready, y_ready, y_kept):
                    w1_landed, w2_landed = (w1_landed0, w1_landed1), (w2_landed0, w2_landed1)
                    w1 = sb("w1", [P, 2, KC, F], where=inner)
                    w2 = sb("w2", [P, 2, FCH, D], where=inner)
                    hid = sb("hid", [P, 2, FCH, P], where=inner)
                    with nc.Block() as block:
                        @block.sync
                        def _(sp):
                            for e in range(E):
                                i = e % 2
                                if e >= 2:
                                    sp.wait_ge(raw_ready, 2 * (e - 1))
                                sp.dma_start(w1[:, i], dram["l1f_w1"][e].rearrange("p (k f) -> p k f", k=KC))\
                                    .then_inc(w1_landed[i], 16)
                                if e >= 2:
                                    sp.wait_ge(y_ready, e - 1)
                                sp.dma_start(w2[:, i], dram["l1f_w2"][e].rearrange("p (k f) -> p k f", k=FCH))\
                                    .then_inc(w2_landed[i], 16)

                        @block.tensor
                        def _(pe):
                            def first_product(e):
                                i = e % 2
                                pe.wait_ge(w1_landed[i], 16 * (e // 2 + 1))
                                for g in range(2):
                                    if e >= 2:
                                        pe.wait_ge(hidden_ready, 2 * (e - 2) + g + 1)
                                    for m in range(4 * g, 4 * g + 4):
                                        for c in range(KC):
                                            last = pe.matmul(ps[:, 2 * i + g, (m % 4) * P:(m % 4 + 1) * P],
                                                             w1[:, i, c, m * P:(m + 1) * P],
                                                             taken[:, c, e * P:(e + 1) * P],
                                                             start=(c == 0), stop=(c == KC - 1))
                                    last.then_inc(raw_ready, 1)

                            def second_product(e):
                                i = e % 2
                                pe.wait_ge(w2_landed[i], 16 * (e // 2 + 1))
                                pe.wait_ge(hidden_ready, 2 * (e + 1))
                                if e >= 2:
                                    pe.wait_ge(y_kept, e - 1)
                                for m in range(FCH):
                                    last = pe.matmul(ps[:, 4 + i, 0:D], hid[:, i, m, :], w2[:, i, m, :],
                                                     start=(m == 0), stop=(m == FCH - 1))
                                last.then_inc(y_ready, 1)

                            first_product(0)
                            for e in range(E):
                                if e + 1 < E:
                                    first_product(e + 1)
                                second_product(e)

                        @block.scalar
                        def _(act):
                            for e in range(E):
                                i = e % 2
                                for g in range(2):
                                    act.wait_ge(raw_ready, 2 * e + g + 1)
                                    if e >= 2:
                                        act.wait_ge(y_ready, e - 1)
                                    nc.scalar.activation(hid[:, i, 4 * g:4 * g + 4, :],
                                                         ps[:, 2 * i + g, :].rearrange("p (m s) -> p m s", s=P),
                                                         ACT.Gelu_apprx_tanh).then_inc(hidden_ready, 1)

                        @block.vector
                        def _(dve):
                            for e in range(E):
                                dve.wait_ge(y_ready, e + 1)
                                dve.tensor_copy(y[:, e, :], ps[:, 4 + e % 2, 0:D]).then_inc(y_kept, 1)
                dense([([(shareT[:, e, t * P:(t + 1) * P], y[:, e, :]) for e in range(E)] + [(ones[0:1, :], w("bias", 1))],
                        P, D, "dve", add_to_x(t)) for t in range(NT)])

        def gated_experts(name, routed, total, hidden, kind, bias=False):
            weights_here(name)
            w = weights(name)
            with ExitStack() as own:
                combine = sb("combine", [P, total * NT], where=own)
                width = routed + (kind == "share")
                logits = sb("logits", [P, NT, width], where=own)
                dense(token_rows(xT, w.chunks("router", KC), lambda t: copy_to(logits[:, t, :]), width=width))
                route(logits[:, :, 0:routed], routed, combine, kind)
                shared = combine[:, routed * NT:total * NT].rearrange("p (e t) -> p e t", t=NT)
                with signals(nc, "chain", "gate_ready") as (chain, gate_ready), nc.Block() as block:
                    if kind == "share":
                        @block.scalar
                        def _(act):
                            nc.scalar.activation(std[:], logits[:, :, routed], ACT.Sigmoid).then_inc(gate_ready, 1)

                    @block.vector
                    def _(dve):
                        link = Chain(dve, chain)
                        if kind == "share":
                            dve.wait_ge(gate_ready, 1)
                            link(dve.tensor_copy(shared, std[:].unsqueeze(1).broadcast_to([P, total - routed, NT])))
                        else:
                            link(dve.memset(shared, 1.0))
                experts(dram[name + "_guide"], dram[name + "_down"], total, hidden, combine, bias)

        if LAYERS >= 1:
            held, inner, mid = two_attentions()
            pending = [inner, mid]
        else:
            held, pending = ExitStack(), []
        if LAYERS >= 2:
            normalise(x, xn, [(xT, None, None)], add=pending)
            weights_used = weights("l0a")
            inner_attention("l0a", True, True, "bo", lambda t: plus(mid[:, t, :], xn[:, t, :]))
            normalise(mid, inner, affine=(weights_used("gamma"), weights_used("beta")))
            pending = [inner]
        with held:
            if LAYERS == 2 or LAYERS == 1:
                normalise(x, xn, add=pending)
            if LAYERS >= 3:
                normalise(x, xn, [(xT, None, None)], add=pending)
        if LAYERS >= 3:
            gated_experts("l0f", 8, 10, 352, "pair")
        if LAYERS >= 4:
            normalise(x, xn, [(xT, None, None)])
            one_head_cross()
        if LAYERS >= 5:
            normalise(x, xn, [(xT, None, None)])
            recurrence()
        if LAYERS >= 6:
            normalise(x, xn, [(xT, None, None)])
            capacity_experts()
        if LAYERS >= 7:
            normalise(x, xn, [(xT, None, None)])
            many_head_cross("l2x", 64, 64 ** -0.5, True)
        if LAYERS >= 8:
            normalise(x, xn, [(xT, None, None)])
            inner_attention("l2a", True, False, "bu", add_to_x)
        if LAYERS >= 9:
            normalise(x, xn, [(xT, None, None)])
            gated_experts("l2f", 8, 9, 256, "all", bias=True)
        if LAYERS >= 10:
            normalise(x, xn, [(xT, None, None)])
            many_head_cross("l3x", HP, (D // H) ** -0.5, False)
        if LAYERS >= 11:
            normalise(x, xn, [(xT, None, None)])
            inner_attention("l3a", False, True, "bd", add_to_x)
        if LAYERS >= 12:
            normalise(x, xn, [(xT, None, None)])
            gated_experts("l3f", 16, 22, 128, "share")

        with signals(nc, "out_stored") as (out_stored,), nc.Block() as block:
            @block.sync
            def _(sp):
                sp.dma_start(out.rearrange("(t p) d -> p t d", p=P), x[:]).then_inc(out_stored, 16)
                sp.wait_ge(out_stored, 16)


def chunked(w):
    k = w.shape[0] // P
    return w.reshape(k, P, -1).transpose(1, 0, 2).reshape(P, -1)


def columns(v):
    return v.reshape(-1, P).T


def row(v):
    out = np.zeros((P, v.size), np.float32)
    out[0] = v.reshape(-1)
    return out


def spread(v):
    return np.broadcast_to(v.reshape(1, -1), (P, v.size))


def pad_heads(w):
    out = np.zeros(w.shape[:-1] + (H, HP), np.float32)
    out[..., 0:D // H] = w.reshape(w.shape[:-1] + (H, D // H))
    return out.reshape(w.shape[:-1] + (H * HP,))


def pad_rows(w):
    return np.ascontiguousarray(pad_heads(w.T).T)


def swapped(w):
    return w.reshape(w.shape[:-1] + (-1, 2))[..., ::-1].reshape(w.shape)


def rotary_tables(per_head):
    half = D // H // 2 if per_head else D // 2
    theta = (np.float32(1.0) / np.float32(10000.0) ** (np.arange(half, dtype=np.float32) / np.float32(half)))
    angle = np.arange(S, dtype=np.float32)[:, None] * theta.astype(np.float32)[None, :]
    pair = np.arange(D) // 2 % half
    sign = np.where(np.arange(D) % 2, 1.0, -1.0).astype(np.float32)
    tables = []
    for t in (np.cos(angle)[:, pair], np.sin(angle)[:, pair] * sign):
        t = chunked(np.ascontiguousarray(pad_heads(t.astype(np.float32)).T))
        tables.append(t[:, 0:S] if per_head else t)
    return tables


def lay_out(a):
    packs = {}

    def heads_last(w):
        return w.transpose(1, 0, 2).reshape(w.shape[1], -1)

    for name, pre in (("a1", "L0_xattn_a1_"), ("a2", "L0_xattn_a2_")):
        g = lambda k: a[pre + k]
        packs[name] = dict(
            wq=chunked(heads_last(g("wq"))), li1_w=chunked(g("li1_w")), li2_w=chunked(g("li2_w")),
            li3_w=chunked(g("li3_w")), li1_b=row(g("li1_b")), li3_b=row(g("li3_b")), li2_b=columns(g("li2_b")),
            **{k: columns(g(k)) for k in ("lnx_g", "lnx_b", "lny_g", "lny_b", "ln3_g", "ln3_b")})
    at = np.arange(S)
    packs["a1"].update(wk=chunked(heads_last(a["L0_xattn_a1_wk"])), wv=chunked(heads_last(a["L0_xattn_a1_wv"])),
                       ln1_g=spread(a["L0_xattn_ln1_g"]), ln1_b=spread(a["L0_xattn_ln1_b"]),
                       later=np.tile((at[None, :] > at[:, None]).astype(np.float32), (2, 1)))
    packs["a2"].update(wkT=chunked(a["L0_xattn_a2_wk"].transpose(0, 2, 1).reshape(H * HP, CD)),
                       wv=heads_last(a["L0_xattn_a2_wv"]),
                       ln2_g=spread(a["L0_xattn_ln2_g"]), ln2_b=spread(a["L0_xattn_ln2_b"]))
    cos, sin = rotary_tables(True)
    wqkv, bqkv = a["L0_attn_Wqkv"], a["L0_attn_bqkv"]
    packs["l0a"] = dict(wv=chunked(pad_heads(wqkv[:, 2 * D:])), bv=row(pad_heads(bqkv[2 * D:])),
                        wo=chunked(pad_rows(a["L0_attn_Wo"])),
                        bo=row(a["L0_attn_bo"]), gamma=spread(a["L0_attn_gamma"]), beta=spread(a["L0_attn_beta"]),
                        cos=cos, sin=sin)
    cos, sin = rotary_tables(False)
    packs["l2a"] = dict(wv=chunked(pad_heads(a["L2_attn_Wv"].T)), wo=chunked(pad_rows(a["L2_attn_Wu"].T)), bu=row(a["L2_attn_bu"]),
                        cos=cos, sin=sin)
    for n, m, b in (("q", wqkv[:, 0:D], bqkv[0:D]), ("k", wqkv[:, D:2 * D], bqkv[D:2 * D])):
        packs["l0a"].update({"w" + n: chunked(pad_heads(m)), f"w{n}_swapped": chunked(pad_heads(swapped(m))),
                             "b" + n: columns(pad_heads(b)), f"b{n}_swapped": columns(pad_heads(swapped(b)))})
        m = a["L2_attn_W" + n].T
        packs["l2a"].update({"w" + n: chunked(pad_heads(m)), f"w{n}_swapped": chunked(pad_heads(swapped(m)))})
    packs["l0f"] = dict(router=chunked(a["L0_ffn_Wg"]))
    packs["l1x"] = dict(wq=chunked(a["L1_xattn_Wq"]), wkT=chunked(a["L1_xattn_Wk"].T), wv=a["L1_xattn_Wv"],
                        bq=columns(a["L1_xattn_bq"]), bk=columns(a["L1_xattn_bk"]), bv=row(a["L1_xattn_bv"]))
    packs["l1a"] = dict(**{"w" + n: chunked(a["L1_attn_W" + n].T) for n in "kvro"},
                        decay=columns(a["L1_attn_time_decay"]), first=columns(a["L1_attn_time_first"]),
                        mix=np.concatenate([columns(a["L1_attn_time_mix_" + n]) for n in "kvr"], 1))
    p = np.arange(P)
    packs["l1f"] = dict(router=chunked(a["L1_ffn_w_router"]), bias=row(a["L1_ffn_bias"]),
                        ones=np.ones((P, P), np.float32), earlier=(p[:, None] < p[None, :]).astype(np.float32))
    packs["l2x"] = dict(wq=chunked(a["L2_xattn_Wq"]), wkT=chunked(a["L2_xattn_Wk"].T), wv=a["L2_xattn_Wv"],
                        wo=chunked(a["L2_xattn_Wo"]), bo=row(a["L2_xattn_bo"]))
    packs["l2f"] = dict(router=chunked(a["L2_ffn_gate_w"].T))
    packs["l3x"] = dict(wq=chunked(pad_heads(a["L3_xattn_Wq"].T)),
                        wkT=chunked(pad_rows(a["L3_xattn_Wkv"][0:D])),
                        wv=pad_heads(a["L3_xattn_Wkv"][D:].T),
                        wo=chunked(pad_rows(a["L3_xattn_Wo"].T)))
    packs["l3a"] = dict(wq=chunked(pad_heads(a["L3_attn_Wq"])), wk=chunked(pad_heads(a["L3_attn_Wk"])),
                        bq=columns(pad_heads(a["L3_attn_bq"])), bk=columns(pad_heads(a["L3_attn_bk"])),
                        wv=chunked(pad_heads(a["L3_attn_Wv"])), bv=row(pad_heads(a["L3_attn_bv"])),
                        wo=chunked(pad_rows(a["L3_attn_Wd"])),
                        bd=row(a["L3_attn_bd"]))
    packs["l3f"] = dict(router=chunked(np.concatenate([a["L3_ffn_gate_w"].T, a["L3_ffn_shared_gate_w"].T], 1)))
    return packs


def guides(gate, up):
    return np.stack([np.concatenate([chunked(g), chunked(u)], 1) for g, u in zip(gate, up)])


def downs(down):
    e, f, d = down.shape
    pad = np.zeros((e, -(-f // P) * P, d), np.float32)
    pad[:, 0:f] = down
    return np.stack([chunked(w) for w in pad])


def expert_arrays(a):
    out = {}
    halves = lambda w: w.reshape(D, 2, -1).transpose(1, 0, 2)
    out["l0f_guide"] = guides(np.concatenate([a["L0_ffn_W1"], halves(a["L0_ffn_Ws1"])]),
                              np.concatenate([a["L0_ffn_W2"], halves(a["L0_ffn_Ws2"])]))
    out["l0f_down"] = downs(np.concatenate([a["L0_ffn_W3"], a["L0_ffn_Ws3"].reshape(2, -1, D)]))
    out["l1f_w1"] = np.stack([chunked(w) for w in a["L1_ffn_w1"]])
    out["l1f_w2"] = np.stack([chunked(w) for w in a["L1_ffn_w2"]])
    g = lambda k: np.concatenate([a["L2_ffn_" + k], a["L2_ffn_s" + k][None]])
    out["l2f_guide"] = np.concatenate([guides(g("w1"), g("w3")), np.stack([columns(b) for b in g("b1")]),
                                       np.stack([columns(b) for b in g("b3")])], 2)
    out["l2f_down"] = np.concatenate([downs(g("w2")), np.stack([row(b) for b in g("b2")])], 2)
    gu = a["L3_ffn_w_gate_up"]
    wide = lambda w: np.concatenate([w, np.zeros((6 * P - w.shape[0], D), np.float32)]).reshape(6, P, D)
    out["l3f_guide"] = guides(
        np.concatenate([gu[:, :, 0:P], wide(a["L3_ffn_shared_w_gate"]).transpose(0, 2, 1)]),
        np.concatenate([gu[:, :, P:], wide(a["L3_ffn_shared_w_up"]).transpose(0, 2, 1)]))
    out["l3f_down"] = downs(np.concatenate([a["L3_ffn_w_down"], wide(a["L3_ffn_shared_w_down"].T)]))
    return out


def kernel(**inputs):
    import concourse.bacc as bacc
    from concourse.bass_utils import run_bass_kernel_spmd

    a = {n: np.asarray(v) for n, v in inputs.items()}
    arrays, fields = {"x": a["x"].reshape(N, D)}, {}
    for name, parts in lay_out(a).items():
        at, place = 0, {}
        for part, v in parts.items():
            place[part] = (at, v.shape[1])
            at += v.shape[1]
        fields[name] = (place, at)
        arrays[name] = np.concatenate(list(parts.values()), 1)
    arrays.update(expert_arrays(a))
    ctx = a["ctx_512"]
    padded = np.zeros((B, KPAD, CD), np.float32)
    padded[:, 0:KEYS] = ctx
    arrays["ctx"] = padded.reshape(B, KCH, P, CD).transpose(0, 2, 1, 3).reshape(B, P, KPAD)
    arrays["ctxT"] = ctx.transpose(0, 2, 1)
    arrays = {n: np.ascontiguousarray(v) for n, v in arrays.items()}

    nc = bacc.Bacc("TRN2", target_bir_lowering=False, num_devices=1)
    dram = {n: nc.dram_tensor(n + "_in", v.shape, mybir.dt.from_np(v.dtype), kind="ExternalInput").ap()
            for n, v in arrays.items()}
    out = nc.dram_tensor("out", (N, D), F32, kind="ExternalOutput").ap()
    dram["z"] = nc.dram_tensor("z", (B, P, KPAD), F32, kind="Internal").ap()
    dram["zT"] = nc.dram_tensor("zT", (B, P, KEYS), F32, kind="Internal").ap()
    perceiver_kernel(nc, dram, fields, out)
    r = run_bass_kernel_spmd(nc, [{n + "_in": v for n, v in arrays.items()}], core_ids=[0])
    return r.results[0]["out"].reshape(B, S, D)
```

```python
from contextlib import ExitStack, contextmanager

import numpy as np

import concourse.bass as bass
from concourse import mybir

ACT = mybir.ActivationFunctionType
ALU = mybir.AluOpType
AX = mybir.AxisListType
F32 = mybir.dt.float32
F32R = mybir.dt.float32r
U32 = mybir.dt.uint32

P = 128
B, S, D = 8, 64, 256
N = B * S
NT = N // P
KC = D // P
KEYS, CD = 1601, 128
KCH = -(-KEYS // P)
KPAD = KCH * P
KEVEN = KEYS + KEYS % 2
KLAST = KEYS - (KCH - 1) * P
H = 16
HP = 32
BANK = 512
EPS = 1e-5
LAYERS = 12


@contextmanager
def signals(nc, *names):
    with ExitStack() as stack:
        sems = [stack.enter_context(nc.semaphore(n)) for n in names]
        yield sems
        for s in sems:
            nc.sync.sem_clear(s)
        nc.all_engine_barrier()


class Chain:

    def __init__(self, engine, sem):
        self.engine, self.sem, self.count = engine, sem, 0

    def __call__(self, instruction):
        self.count += 1
        instruction.then_inc(self.sem, 1)
        self.engine.wait_ge(self.sem, self.count)


class Weights:

    def __init__(self, region, fields):
        self.region, self.fields = region, fields

    def __call__(self, name, rows=P):
        at, width = self.fields[name]
        return self.region[0:rows, at:at + width]

    def chunks(self, name, n):
        return self(name).rearrange("p (k n) -> p k n", k=n)


def perceiver_kernel(nc, dram, packs, out):
    with ExitStack() as stack:
        made_so_far = {}

        def sb(name, shape, dt=F32, where=stack):
            made_so_far[name] = made_so_far.get(name, 0) + 1
            return where.enter_context(nc.sbuf_tensor(f"{name}_{made_so_far[name]}", shape, dt))

        x = sb("x", [P, NT, D])
        normed = sb("normed", [P, NT * D + KC * N])
        xn = normed[:, 0:NT * D].rearrange("p (t d) -> p t d", t=NT)
        xT = normed[:, NT * D:].rearrange("p (k n) -> p k n", k=KC)
        ident = sb("ident", [P, P])
        ones = sb("ones", [P, P])
        iota = sb("iota", [P, P])
        stat = sb("stat", [P, NT, 6])
        mv = sb("mv", [P, NT, 2])
        std = sb("std", [P, NT])
        rstd = sb("rstd", [P, NT])
        zero = sb("zero", [P, 1])
        order = ["a1", "a1_mlp", "a2", "a2_mlp", "l0a", "l0f", "l1x", "l1a", "l1f", "l2x", "l2a", "l2f", "l3x", "l3a",
                 "l3f"]
        widths = [max(packs[n][1] for n in names) for names in
                  (order[0::2], order[1::2])]
        regions = [sb(f"weights{i}", [P, w]) for i, w in enumerate(widths)]
        ps = stack.enter_context(nc.psum_tensor("ps", [P, 8, BANK], F32))
        loaded = [stack.enter_context(nc.semaphore(f"weights_loaded{i}")) for i in range(2)]
        loads = [0, 0]

        def weights(name):
            return Weights(regions[order.index(name) % 2], packs[name][0])

        def load_weights(engine, name):
            i = order.index(name) % 2
            engine.dma_start(regions[i][:, 0:packs[name][1]], dram[name]).then_inc(loaded[i], 16)
            loads[i] += 1

        def weights_here(name):
            i = order.index(name) % 2
            k = order.index(name) + 1
            with nc.Block() as block:
                @block.sync
                def _(sp):
                    sp.wait_ge(loaded[i], 16 * loads[i])
                    if k < len(order):
                        load_weights(sp, order[k])

        with signals(nc, "x_landed", "filled", "made") as (x_landed, filled, made), nc.Block() as block:
            @block.sync
            def _(sp):
                sp.dma_start(x[:], dram["x"].rearrange("(t p) d -> p t d", p=P)).then_inc(x_landed, 16)
                load_weights(sp, "a1")
                sp.wait_ge(x_landed, 16)

            @block.gpsimd
            def _(pool):
                pool.memset(ident[:], 0.0).then_inc(filled, 1)
                pool.memset(ones[:], 1.0).then_inc(filled, 1)
                pool.memset(zero[:], 0.0).then_inc(filled, 1)
                pool.iota(iota[:], pattern=[[1, P]], base=0, channel_multiplier=0,
                          allow_small_or_imprecise_dtypes=True).then_inc(made, 1)
                pool.wait_ge(filled, 3)
                pool.affine_select(out=ident[:], in_=ident[:], compare_op=ALU.not_equal, fill=1.0, base=0,
                                   pattern=[[-1, P]], channel_multiplier=1).then_inc(made, 1)
                pool.wait_ge(made, 2)

        def normalise(src, z, turned=(), add=(), affine=None):
            with signals(nc, "chain", "var_ready", "std_ready", "z_ready", "turned_ready") as \
                    (chain, var_ready, std_ready, z_ready, turned_ready), nc.Block() as block:
                @block.vector
                def _(dve):
                    link = Chain(dve, chain)
                    for other in add:
                        link(dve.tensor_tensor(src[:], src[:], other[:], ALU.add))
                    for t in range(NT):
                        last = dve.bn_stats(stat[:, t, :], src[:, t, :])
                    link(last)
                    for t in range(NT):
                        last = dve.bn_aggr(mv[:, t, :], stat[:, t, :])
                    link(last)
                    link(dve.tensor_scalar(std[:], mv[:, :, 1], EPS, None, ALU.add))
                    dve.sem_inc(var_ready, 1)
                    dve.wait_ge(std_ready, 1)
                    link(dve.reciprocal(rstd[:], std[:]))
                    for t in range(NT):
                        last = dve.tensor_scalar(z[:, t, :], src[:, t, :], mv[:, t, 0:1], rstd[:, t:t + 1],
                                                 ALU.subtract, ALU.mult)
                        if affine is None:
                            last.then_inc(z_ready, 1)
                    if affine is not None:
                        link(last)
                        for t in range(NT):
                            last = dve.tensor_tensor(z[:, t, :], z[:, t, :], affine[0], ALU.mult)
                        link(last)
                        for t in range(NT):
                            dve.tensor_tensor(z[:, t, :], z[:, t, :], affine[1], ALU.add).then_inc(z_ready, 1)

                @block.scalar
                def _(act):
                    act.wait_ge(var_ready, 1)
                    nc.scalar.activation(std[:], std[:], ACT.Sqrt).then_inc(std_ready, 1)
                    act.wait_ge(std_ready, 1)
                    if turned:
                        act.wait_ge(turned_ready, NT)
                    for dst, scale, bias in turned:
                        for c in range(KC):
                            if scale is None:
                                nc.scalar.activation(dst[:, c, :], ps[:, c, :], ACT.Copy)
                            else:
                                nc.scalar.activation(dst[:, c, :], ps[:, c, :], ACT.Identity,
                                                     bias=bias[:, c:c + 1], scale=scale[:, c:c + 1])

                if turned:
                    @block.tensor
                    def _(pe):
                        for t in range(NT):
                            pe.wait_ge(z_ready, t + 1)
                            for c in range(KC):
                                last = pe.transpose(ps[:, c, t * P:(t + 1) * P], z[:, t, c * P:(c + 1) * P], ident[:])
                            last.then_inc(turned_ready, 1)

        def dense(products):
            def nth(n):
                return sum(p[3] == products[n][3] for p in products[:n + 1])

            with signals(nc, "product_ready", "taken_by_scalar", "taken_by_vector") as \
                    (product_ready, taken_by_scalar, taken_by_vector), nc.Block() as block:
                taken = {"act": taken_by_scalar, "dve": taken_by_vector}

                @block.tensor
                def _(pe):
                    for n, (terms, rows, cols, engine, take) in enumerate(products):
                        if n >= 8:
                            pe.wait_ge(taken[products[n - 8][3]], nth(n - 8))
                        bank = ps[0:rows, n % 8, 0:cols]
                        if terms[0] is None:
                            for i, block_in in enumerate(terms[1]):
                                last = pe.transpose(ps[0:rows, n % 8, i * P:(i + 1) * P], block_in, ident[:])
                        elif terms[0] == "rows":
                            for at, lhsT, rhs in terms[1]:
                                last = pe.matmul(ps[at:at + lhsT.shape[1], n % 8, 0:cols], lhsT, rhs,
                                                 start=True, stop=True)
                        else:
                            for i, (lhsT, rhs) in enumerate(terms):
                                last = pe.matmul(bank, lhsT, rhs, start=(i == 0), stop=(i == len(terms) - 1))
                        last.then_inc(product_ready, 1)

                @block.scalar
                def _(act):
                    for n, (terms, rows, cols, engine, take) in enumerate(products):
                        if engine == "act":
                            act.wait_ge(product_ready, n + 1)
                            take(nc.scalar, ps[0:rows, n % 8, 0:cols]).then_inc(taken_by_scalar, 1)

                @block.vector
                def _(dve):
                    for n, (terms, rows, cols, engine, take) in enumerate(products):
                        if engine == "dve":
                            dve.wait_ge(product_ready, n + 1)
                            take(nc.vector, ps[0:rows, n % 8, 0:cols]).then_inc(taken_by_vector, 1)

        def copy_to(dst):
            def take(engine, psum):
                if engine is nc.scalar:
                    return engine.activation(dst, psum, ACT.Copy)
                return engine.tensor_copy(dst, psum)
            return take

        def plus_column(dst, column):
            def take(engine, psum):
                if engine is nc.scalar:
                    return engine.activation(dst, psum, ACT.Identity, bias=column)
                return engine.tensor_scalar(dst, psum, column, None, ALU.add)
            return take

        def plus(dst, other):
            return lambda engine, psum: engine.tensor_tensor(dst, psum, other, ALU.add)

        def activated(dst, func, bias=0.0):
            return lambda engine, psum: engine.activation(dst, psum, func, bias=bias)

        def either(n):
            return "act" if n % 2 else "dve"

        def feature_rows(w, src, dst, column=None, chunks=None):
            k_chunks = w.shape[1]
            chunks = chunks or w.shape[2] // P
            return [([(w[:, k, m * P:(m + 1) * P], src[:, k, :]) for k in range(k_chunks)], P, N, either(m),
                     copy_to(dst[:, m, :]) if column is None else plus_column(dst[:, m, :], column[:, m:m + 1]))
                    for m in range(chunks)]

        def token_rows(src, w, take, row=None, width=D, engine="dve"):
            products = []
            for t in range(NT):
                terms = [(src[:, k, t * P:(t + 1) * P], w[:, k, :]) for k in range(w.shape[1])]
                if row is not None:
                    terms.append((ones[0:1, :], row))
                products.append((terms, P, width, engine if engine != "both" else either(t), take(t)))
            return products

        def self_attention(qT, kT, v, oT, scale, mask=None):
            names = ("chain", "cleared", "scores_ready", "shifted", "exp_ready", "probs_ready", "turned_ready",
                     "turned_kept", "out_ready", "out_kept")
            with ExitStack() as own, signals(nc, *names) as \
                    (chain, cleared, scores_ready, shifted, exp_ready, probs_ready, turned_ready,
                     turned_kept, out_ready, out_kept):
                less = sb("less", [P, 2, H, S], where=own)
                probs = sb("probs", [P, 2, H, P], where=own)
                probsT = sb("probsT", [P, 2, H, P], where=own)
                top = sb("top", [P, H], where=own)
                total = sb("total", [P, H], where=own)
                rtotal = sb("rtotal", [P, H], where=own)
                with nc.Block() as block:
                    @block.tensor
                    def _(pe):
                        def scores(t):
                            if t:
                                pe.wait_ge(shifted, t)
                            for i in range(4):
                                for j in range(4):
                                    for half in range(2):
                                        rows = slice(HP * j, HP * j + HP)
                                        at = (2 * t + half) * S
                                        last = pe.matmul(ps[half * S:half * S + S, j, i * S:(i + 1) * S],
                                                         qT[rows, i, at:at + S], kT[rows, i, at:at + S],
                                                         start=True, stop=True)
                            last.then_inc(scores_ready, 1)

                        scores(0)
                        for t in range(NT):
                            if t + 1 < NT:
                                scores(t + 1)
                            pe.wait_ge(probs_ready, 2 * (t + 1))
                            for g in range(4):
                                n = 4 * t + g
                                if n >= 2:
                                    pe.wait_ge(turned_kept, n - 1)
                                for i in range(4):
                                    last = pe.transpose(ps[:, 4 + n % 2, i * P:(i + 1) * P],
                                                        probs[:, t % 2, 4 * g + i, :], ident[:])
                                last.then_inc(turned_ready, 1)
                            if t >= 2:
                                pe.wait_ge(out_kept, t - 1)
                            for j in range(4):
                                pe.wait_ge(turned_kept, 4 * t + j + 1)
                                for i in range(4):
                                    last = pe.matmul(ps[HP * j:HP * j + HP, 6 + t % 2, i * P:(i + 1) * P],
                                                     v[:, t, (4 * i + j) * HP:(4 * i + j + 1) * HP],
                                                     probsT[:, t % 2, 4 * j + i, :], start=True, stop=True)
                            last.then_inc(out_ready, 1)

                    @block.gpsimd
                    def _(pool):
                        pool.memset(probs[:, 0], 0.0).then_inc(cleared, 1)
                        pool.memset(probs[:, 1], 0.0).then_inc(cleared, 1)

                    @block.scalar
                    def _(act):
                        def exponents(t):
                            act.wait_ge(shifted, t + 1)
                            nc.scalar.activation(less[:, t % 2], less[:, t % 2], ACT.Exp, scale=scale)\
                                .then_inc(exp_ready, 1)

                        exponents(0)
                        for t in range(NT):
                            if t >= 2:
                                act.wait_ge(out_ready, t - 1)
                            for g in range(4):
                                n = 4 * t + g
                                act.wait_ge(turned_ready, n + 1)
                                nc.scalar.activation(probsT[:, t % 2, 4 * g:4 * g + 4, :],
                                                     ps[:, 4 + n % 2, :].rearrange("p (i q) -> p i q", q=P),
                                                     ACT.Copy).then_inc(turned_kept, 1)
                            if t + 1 < NT:
                                exponents(t + 1)

                    @block.vector
                    def _(dve):
                        link = Chain(dve, chain)

                        def shift(t):
                            dve.wait_ge(scores_ready, t + 1)
                            if t >= 2:
                                dve.wait_ge(probs_ready, 2 * (t - 1))
                            s = ps[:, 0:4, 0:4 * S].rearrange("p j (i q) -> p j i q", q=S)
                            link(dve.tensor_reduce(top[:], s, AX.X, ALU.max))
                            dve.tensor_tensor(less[:, t % 2].rearrange("p (j i) q -> p j i q", j=4), s,
                                              top[:].rearrange("p (j i) -> p j i", j=4).unsqueeze(3)
                                              .broadcast_to([P, 4, 4, S]), ALU.subtract).then_inc(shifted, 1)
                            dve.wait_ge(shifted, t + 1)

                        def normal(t):
                            dve.wait_ge(exp_ready, t + 1)
                            link(dve.tensor_reduce(total[:], less[:, t % 2], AX.X, ALU.add))
                            link(dve.reciprocal(rtotal[:], total[:]))
                            if mask is not None:
                                link(dve.tensor_tensor(less[:, t % 2], less[:, t % 2],
                                                       mask.unsqueeze(1).broadcast_to([P, H, S]), ALU.mult))
                            dve.wait_ge(cleared, min(t + 1, 2))
                            if t >= 2:
                                dve.wait_ge(turned_ready, 4 * (t - 1))
                            for half in range(2):
                                rows = slice(half * S, half * S + S)
                                dve.tensor_tensor(probs[rows, t % 2, :, half * S:half * S + S], less[rows, t % 2],
                                                  rtotal[rows].unsqueeze(2).broadcast_to([S, H, S]),
                                                  ALU.mult).then_inc(probs_ready, 1)

                        shift(0)
                        normal(0)
                        for t in range(NT):
                            if t + 1 < NT:
                                shift(t + 1)
                                normal(t + 1)
                            dve.wait_ge(out_ready, t + 1)
                            dve.tensor_copy(oT[:, :, t * P:(t + 1) * P],
                                            ps[:, 6 + t % 2, :].rearrange("p (i q) -> p i q", q=P)).then_inc(out_kept, 1)

        def three_passes(pe, out, high, low, moving_high, moving_low, start, stop):
            pe.matmul(out, high, moving_high, start=start, stop=False)
            pe.matmul(out, high, moving_low, start=False, stop=False)
            return pe.matmul(out, low, moving_high, start=False, stop=stop)

        PARTS = [range(0, 4), range(4, 8), range(8, 12), range(12, KCH)]

        def keys_in(chunk):
            return P if chunk < KCH - 1 else KLAST

        def one_head_attention(q, term):
            held = 4
            names = tuple(f"landed{i}" for i in range(held)) + (
                "chain", "scores_half", "scores_ready", "top_ready", "probs_ready", "turned_ready", "turned_act",
                "turned_dve", "value_ready", "value_kept", "value_turned", "value_stored")
            with ExitStack() as own, signals(nc, *names) as sems:
                landed = sems[0:held]
                (chain, scores_half, scores_ready, top_ready, probs_ready, turned_ready, turned_act, turned_dve,
                 value_ready, value_kept, value_turned, value_stored) = sems[held:]
                cT = sb("cT", [P, held, KEYS], where=own)
                c = sb("c", [P, held, KCH, CD], where=own)
                probs = sb("probs", [S, 2, KEYS], where=own)
                probsT = sb("probsT", [P, KCH, S], where=own)
                value = sb("value", [S, 2, CD], where=own)
                top = sb("top", [S, 2, 4], where=own)
                ntop = sb("ntop", [S, 2], where=own)
                total = sb("total", [S, 2], where=own)
                rtotal = sb("rtotal", [S, 2], where=own)
                flat = ps[0:S, 0:4, :].rearrange("p n k -> p (n k)")

                with nc.Block() as block:
                    @block.sync
                    def _(sp):
                        for b in range(B):
                            i = b % held
                            if b >= held:
                                sp.wait_ge(value_ready, b - held + 1)
                            sp.dma_start(cT[:, i, :], dram["ctxT"][b][:, 0:KEYS]).then_inc(landed[i], 16)
                            sp.dma_start(c[:, i], dram["ctx"][b].rearrange("p (k d) -> p k d", d=CD))\
                                .then_inc(landed[i], 16)

                    @block.tensor
                    def _(pe):
                        def scores(b):
                            pe.wait_ge(landed[b % held], 32 * (b // held + 1))
                            if b:
                                pe.wait_ge(probs_ready, b)
                            for n in range(4):
                                w = min(BANK, KEYS - n * BANK)
                                last = pe.matmul(ps[0:S, n, 0:w], q[:, b * S:(b + 1) * S],
                                                 cT[:, b % held, n * BANK:n * BANK + w], start=True, stop=True)
                                if n == 1:
                                    last.then_inc(scores_half, 1)
                            last.then_inc(scores_ready, 1)

                        def turn_part(b, g):
                            n = 2 * b + g // 2
                            if n:
                                pe.wait_ge(turned_act if g % 2 else turned_dve, n)
                            for k, chunk in enumerate(PARTS[g]):
                                w = keys_in(chunk)
                                last = pe.transpose(ps[0:w, 4 + g % 2, k * S:(k + 1) * S],
                                                    probs[:, b % 2, chunk * P:chunk * P + w], ident[0:S, 0:S])
                            last.then_inc(turned_ready, 1)

                        def turn_value(b):
                            pe.wait_ge(value_kept, b + 1)
                            if b:
                                pe.wait_ge(value_stored, b)
                            pe.transpose(ps[:, 7, 0:S], value[:, b % 2, :], ident[0:S, 0:S]).then_inc(value_turned, 1)

                        scores(0)
                        for b in range(B):
                            pe.wait_ge(probs_ready, b + 1)
                            turn_part(b, 0)
                            turn_part(b, 1)
                            if b + 1 < B:
                                scores(b + 1)
                            turn_part(b, 2)
                            turn_part(b, 3)
                            if b:
                                turn_value(b - 1)
                            for k in range(KCH):
                                if k % 4 == 0:
                                    pe.wait_ge(turned_act if (k // 4) % 2 else turned_dve, 2 * b + k // 8 + 1)
                                w = keys_in(k)
                                last = pe.matmul(ps[0:S, 6, (b % 2) * CD:(b % 2) * CD + CD], probsT[0:w, k, :],
                                                 c[0:w, b % held, k, :], start=(k == 0), stop=(k == KCH - 1))
                            last.then_inc(value_ready, 1)
                        turn_value(B - 1)

                    @block.scalar
                    def _(act):
                        def exponents(b):
                            act.wait_ge(top_ready, b + 1)
                            if b >= 2:
                                act.wait_ge(turned_ready, 4 * (b - 1))
                            nc.scalar.activation(probs[:, b % 2, :], flat[:, 0:KEYS], ACT.Exp, bias=ntop[:, b % 2:b % 2 + 1],
                                                 accum_out=total[:, b % 2:b % 2 + 1]).then_inc(probs_ready, 1)

                        def copy_turned(b, g):
                            act.wait_ge(turned_ready, 4 * b + g + 1)
                            w, n = keys_in(PARTS[g][-1]), len(PARTS[g])
                            nc.scalar.activation(probsT[0:w, PARTS[g][0]:PARTS[g][0] + n, :],
                                                 ps[0:w, 5, 0:n * S].rearrange("p (k r) -> p k r", r=S),
                                                 ACT.Copy).then_inc(turned_act, 1)

                        def store(b):
                            act.wait_ge(value_turned, b + 1)
                            nc.scalar.activation(q[:, b * S:(b + 1) * S], ps[:, 7, 0:S], ACT.Copy)\
                                .then_inc(value_stored, 1)

                        exponents(0)
                        for b in range(B):
                            if b:
                                act.wait_ge(value_ready, b)
                            copy_turned(b, 1)
                            copy_turned(b, 3)
                            if b:
                                store(b - 1)
                            if b + 1 < B:
                                exponents(b + 1)
                        store(B - 1)

                    @block.vector
                    def _(dve):
                        link = Chain(dve, chain)

                        def maximum(b):
                            i = b % 2
                            dve.wait_ge(scores_half, b + 1)
                            dve.tensor_reduce(top[:, i, 0:1], flat[:, 0:2 * BANK], AX.X, ALU.max).then_inc(chain, 1)
                            link.count += 1
                            dve.wait_ge(scores_ready, b + 1)
                            link(dve.tensor_reduce(top[:, i, 1:2], flat[:, 2 * BANK:KEYS], AX.X, ALU.max))
                            link(dve.tensor_scalar(top[:, i, 2:3], top[:, i, 0:1], top[:, i, 1:2], None, ALU.max))
                            link(dve.tensor_tensor(top[:, i, 3:4], top[:, i, 2:3], term[:, b:b + 1], ALU.add))
                            dve.tensor_tensor(ntop[:, i:i + 1], term[:, b:b + 1], top[:, i, 3:4], ALU.subtract)\
                                .then_inc(top_ready, 1)

                        def copy_turned(b, g):
                            dve.wait_ge(turned_ready, 4 * b + g + 1)
                            dve.tensor_copy(probsT[:, PARTS[g][0]:PARTS[g][0] + 4, :],
                                            ps[:, 4, 0:4 * S].rearrange("p (k r) -> p k r", r=S)).then_inc(turned_dve, 1)

                        maximum(0)
                        for b in range(B):
                            if b:
                                dve.wait_ge(value_ready, b)
                            copy_turned(b, 0)
                            if b + 1 < B:
                                maximum(b + 1)
                            copy_turned(b, 2)
                            dve.wait_ge(probs_ready, b + 1)
                            link(dve.reciprocal(rtotal[:, b % 2:b % 2 + 1], total[:, b % 2:b % 2 + 1]))
                            dve.wait_ge(value_ready, b + 1)
                            if b >= 2:
                                dve.wait_ge(value_turned, b - 1)
                            dve.tensor_scalar(value[:, b % 2, :], ps[0:S, 6, (b % 2) * CD:(b % 2) * CD + CD],
                                              rtotal[:, b % 2:b % 2 + 1], None, ALU.mult).then_inc(value_kept, 1)

        def cross_attention(q, scale, keysT, keys, affine=None):
            PER, UNITS = H // 2, H
            STEPS, COUPLES = B // 2, H // 2
            names = ("top_step", "total_step", "raw_landed", "high_ready", "low_ready", "high_staged", "high_seen", "staged", "scores_half",
                     "scores_ready", "top_ready", "probs_half", "probs_ready", "turned_ready", "high_kept", "low_kept", "diag_ready",
                     "spread_ready", "spread_kept", "value_part", "value_ready", "value_kept", "value_stored")
            with ExitStack() as own, signals(nc, *names) as \
                    (top_step, total_step, raw_landed, high_ready, low_ready, high_staged, high_seen, staged, scores_half, scores_ready,
                     top_ready, probs_half, probs_ready, turned_ready, high_kept, low_kept, diag_ready, spread_ready,
                     spread_kept, value_part, value_ready, value_kept, value_stored):
                raw = sb("raw", [P, KPAD], where=own)
                cTh, cTl = (sb(n, [P, 2, KEVEN], F32R, own) for n in ("cTh", "cTl"))
                ch, cl = (sb(n, [P, 2, KCH, CD], F32R, own) for n in ("ch", "cl"))
                qh, ql = (sb(n, [P, 2, 2 * P], F32R, own) for n in ("qh", "ql"))
                probs = normed[:, 0:KEYS], sb("probs", [P, KEYS], where=own)[:]
                pTh, pTl = (sb(n, [P, KCH, 2, P], F32R, own) for n in ("pTh", "pTl"))
                top = sb("top", [P, 2, 2], where=own)
                ntop = sb("ntop", [P, 2], where=own)
                total = sb("total", [P, 2, 2], where=own)
                rtotal = sb("rtotal", [P, 2], where=own)
                diag = sb("diag", [P, 2, 2 * P], where=own)
                share = sb("share", [P, 2 * P], where=own)
                value = sb("value", [P, 2 * P], where=own)
                flat = ps[:, 0:4, :].rearrange("p n k -> p (n k)")
                turned_bank = (4, 5, 7, 4)

                def loop_steps(engine, body):
                    body(0, True)
                    with engine.Fori(1, STEPS) as step:
                        body(step, False)

                with nc.Block() as block:
                    @block.sync
                    def _(sp):
                        def fetch_keysT(b):
                            sp.dma_start(raw[:, 0:KEVEN], keysT[bass.ds(b, 1)].rearrange("b p k -> (b p) k"))\
                                .then_inc(raw_landed, 16)

                        def fetch_keys(b):
                            sp.dma_start(raw[:], keys[bass.ds(b, 1)].rearrange("b p k -> (b p) k"))\
                                .then_inc(raw_landed, 16)

                        fetch_keysT(0)
                        with sp.Fori(0, B - 1) as b:
                            sp.wait_ge(low_ready, 2 * b + 1)
                            fetch_keys(b)
                            sp.wait_ge(low_ready, 2 * b + 2)
                            fetch_keysT(b + 1)
                        sp.wait_ge(low_ready, 2 * B - 1)
                        fetch_keys(B - 1)

                    @block.gpsimd
                    def _(pool):
                        def low(n, dst, high):
                            pool.wait_ge(high_ready, n + 1)
                            pool.tensor_tensor(dst, raw[:, 0:dst.shape[1]], high.bitcast(F32), ALU.subtract)\
                                .then_inc(low_ready, 1)

                        def stage(c, batch, k, early):
                            if not early:
                                pool.wait_ge(scores_ready, 2 * (c - 1))
                            pool.tensor_copy(qh[:, k % 2].rearrange("p (h s) -> p h s", s=S),
                                             q[:, 4 * (k % 4):4 * (k % 4) + 4, bass.ds(batch * S, S)])\
                                .then_inc(high_staged, 1)
                            pool.wait_ge(high_staged, c + 1)
                            pool.sem_inc(high_seen, 1)
                            pool.tensor_tensor(ql[:, k % 2].rearrange("p (h s) -> p h s", s=S),
                                               q[:, 4 * (k % 4):4 * (k % 4) + 4, bass.ds(batch * S, S)],
                                               qh[:, k % 2].bitcast(F32).rearrange("p (h s) -> p h s", s=S),
                                               ALU.subtract).then_inc(staged, 1)

                        def flat_keys(t, i):
                            return t[:, i].rearrange("p k d -> p (k d)")

                        def body(step, first):
                            for k in range(COUPLES):
                                i, at = k // 4, k % 4
                                n = 2 * (2 * step + i)
                                stage(step * COUPLES + k, 2 * step + i, k, first and k < 2)
                                if at == 1:
                                    low(n + 2, cTl[:, 1 - i], cTh[:, 1 - i])
                                if at == 3:
                                    low(n + 3, flat_keys(cl, 1 - i), flat_keys(ch, 1 - i))

                        def last_body(step):
                            for k in range(COUPLES):
                                i, at = k // 4, k % 4
                                stage(step * COUPLES + k, 2 * step + i, k, False)
                                if i == 0 and at == 1:
                                    low(2 * B - 2, cTl[:, 1], cTh[:, 1])
                                if i == 0 and at == 3:
                                    low(2 * B - 1, flat_keys(cl, 1), flat_keys(ch, 1))

                        body(0, True)
                        with pool.Fori(1, STEPS - 1) as step:
                            body(step, False)
                        last_body(STEPS - 1)

                    @block.tensor
                    def _(pe):
                        def scores(u, step, first):
                            i = u // PER
                            if u % PER == 0:
                                pe.wait_ge(low_ready, 2 * (2 * step + i) + 1)
                            if u % 2 == 0:
                                pe.wait_ge(staged, step * COUPLES + u // 2 + 1)
                            k, at = (u // 2) % 2, (u % 2) * P
                            for n in range(4):
                                if n in (0, 2) and not (first and u == 0):
                                    pe.wait_ge(probs_ready if n else probs_half, step * UNITS + u)
                                cols = slice(n * BANK, min(KEVEN, (n + 1) * BANK))
                                last = three_passes(pe, ps[:, n, 0:cols.stop - cols.start], qh[:, k, at:at + P],
                                                    ql[:, k, at:at + P], cTh[:, i, cols], cTl[:, i, cols], True, True)
                                if n == 1:
                                    last.then_inc(scores_half, 1)
                            last.then_inc(scores_ready, 1)

                        def turn(g, v, slot, early=False):
                            if g == 0 and not early:
                                pe.wait_ge(low_kept, 4 * v)
                            if g == 3:
                                pe.wait_ge(low_kept, 4 * v + 1)
                            for k, chunk in enumerate(PARTS[g]):
                                w = keys_in(chunk)
                                last = pe.transpose(ps[0:w, turned_bank[g], k * P:(k + 1) * P],
                                                    probs[slot][:, chunk * P:chunk * P + w], ident[:])
                            last.then_inc(turned_ready, 1)

                        def spread_shares(c, k):
                            pe.wait_ge(diag_ready, 2 * c + 2)
                            pe.matmul(ps[:, 6, 2 * P:4 * P], ones[:], diag[:, k],
                                      start=True, stop=True).then_inc(spread_ready, 1)

                        def values(g, c, i):
                            pe.wait_ge(low_kept, 4 * (2 * c + 1) + g + 1)
                            for k in PARTS[g]:
                                w = keys_in(k)
                                moving = [t[0:w, k].rearrange("p u r -> p (u r)") for t in (pTh, pTl)]
                                last = three_passes(pe, ps[:, 6, 0:2 * P], ch[0:w, i, k, :], cl[0:w, i, k, :],
                                                    moving[0], moving[1], k == 0, k == KCH - 1)
                            last.then_inc(value_ready if g == 3 else value_part, 1)

                        def second_turned(v, c, i, first=False, new_batch=None):
                            turn(0, v, 1)
                            turn(1, v, 1)
                            turn(2, v, 1)
                            if not first:
                                pe.wait_ge(value_kept, c)
                            if new_batch is not None:
                                pe.wait_ge(low_ready, 2 * new_batch + 2)
                            values(0, c, i)
                            turn(3, v, 1)

                        def body(step, first):
                            for u in range(0, UNITS, 2):
                                v = step * UNITS + u
                                c = step * COUPLES + u // 2
                                i = ((u - 2) % UNITS) // PER
                                new_batch = None
                                if (u - 2) % PER == 0:
                                    new_batch = 2 * step + (u - 2) // PER
                                before = not (first and u == 0)
                                scores(u, step, first)
                                if before:
                                    second_turned(v - 1, c - 1, i, first and u == 2, new_batch)
                                scores(u + 1, step, first)
                                turn(0, v, 0, not before)
                                if before:
                                    values(1, c - 1, i)
                                turn(1, v, 0)
                                if before:
                                    values(2, c - 1, i)
                                turn(2, v, 0)
                                if before:
                                    values(3, c - 1, i)
                                    spread_shares(c - 1, (u // 2 - 1) % 2)
                                turn(3, v, 0)

                        loop_steps(pe, body)
                        units = STEPS * UNITS
                        pe.wait_ge(probs_ready, units)
                        second_turned(units - 1, units // 2 - 1, 1)
                        for g in range(1, 4):
                            values(g, units // 2 - 1, 1)
                        spread_shares(units // 2 - 1, 1)

                    @block.scalar
                    def _(act):
                        def high(n, dst):
                            act.wait_ge(raw_landed, 16 * (n + 1))
                            nc.scalar.activation(dst, raw[:, 0:dst.shape[1]], ACT.Copy).then_inc(high_ready, 1)

                        def exponents(v, slot, early, half):
                            if half == 0:
                                act.wait_ge(top_ready, v + 1)
                                if not early:
                                    act.wait_ge(turned_ready, 4 * (v - 1))
                                    act.wait_ge(diag_ready, v - 1)
                            cols = slice(half * 2 * BANK, (2 * BANK, KEYS)[half])
                            nc.scalar.activation(probs[slot][:, cols], flat[:, cols], ACT.Exp,
                                                 bias=ntop[:, slot:slot + 1], scale=scale,
                                                 accum_out=total[:, slot, half:half + 1])\
                                .then_inc(probs_ready if half else probs_half, 1)

                        def keep(g, v, slot, c=None):
                            act.wait_ge(turned_ready, 4 * v + g + 1)
                            if c is not None:
                                act.wait_ge(value_ready if g == 3 else value_part, c if g == 3 else 3 * (c - 1) + g + 1)
                            w, n = keys_in(PARTS[g][-1]), len(PARTS[g])
                            nc.scalar.activation(
                                pTh[0:w, PARTS[g][0]:PARTS[g][0] + n, slot, :],
                                ps[0:w, turned_bank[g], 0:n * P].rearrange("p (k r) -> p k r", r=P),
                                ACT.Copy).then_inc(high_kept, 1)

                        def keep_shares(c, early):
                            act.wait_ge(spread_ready, c + 1)
                            if not early:
                                act.wait_ge(value_kept, c)
                            nc.scalar.activation(share[:], ps[:, 6, 2 * P:4 * P], ACT.Copy).then_inc(spread_kept, 1)

                        def store(c, batch, k):
                            act.wait_ge(value_kept, c + 1)
                            dst = q[:, 4 * k:4 * k + 4, bass.ds(batch * S, S)]
                            src = value[:].rearrange("p (h s) -> p h s", s=S)
                            if affine is None:
                                nc.scalar.activation(dst, src, ACT.Copy).then_inc(value_stored, 1)
                            else:
                                nc.scalar.activation(dst, src, ACT.Identity, bias=affine[1],
                                                     scale=affine[0]).then_inc(value_stored, 1)

                        def body(step, first, final=False):
                            for u in range(0, UNITS, 2):
                                v = step * UNITS + u
                                c = step * COUPLES + u // 2
                                n = 2 * (2 * step + u // PER)
                                other = 1 - u // PER
                                before = not (first and u == 0)
                                if before:
                                    keep(0, v - 1, 1)
                                exponents(v, 0, first and u < 2, 0)
                                if before:
                                    keep(1, v - 1, 1)
                                exponents(v, 0, first and u < 2, 1)
                                if before:
                                    for g in range(2, 4):
                                        keep(g, v - 1, 1)
                                    if not (first and u == 2):
                                        store(c - 2, 2 * step + (u - 4) // PER, ((u - 4) // 2) % 4)
                                keep(0, v, 0, c if before else None)
                                exponents(v + 1, 1, first and u < 2, 0)
                                keep(1, v, 0, c if before else None)
                                exponents(v + 1, 1, first and u < 2, 1)
                                for g in range(2, 4):
                                    if g == 3 and before:
                                        keep_shares(c - 1, first and u == 2)
                                    keep(g, v, 0, c if before else None)
                                if final and u >= PER:
                                    continue
                                if u % PER == 0:
                                    if not (first and u == 0):
                                        act.wait_ge(scores_ready, v)
                                    high(n + 2, cTh[:, other])
                                if u % PER == 4:
                                    high(n + 3, ch[:, other].rearrange("p k d -> p (k d)"))

                        high(0, cTh[:, 0])
                        high(1, ch[:, 0].rearrange("p k d -> p (k d)"))
                        body(0, True)
                        with act.Fori(1, STEPS - 1) as step:
                            body(step, False)
                        body(STEPS - 1, False, True)
                        units = STEPS * UNITS
                        for g in range(4):
                            keep(g, units - 1, 1)
                        store(units // 2 - 2, B - 1, 2)
                        keep_shares(units // 2 - 1, False)
                        store(units // 2 - 1, B - 1, 3)

                    @block.vector
                    def _(dve):
                        def maximum(v, slot):
                            dve.wait_ge(scores_half, v + 1)
                            dve.tensor_reduce(top[:, slot, 0:1], flat[:, 0:2 * BANK], AX.X, ALU.max).then_inc(top_step, 1)
                            dve.wait_ge(scores_ready, v + 1)
                            dve.tensor_reduce(top[:, slot, 1:2], flat[:, 2 * BANK:KEYS], AX.X, ALU.max)\
                                .then_inc(top_step, 1)
                            dve.wait_ge(top_step, 2 * v + 2)
                            dve.tensor_scalar(ntop[:, slot:slot + 1], top[:, slot, 0:1], top[:, slot, 1:2], -scale,
                                              ALU.max, ALU.mult).then_inc(top_ready, 1)

                        def keep(v, slot, k):
                            r = rtotal[:, slot:slot + 1]
                            for g in range(4):
                                dve.wait_ge(high_kept, 4 * v + g + 1)
                                w, n = keys_in(PARTS[g][-1]), len(PARTS[g])
                                at = slice(PARTS[g][0], PARTS[g][0] + n)
                                dve.tensor_tensor(
                                    pTl[0:w, at, slot, :],
                                    ps[0:w, turned_bank[g], 0:n * P].rearrange("p (k r) -> p k r", r=P),
                                    pTh[0:w, at, slot, :].bitcast(F32), ALU.subtract).then_inc(low_kept, 1)
                                if g == 0:
                                    dve.wait_ge(probs_ready, v + 1)
                                    dve.tensor_tensor(r, total[:, slot, 0:1], total[:, slot, 1:2], ALU.add)\
                                        .then_inc(total_step, 1)
                                if g == 1:
                                    dve.wait_ge(total_step, 2 * v + 1)
                                    dve.reciprocal(r, r).then_inc(total_step, 1)
                                if g == 2:
                                    dve.wait_ge(total_step, 2 * v + 2)
                                    dve.tensor_scalar(diag[:, k, slot * P:(slot + 1) * P], ident[:], r, None, ALU.mult)\
                                        .then_inc(diag_ready, 1)

                        def scale_values(c, early):
                            dve.wait_ge(value_ready, c + 1)
                            dve.wait_ge(spread_kept, c + 1)
                            if not early:
                                dve.wait_ge(value_stored, c)
                            dve.tensor_tensor(value[:], ps[:, 6, 0:2 * P], share[:], ALU.mult).then_inc(value_kept, 1)

                        def low_of_first(n, dst, high):
                            dve.wait_ge(high_ready, n + 1)
                            dve.tensor_tensor(dst, raw[:, 0:dst.shape[1]], high.bitcast(F32), ALU.subtract)\
                                .then_inc(low_ready, 1)

                        def body(step, first):
                            for u in range(0, UNITS, 2):
                                v = step * UNITS + u
                                c = step * COUPLES + u // 2
                                before = not (first and u == 0)
                                if before and not (first and u == 2):
                                    scale_values(c - 2, first and u == 4)
                                maximum(v, 0)
                                if before:
                                    keep(v - 1, 1, (u // 2 - 1) % 2)
                                maximum(v + 1, 1)
                                if not before:
                                    low_of_first(1, cl[:, 0].rearrange("p k d -> p (k d)"),
                                                 ch[:, 0].rearrange("p k d -> p (k d)"))
                                keep(v, 0, (u // 2) % 2)

                        low_of_first(0, cTl[:, 0], cTh[:, 0])
                        loop_steps(dve, body)
                        units = STEPS * UNITS
                        scale_values(units // 2 - 2, False)
                        keep(units - 1, 1, 1)
                        scale_values(units // 2 - 1, False)

        def experts(guide, down, count, hidden, combine, bias=False):
            chunks = -(-hidden // P)
            gw, dw = guide.shape[2], down.shape[2]
            steps = (count - 1) // 2
            names = ("guide_landed0", "guide_landed1", "down_landed0", "down_landed1", "x_high", "x_low", "guide_high",
                     "guide_low", "down_high", "down_low", "raw_ready", "silu_ready", "gated_ready", "hidden_high",
                     "hidden_ready", "down_ready", "added")
            with ExitStack() as own, signals(nc, *names) as \
                    (guide_landed0, guide_landed1, down_landed0, down_landed1, x_high, x_low, guide_high, guide_low,
                     down_high, down_low, raw_ready, silu_ready, gated_ready, hidden_high, hidden_ready,
                     down_ready, added):
                guide_landed, down_landed = (guide_landed0, guide_landed1), (down_landed0, down_landed1)
                wg = sb("wg", [P, 2, gw], where=own)
                wd = sb("wd", [P, 2, dw], where=own)
                silu = sb("silu", [P, 2, N], where=own)
                gated = sb("gated", [P, 2, N], where=own)
                xh, xl = (sb(n, [P, KC, N], F32R, own) for n in ("xh", "xl"))
                wgh, wgl = (sb(n, [P, 2, 2 * KC * hidden], F32R, own) for n in ("wgh", "wgl"))
                wdh, wdl = (sb(n, [P, 2, chunks * D], F32R, own) for n in ("wdh", "wdl"))
                hidh, hidl = (sb(n, [P, 2, chunks, N], F32R, own) for n in ("hidh", "hidl"))
                columns_ = sb("columns", [P, 2, 2 * chunks], where=own)

                def has_next(e):
                    return not isinstance(e, int) or e + 1 < count

                def width(c):
                    return min(P, hidden - c * P)

                with nc.Block() as block:
                    @block.sync
                    def _(sp):
                        def fetch_guide(e, slot, first=False):
                            if not first:
                                sp.wait_ge(guide_low, e - 1)
                            sp.dma_start(wg[:, slot], guide[bass.ds(e, 1)].rearrange("e p n -> (e p) n"))\
                                .then_inc(guide_landed[slot], 16)

                        def fetch_down(e, slot, first=False):
                            if not first:
                                sp.wait_ge(down_ready, (e - 1) * NT)
                            sp.dma_start(wd[:, slot], down[bass.ds(e, 1)].rearrange("e p n -> (e p) n"))\
                                .then_inc(down_landed[slot], 16)

                        def two(i, first=False):
                            fetch_guide(2 * i, 0)
                            fetch_down(2 * i - 1, 1, first)
                            fetch_guide(2 * i + 1, 1)
                            fetch_down(2 * i, 0)
                        fetch_guide(0, 0, True)
                        fetch_guide(1, 1, True)
                        fetch_down(0, 0, True)
                        two(1, True)
                        with sp.Fori(2, count // 2) as i:
                            two(i)
                        if count % 2:
                            fetch_guide(count - 1, 0)
                            fetch_down(count - 2, 1)
                            fetch_down(count - 1, 0)
                        else:
                            fetch_down(count - 1, 1)

                    def in_order(first_product, second_product, loop):
                        first_product(0, 0, 0, True)
                        for at in (None, 1):
                            if at is None:
                                first_product(1, 1, 0, True)
                                second_product(0, 0, 0, True)
                                first_product(2, 0, 1, False)
                                second_product(1, 1, 0, False)
                            else:
                                def two(i):
                                    first_product(2 * i + 1, 1, i, False)
                                    second_product(2 * i, 0, i, False)
                                    first_product(2 * i + 2, 0, i + 1, False)
                                    second_product(2 * i + 1, 1, i, False)
                                with loop(1, steps - count % 2) as i:
                                    two(i)
                                if count % 2:
                                    two(steps - 1)
                        if count % 2 == 0:
                            first_product(count - 1, 1, steps, False)
                            second_product(count - 2, 0, steps, False)
                            second_product(count - 1, 1, steps, False)
                        else:
                            second_product(count - 1, 0, steps, False)

                    @block.tensor
                    def _(pe):
                        def first_product(e, slot, turn_, first):
                            pe.wait_ge(guide_low, e + 1)
                            for c in range(chunks):
                                pair = 2 * (((slot * chunks) + c) % 2)
                                w = width(c)
                                if not (first and slot * chunks + c < 2):
                                    pe.wait_ge(gated_ready, e * chunks + c - 1)
                                for half in range(2):
                                    for k in range(KC):
                                        at = (half * KC + k) * hidden + c * P
                                        last = three_passes(pe, ps[0:w, pair + half, :], wgh[:, slot, at:at + w],
                                                            wgl[:, slot, at:at + w], xh[:, k, :], xl[:, k, :],
                                                            k == 0, k == KC - 1)
                                last.then_inc(raw_ready, 1)

                        def second_product(e, slot, turn_, first):
                            pe.wait_ge(down_low, e + 1)
                            pe.wait_ge(hidden_ready, (e + 1) * chunks)
                            for t in range(NT):
                                if not first:
                                    pe.wait_ge(added, (e - 1) * NT + t + 1)
                                for c in range(chunks):
                                    w = width(c)
                                    rows, cols = slice(t * P, t * P + P), slice(c * D, c * D + D)
                                    last = three_passes(pe, ps[:, 4 + t, 0:D], hidh[0:w, slot, c, rows],
                                                        hidl[0:w, slot, c, rows], wdh[0:w, slot, cols],
                                                        wdl[0:w, slot, cols], c == 0, not bias and c == chunks - 1)
                                if bias:
                                    last = pe.matmul(ps[:, 4 + t, 0:D], ones[0:1, :],
                                                     wd[0:1, slot, chunks * D:(chunks + 1) * D],
                                                     start=False, stop=True)
                                last.then_inc(down_ready, 1)
                        pe.wait_ge(x_low, 1)
                        in_order(first_product, second_product, pe.Fori)

                    @block.scalar
                    def _(act):
                        def split_guide(e, slot, turn_):
                            act.wait_ge(guide_landed[slot], 16 * turn_ + 16)
                            if bias:
                                nc.scalar.activation(columns_[:, slot], wg[:, slot, 2 * KC * hidden:], ACT.Copy)
                            nc.scalar.activation(wgh[:, slot], wg[:, slot, 0:2 * KC * hidden], ACT.Copy)\
                                .then_inc(guide_high, 1)

                        def split_down(e, slot, turn_):
                            act.wait_ge(down_landed[slot], 16 * turn_ + 16)
                            nc.scalar.activation(wdh[:, slot], wd[:, slot, 0:chunks * D], ACT.Copy)\
                                .then_inc(down_high, 1)

                        def first_product(e, slot, turn_, first):
                            if has_next(e):
                                if not (first and slot == 0):
                                    act.wait_ge(gated_ready, e * chunks)
                                split_guide(e + 1, 1 - slot, turn_ + slot)

                            def high(c):
                                act.wait_ge(gated_ready, e * chunks + c + 1)
                                if not first:
                                    act.wait_ge(down_ready, (e - 1) * NT)
                                w = width(c)
                                nc.scalar.activation(hidh[0:w, slot, c, :], gated[0:w, (slot * chunks + c) % 2, :],
                                                     ACT.Copy).then_inc(hidden_high, 1)

                            for c in range(chunks):
                                n2 = (slot * chunks + c) % 2
                                w = width(c)
                                act.wait_ge(raw_ready, e * chunks + c + 1)
                                if not (first and slot * chunks + c < 2):
                                    act.wait_ge(gated_ready, e * chunks + c - 1)
                                nc.scalar.activation(silu[0:w, n2, :], ps[0:w, 2 * n2, :], ACT.Silu,
                                                     bias=columns_[0:w, slot, c:c + 1] if bias else 0.0)\
                                    .then_inc(silu_ready, 1)
                                if c:
                                    high(c - 1)
                            high(chunks - 1)

                        def second_product(e, slot, turn_, first):
                            if has_next(e):
                                if not (first and slot == 0):
                                    act.wait_ge(down_ready, e * NT)
                                split_down(e + 1, 1 - slot, turn_ + slot)

                        nc.scalar.activation(xh[:], xT, ACT.Copy).then_inc(x_high, 1)
                        split_guide(0, 0, 0)
                        split_down(0, 0, 0)
                        in_order(first_product, second_product, act.Fori)

                    @block.gpsimd
                    def _(pool):
                        def split_guide(e, slot):
                            pool.wait_ge(guide_high, e + 1)
                            pool.tensor_tensor(wgl[:, slot], wg[:, slot, 0:2 * KC * hidden], wgh[:, slot].bitcast(F32),
                                               ALU.subtract).then_inc(guide_low, 1)

                        def split_down(e, slot):
                            pool.wait_ge(down_high, e + 1)
                            pool.tensor_tensor(wdl[:, slot], wd[:, slot, 0:chunks * D], wdh[:, slot].bitcast(F32),
                                               ALU.subtract).then_inc(down_low, 1)

                        def first_product(e, slot, turn_, first):
                            if has_next(e):
                                split_guide(e + 1, 1 - slot)

                        def second_product(e, slot, turn_, first):
                            if has_next(e):
                                split_down(e + 1, 1 - slot)

                        split_guide(0, 0)
                        split_down(0, 0)
                        in_order(first_product, second_product, pool.Fori)

                    @block.vector
                    def _(dve):
                        def first_product(e, slot, turn_, first):
                            def low(c):
                                w = width(c)
                                dve.wait_ge(hidden_high, e * chunks + c + 1)
                                dve.tensor_tensor(hidl[0:w, slot, c, :], gated[0:w, (slot * chunks + c) % 2, :],
                                                  hidh[0:w, slot, c, :].bitcast(F32), ALU.subtract)\
                                    .then_inc(hidden_ready, 1)

                            for c in range(chunks):
                                n2 = (slot * chunks + c) % 2
                                w = width(c)
                                dve.wait_ge(silu_ready, e * chunks + c + 1)
                                if not (first and slot * chunks + c < 2):
                                    dve.wait_ge(hidden_ready, e * chunks + c - 1)
                                dve.scalar_tensor_tensor(
                                    out=gated[0:w, n2, :], in0=ps[0:w, 2 * n2 + 1, :],
                                    scalar=columns_[0:w, slot, chunks + c:chunks + c + 1] if bias else zero[0:w, :],
                                    in1=silu[0:w, n2, :], op0=ALU.add, op1=ALU.mult).then_inc(gated_ready, 1)
                                if c:
                                    low(c - 1)
                            low(chunks - 1)

                        def second_product(e, slot, turn_, first):
                            for t in range(NT):
                                dve.wait_ge(down_ready, e * NT + t + 1)
                                if not first:
                                    dve.wait_ge(added, (e - 1) * NT + t + 1)
                                dve.scalar_tensor_tensor(
                                    out=x[:, t, :], in0=ps[:, 4 + t, 0:D], scalar=combine[:, bass.ds(e * NT + t, 1)],
                                    in1=x[:, t, :], op0=ALU.mult, op1=ALU.add).then_inc(added, 1)
                        dve.wait_ge(x_high, 1)
                        dve.tensor_tensor(xl[:], xT, xh[:].bitcast(F32), ALU.subtract).then_inc(x_low, 1)
                        in_order(first_product, second_product, dve.Fori)

        def route(logits, count, combine, kind, picked=None):
            with ExitStack() as own, signals(nc, "chain", "exp_wanted", "exp_done") as (chain, exp_wanted, exp_done):
                small = sb("small", [P, NT, count], where=own)
                eight = sb("eight", [P, NT, 8], where=own)
                index = sb("index", [P, NT, 8], U32, where=own)
                where_ = sb("where", [P, NT, 8], where=own)
                first = sb("first", [P, NT, count], where=own)
                second = sb("second", [P, NT, count], where=own)
                row = sb("row", [P, 4, NT], where=own)
                pair = sb("pair", [P, 2, NT], where=own)

                def spread(v):
                    return v.unsqueeze(2).broadcast_to([P, NT, count])

                with nc.Block() as block:
                    @block.scalar
                    def _(act):
                        act.wait_ge(exp_wanted, 1)
                        if kind == "pair":
                            nc.scalar.activation(row[:, 0, :], row[:, 0, :], ACT.Exp).then_inc(exp_done, 1)
                        else:
                            nc.scalar.activation(small[:], small[:], ACT.Exp).then_inc(exp_done, 1)
                        act.wait_ge(exp_done, 1)

                    @block.vector
                    def _(dve):
                        link = Chain(dve, chain)
                        if kind == "pair":
                            scores = logits
                        else:
                            link(dve.tensor_reduce(row[:, 1, :], logits, AX.X, ALU.max))
                            link(dve.tensor_tensor(small[:], logits, spread(row[:, 1, :]), ALU.subtract))
                            dve.sem_inc(exp_wanted, 1)
                            dve.wait_ge(exp_done, 1)
                            link(dve.tensor_reduce(row[:, 2, :], small[:], AX.X, ALU.add))
                            link(dve.reciprocal(row[:, 3, :], row[:, 2, :]))
                            link(dve.tensor_tensor(small[:], small[:], spread(row[:, 3, :]), ALU.mult))
                            scores = small[:]
                        for t in range(NT):
                            last = dve.max(eight[:, t, :], scores[:, t, :])
                        link(last)
                        for t in range(NT):
                            last = dve.max_index(index[:, t, :], eight[:, t, :], scores[:, t, :])
                        link(last)
                        link(dve.tensor_copy(where_[:], index[:]))
                        places = iota[:, 0:count].unsqueeze(1).broadcast_to([P, NT, count])
                        dve.tensor_tensor(first[:], places, spread(where_[:, :, 0]), ALU.is_equal).then_inc(chain, 1)
                        chained = dve.tensor_tensor(second[:], places, spread(where_[:, :, 1]), ALU.is_equal)
                        link.count += 1
                        link(chained)
                        if kind == "pair":
                            link(dve.tensor_tensor(row[:, 0, :], eight[:, :, 1], eight[:, :, 0], ALU.subtract))
                            dve.sem_inc(exp_wanted, 1)
                            dve.wait_ge(exp_done, 1)
                            link(dve.tensor_scalar(row[:, 1, :], row[:, 0, :], 1.0, None, ALU.add))
                            link(dve.reciprocal(pair[:, 0, :], row[:, 1, :]))
                            link(dve.tensor_tensor(pair[:, 1, :], pair[:, 0, :], row[:, 0, :], ALU.mult))
                            weight = pair[:, 0, :], pair[:, 1, :]
                        elif kind == "share":
                            link(dve.tensor_tensor(row[:, 0, :], eight[:, :, 0], eight[:, :, 1], ALU.add))
                            link(dve.reciprocal(row[:, 1, :], row[:, 0, :]))
                            link(dve.tensor_tensor(pair[:, 0, :], eight[:, :, 0], row[:, 1, :], ALU.mult))
                            link(dve.tensor_tensor(pair[:, 1, :], eight[:, :, 1], row[:, 1, :], ALU.mult))
                            weight = pair[:, 0, :], pair[:, 1, :]
                        else:
                            weight = eight[:, :, 0], eight[:, :, 1]
                        if picked is not None:
                            link(dve.tensor_tensor(picked, first[:], second[:], ALU.add))
                        link(dve.tensor_tensor(first[:], first[:], spread(weight[0]), ALU.mult))
                        link(dve.tensor_tensor(second[:], second[:], spread(weight[1]), ALU.mult))
                        link(dve.tensor_tensor(combine[:, 0:count * NT].rearrange("p (e t) -> p t e", t=NT),
                                               first[:], second[:], ALU.add))

        def vector_steps(steps):
            with signals(nc, "chain") as (chain,), nc.Block() as block:
                @block.vector
                def _(dve):
                    link = Chain(dve, chain)
                    for step in steps:
                        link(step(dve))

        def rotary_rows(w, name, dst, tmp, bias):
            products = []
            tables = w("cos"), w("sin")
            n_tab = tables[0].shape[1] // S
            for part, (suffix, to) in enumerate((("", dst), ("_swapped", tmp))):
                mat = w.chunks(name + suffix, KC)
                for m in range(4):
                    tab = tables[part][:, (m % n_tab) * S:(m % n_tab + 1) * S].unsqueeze(1).broadcast_to([P, B, S])
                    col = w("b" + name[1:] + suffix)[:, m:m + 1] if bias else zero[:, 0:1]

                    def take(engine, psum, to=to, m=m, tab=tab, col=col):
                        return engine.scalar_tensor_tensor(
                            out=to[:, m, :].rearrange("p (b s) -> p b s", s=S),
                            in0=psum.rearrange("p (b s) -> p b s", s=S), scalar=col, in1=tab,
                            op0=ALU.add, op1=ALU.mult)
                    products.append(([(mat[:, k, m * P:(m + 1) * P], xT[:, k, :]) for k in range(KC)],
                                     P, N, "dve", take))
            return products

        def add_to_x(t):
            return plus(x[:, t, :], x[:, t, :])

        def two_attentions():
            with ExitStack() as own:
                inner = sb("inner", [P, NT, D], where=own)
                mid = sb("mid", [P, NT, D], where=own)

                def tail(name, w, oT):
                    with ExitStack() as tmp:
                        hT = sb("hT", [P, 4 * KC, N], where=tmp)
                        dense(token_rows(oT, w.chunks("li1_w", 4), lambda t: plus(mid[:, t, :], inner[:, t, :]),
                                         row=w("li1_b", 1)))
                        weights_here(name + "_mlp")
                        w = weights(name + "_mlp")
                        normalise(mid, xn, [(xT, w("ln3_g"), w("ln3_b"))])
                        li2 = w.chunks("li2_w", KC)
                        dense([([(li2[:, k, m * P:(m + 1) * P], xT[:, k, :]) for k in range(KC)], P, N, "act",
                                activated(hT[:, m, :], ACT.Gelu, w("li2_b")[:, m:m + 1])) for m in range(4 * KC)])
                        dense(token_rows(hT, w.chunks("li3_w", 4 * KC), lambda t: plus(mid[:, t, :], mid[:, t, :]),
                                         row=w("li3_b", 1)))

                weights_here("a1")
                w = weights("a1")
                with ExitStack() as tmp:
                    yT = sb("yT", [P, KC, N], where=tmp)
                    qT = sb("qT", [P, 4, N], where=tmp)
                    kT = sb("kT", [P, 4, N], where=tmp)
                    v = sb("v", [P, NT, H * HP], where=tmp)
                    oT = sb("oT", [P, 4, N], where=tmp)
                    normalise(x, xn)
                    normalise(xn, inner, affine=(w("ln1_g"), w("ln1_b")))
                    normalise(inner, xn, [(xT, w("lnx_g"), w("lnx_b")), (yT, w("lny_g"), w("lny_b"))])
                    dense(feature_rows(w.chunks("wq", KC), xT, qT) + feature_rows(w.chunks("wk", KC), yT, kT)
                          + token_rows(yT, w.chunks("wv", KC), lambda t: copy_to(v[:, t, :]), width=H * HP, engine="both"))
                    self_attention(qT, kT, v, oT, HP ** -0.5, mask=w("later"))
                    tail("a1", w, oT)

                weights_here("a2")
                w = weights("a2")
                normalise(mid, inner, add=[inner], affine=(w("ln2_g"), w("ln2_b")))
                normalise(inner, xn, [(xT, w("lnx_g"), w("lnx_b"))])
                context_norm(w("lny_g"), w("lny_b"))
                with ExitStack() as tmp:
                    q = sb("q", [P, H, N], where=tmp)
                    with ExitStack() as early:
                        qT = sb("qT", [P, 4, N], where=early)
                        dense(feature_rows(w.chunks("wq", KC), xT, qT))
                        dense(head_queries(w.chunks("wkT", 4), qT, q, HP))
                    cross_attention(q, HP ** -0.5, dram["zT"], dram["z"], affine=(w("lny_g"), w("lny_b")))
                    oT = sb("oT", [P, 4, N], where=tmp)
                    dense(head_values(w("wv"), q, oT, HP))
                    tail("a2", w, oT)
                return own.pop_all(), inner, mid

        def head_queries(wkT, qT, q, dh):
            per = P // dh
            return [([(wkT[dh * (h % per):dh * (h % per + 1), h // per, :],
                       qT[dh * (h % per):dh * (h % per + 1), h // per, :])], P, N, either(h), copy_to(q[:, h, :]))
                    for h in range(H)]

        def head_values(wv, q, oT, dh):
            per = P // dh
            return [(("rows", [(dh * j, wv[:, (per * m + j) * dh:(per * m + j + 1) * dh], q[:, per * m + j, :])
                               for j in range(per)]), P, N, either(m), copy_to(oT[:, m, :]))
                    for m in range(H // per)]

        def context_norm(gamma, beta):
            names = ("landed0", "landed1", "chain", "var_ready", "std_ready", "z_ready", "turned_ready", "zT_ready",
                     "z_stored0", "z_stored1", "zT_stored0", "zT_stored1", "cleared")
            with ExitStack() as own, signals(nc, *names) as \
                    (landed0, landed1, chain, var_ready, std_ready, z_ready, turned_ready, zT_ready,
                     z_stored0, z_stored1, zT_stored0, zT_stored1, cleared):
                landed, z_stored, zT_stored = (landed0, landed1), (z_stored0, z_stored1), (zT_stored0, zT_stored1)
                raw = sb("raw", [P, 2, KCH, CD], where=own)
                z = sb("z", [P, 2, KCH, CD], where=own)
                zT = sb("zT", [P, 2, KPAD], where=own)
                stats = sb("stats", [P, KCH, 6], where=own)
                means = sb("means", [P, KCH], where=own)
                apart = sb("apart", [P, KCH], where=own)
                dev = sb("dev", [P, KCH], where=own)
                rdev = sb("rdev", [P, KCH], where=own)
                steps = B // 2
                with nc.Block() as block:
                    @block.gpsimd
                    def _(pool):
                        pool.memset(zT[:, :, KEYS:KPAD], 0.0).then_inc(cleared, 1)

                    @block.sync
                    def _(sp):
                        def fetch(step, i):
                            sp.dma_start(raw[:, i], dram["ctx"][bass.ds(2 * step + i, 1)]
                                         .rearrange("b p (k d) -> (b p) k d", d=CD)).then_inc(landed[i], 16)

                        def store(step, i):
                            b = 2 * step + i
                            sp.wait_ge(z_ready, b + 1)
                            sp.dma_start(dram["z"][bass.ds(b, 1)].rearrange("b p (k d) -> (b p) k d", d=CD), z[:, i])\
                                .then_inc(z_stored[i], 16)
                            sp.wait_ge(zT_ready, 4 * b + 4)
                            sp.dma_start(dram["zT"][bass.ds(b, 1)].rearrange("b p k -> (b p) k"), zT[:, i, 0:KEVEN])\
                                .then_inc(zT_stored[i], 16)
                        fetch(0, 0)
                        fetch(0, 1)
                        sp.wait_ge(cleared, 1)
                        with sp.Fori(0, steps - 1) as step:
                            for i in range(2):
                                store(step, i)
                                fetch(step + 1, i)
                        for i in range(2):
                            store(steps - 1, i)
                        for i in range(2):
                            sp.wait_ge(z_stored[i], 16 * steps)
                            sp.wait_ge(zT_stored[i], 16 * steps)

                    @block.vector
                    def _(dve):
                        def one(step, i, first):
                            b = 2 * step + i
                            dve.wait_ge(landed[i], 16 * step + 16)
                            for k in range(KCH):
                                last = dve.bn_stats(stats[:, k, :], raw[:, i, k, :])
                            last.then_inc(chain, 1)
                            dve.wait_ge(chain, 7 * b + 1)
                            dve.tensor_tensor(apart[:], stats[:, :, 1], stats[:, :, 4], ALU.subtract)
                            dve.tensor_tensor(means[:], stats[:, :, 1], stats[:, :, 4], ALU.add)
                            dve.tensor_tensor(dev[:], stats[:, :, 2], stats[:, :, 5], ALU.add).then_inc(chain, 1)
                            dve.wait_ge(chain, 7 * b + 2)
                            dve.tensor_scalar(means[:], means[:], 0.5, None, ALU.mult)
                            dve.tensor_scalar(dev[:], dev[:], 1.0 / CD, EPS, ALU.mult, ALU.add)
                            dve.scalar_tensor_tensor(out=apart[:], in0=apart[:], scalar=0.25, in1=apart[:],
                                                     op0=ALU.mult, op1=ALU.mult).then_inc(chain, 1)
                            dve.wait_ge(chain, 7 * b + 3)
                            dve.tensor_tensor(dev[:], dev[:], apart[:], ALU.add).then_inc(var_ready, 1)
                            dve.wait_ge(std_ready, b + 1)
                            dve.reciprocal(rdev[:], dev[:]).then_inc(chain, 4)
                            dve.wait_ge(chain, 7 * b + 7)
                            if not first:
                                dve.wait_ge(z_stored[i], 16 * step)
                                dve.wait_ge(turned_ready, 4 * b - 4)
                            for k in range(KCH):
                                last = dve.tensor_scalar(z[:, i, k, :], raw[:, i, k, :], means[:, k:k + 1],
                                                         rdev[:, k:k + 1], ALU.subtract, ALU.mult)
                            last.then_inc(z_ready, 1)
                        one(0, 0, True)
                        one(0, 1, True)
                        with dve.Fori(1, steps) as step:
                            one(step, 0, False)
                            one(step, 1, False)

                    @block.tensor
                    def _(pe):
                        def one(step, i, first):
                            b = 2 * step + i
                            pe.wait_ge(z_ready, b + 1)
                            for g in range(4):
                                if not first:
                                    pe.wait_ge(zT_ready, 4 * b - 8 + g + 1)
                                for k in range(4 * g, min(4 * g + 4, KCH)):
                                    rows = P if k < KCH - 1 else KLAST
                                    last = pe.transpose(ps[:, 4 * i + g, (k % 4) * P:(k % 4) * P + rows],
                                                        z[0:rows, i, k, :], ident[0:rows, 0:rows])
                                last.then_inc(turned_ready, 1)
                        one(0, 0, True)
                        one(0, 1, True)
                        with pe.Fori(1, steps) as step:
                            one(step, 0, False)
                            one(step, 1, False)

                    @block.scalar
                    def _(act):
                        def one(step, i, first):
                            b = 2 * step + i
                            act.wait_ge(var_ready, b + 1)
                            nc.scalar.activation(dev[:], dev[:], ACT.Sqrt).then_inc(std_ready, 1)
                            if not first:
                                act.wait_ge(zT_stored[i], 16 * step)
                            for g in range(4):
                                w = min(BANK, KEYS - g * BANK)
                                act.wait_ge(turned_ready, 4 * b + g + 1)
                                nc.scalar.activation(zT[:, i, g * BANK:g * BANK + w], ps[:, 4 * i + g, 0:w],
                                                     ACT.Identity, bias=beta, scale=gamma).then_inc(zT_ready, 1)
                        one(0, 0, True)
                        one(0, 1, True)
                        with act.Fori(1, steps) as step:
                            one(step, 0, False)
                            one(step, 1, False)

        def inner_attention(name, rotary, biases, out_row, finish):
            weights_here(name)
            w = weights(name)
            with ExitStack() as tmp:
                qT = sb("qT", [P, 4, N], where=tmp)
                kT = sb("kT", [P, 4, N], where=tmp)
                v = sb("v", [P, NT, H * HP], where=tmp)
                oT = sb("oT", [P, 4, N], where=tmp)
                values = token_rows(xT, w.chunks("wv", KC), lambda t: copy_to(v[:, t, :]),
                                    row=w("bv", 1) if biases else None, width=H * HP, engine="both")
                if rotary:
                    with ExitStack() as early:
                        qs = sb("qs", [P, 4, N], where=early)
                        ks = sb("ks", [P, 4, N], where=early)
                        dense(rotary_rows(w, "wq", qT, qs, biases) + rotary_rows(w, "wk", kT, ks, biases) + values)
                        vector_steps([lambda dve: dve.tensor_tensor(qT[:], qT[:], qs[:], ALU.add),
                                      lambda dve: dve.tensor_tensor(kT[:], kT[:], ks[:], ALU.add)])
                else:
                    dense(feature_rows(w.chunks("wq", KC), xT, qT, w("bq")) + feature_rows(w.chunks("wk", KC), xT, kT, w("bk"))
                          + values)
                self_attention(qT, kT, v, oT, (D // H) ** -0.5)
                dense(token_rows(oT, w.chunks("wo", 4), finish, row=w(out_row, 1)))

        def many_head_cross(name, dh, scale, row):
            weights_here(name)
            w = weights(name)
            per = H * dh // P
            with ExitStack() as tmp:
                q = sb("q", [P, H, N], where=tmp)
                with ExitStack() as early:
                    qT = sb("qT", [P, per, N], where=early)
                    dense(feature_rows(w.chunks("wq", KC), xT, qT))
                    dense(head_queries(w.chunks("wkT", per), qT, q, dh))
                cross_attention(q, scale, dram["ctxT"], dram["ctx"])
                oT = sb("oT", [P, per, N], where=tmp)
                dense(head_values(w("wv"), q, oT, dh))
                dense(token_rows(oT, w.chunks("wo", per), add_to_x, row=w("bo", 1) if row else None))

        def one_head_cross():
            weights_here("l1x")
            w = weights("l1x")
            with ExitStack() as tmp:
                q = sb("q", [P, N], where=tmp)
                qT = sb("qT", [P, KC, N], where=tmp)
                term = sb("term", [S, B], where=tmp)
                dense(feature_rows(w.chunks("wq", KC), xT, qT, w("bq")))
                wkT = w.chunks("wkT", KC)
                bk = w("bk")
                dense([([(wkT[:, k, :], qT[:, k, :]) for k in range(KC)], P, N, "act", copy_to(q[:]))] +
                      [([(qT[:, k, b * S:(b + 1) * S], bk[:, k:k + 1]) for k in range(KC)], S, 1, "dve",
                        copy_to(term[:, b:b + 1])) for b in range(B)])
                one_head_attention(q, term)
                wv = w("wv").rearrange("p (k n) -> p k n", k=1)
                dense(token_rows(q[:].rearrange("p (k n) -> p k n", k=1), wv, add_to_x, row=w("bv", 1)))

        def recurrence():
            weights_here("l1a")
            w = weights("l1a")
            with ExitStack() as tmp:
                mixed = sb("mixed", [P, 3, KC, N], where=tmp)
                rest = sb("rest", [P, 3, KC], where=tmp)
                decay = sb("decay", [P, KC], where=tmp)
                ndecay = sb("ndecay", [P, KC], where=tmp)
                k = sb("k", [P, KC, N], where=tmp)
                v = sb("v", [P, KC, N], where=tmp)
                r = sb("r", [P, KC, N], where=tmp)
                mix = w("mix").rearrange("p (m k) -> p m k", k=KC)
                with signals(nc, "chain", "decay_ready", "part_ready") as (chain, decay_ready, part_ready), \
                        nc.Block() as block:
                    @block.vector
                    def _(dve):
                        link = Chain(dve, chain)
                        link(dve.tensor_scalar(rest[:], mix, -1.0, 1.0, ALU.mult, ALU.add))
                        for m in range(3):
                            for c in range(KC):
                                last = dve.tensor_scalar(mixed[:, m, c, :], xT[:, c, :], mix[:, m, c:c + 1], None,
                                                         ALU.mult)
                        link(last)
                        for m in range(3):
                            for c in range(KC):
                                here = mixed[:, m, c, :].rearrange("p (b s) -> p b s", s=S)
                                before = xT[:, c, :].rearrange("p (b s) -> p b s", s=S)
                                last = dve.scalar_tensor_tensor(
                                    out=here[:, :, 1:S], in0=before[:, :, 0:S - 1], scalar=rest[:, m, c:c + 1],
                                    in1=here[:, :, 1:S], op0=ALU.mult, op1=ALU.add)
                        link(last)
                        dve.wait_ge(decay_ready, 1)
                        link(dve.tensor_scalar(ndecay[:], decay[:], -1.0, None, ALU.mult))

                    @block.scalar
                    def _(act):
                        nc.scalar.activation(decay[:], w("decay"), ACT.Exp).then_inc(decay_ready, 1)
                dense(feature_rows(w.chunks("wk", KC), mixed[:, 0], k) + feature_rows(w.chunks("wv", KC), mixed[:, 1], v)
                      + [(terms, rows, cols, "act", activated(r[:, m, :], ACT.Sigmoid)) for m, (terms, rows, cols, _, _)
                         in enumerate(feature_rows(w.chunks("wr", KC), mixed[:, 2], r))])

                fall = sb("fall", [P, KC, N], where=tmp)
                top = sb("top", [P, KC, N + 1], where=tmp)
                keep = sb("keep", [P, KC, N], where=tmp)
                new = sb("new", [P, KC, N], where=tmp)
                num = sb("num", [P, KC, N + 1], where=tmp)
                den = sb("den", [P, KC, N + 1], where=tmp)
                peak = mixed[:, 0]
                boost = mixed[:, 1]
                e_old = mixed[:, 2]

                def split(t):
                    return t.rearrange("p k (b s) -> p k b s", s=S)

                with signals(nc, "chain", "arguments", "exponents") as (chain, arguments, exponents), nc.Block() as block:
                    @block.scalar
                    def _(act):
                        act.wait_ge(arguments, 1)
                        nc.scalar.activation(keep[:], keep[:], ACT.Exp).then_inc(exponents, 1)
                        nc.scalar.activation(new[:], new[:], ACT.Exp).then_inc(exponents, 1)
                        act.wait_ge(arguments, 2)
                        nc.scalar.activation(e_old, e_old, ACT.Exp).then_inc(exponents, 1)
                        nc.scalar.activation(boost, boost, ACT.Exp).then_inc(exponents, 1)

                    @block.vector
                    def _(dve):
                        link = Chain(dve, chain)
                        link(dve.memset(fall[:], 0.0))
                        for c in range(KC):
                            last = dve.tensor_scalar(fall[:, c, :], fall[:, c, :], ndecay[:, c:c + 1], None, ALU.add)
                        link(last)
                        link(dve.memset(split(fall[:])[:, :, :, 0:1], -1e38))
                        for c in range(KC):
                            last = dve.tensor_tensor_scan(top[:, c, 1:N + 1], fall[:, c, :], k[:, c, :], 0.0,
                                                          ALU.add, ALU.max)
                        link(last)
                        link(dve.tensor_tensor(new[:], k[:], top[:, :, 1:N + 1], ALU.subtract))
                        link(dve.memset(top[:, :, 0:1], -1e38))
                        link(dve.tensor_tensor(keep[:], fall[:], top[:, :, 0:N], ALU.add))
                        link(dve.memset(split(keep[:])[:, :, :, 0:1], -1e38))
                        link(dve.tensor_tensor(keep[:], keep[:], top[:, :, 1:N + 1], ALU.subtract))
                        dve.sem_inc(arguments, 1)
                        dve.wait_ge(exponents, 2)
                        for c in range(KC):
                            last = dve.tensor_tensor_scan(den[:, c, 1:N + 1], keep[:, c, :], new[:, c, :], 0.0,
                                                          ALU.mult, ALU.add)
                        link(last)
                        link(dve.tensor_tensor(new[:], new[:], v[:], ALU.mult))
                        for c in range(KC):
                            last = dve.tensor_tensor_scan(num[:, c, 1:N + 1], keep[:, c, :], new[:, c, :], 0.0,
                                                          ALU.mult, ALU.add)
                        link(last)
                        link(dve.memset(top[:, :, 0:N:S], -1e38))
                        link(dve.memset(num[:, :, 0:N:S], 0.0))
                        link(dve.memset(den[:, :, 0:N:S], 0.0))
                        for c in range(KC):
                            last = dve.tensor_scalar(boost[:, c, :], k[:, c, :], w("first")[:, c:c + 1], None, ALU.add)
                        link(last)
                        link(dve.tensor_tensor(peak, boost, top[:, :, 0:N], ALU.max))
                        link(dve.tensor_tensor(e_old, top[:, :, 0:N], peak, ALU.subtract))
                        link(dve.tensor_tensor(boost, boost, peak, ALU.subtract))
                        dve.sem_inc(arguments, 1)
                        dve.wait_ge(exponents, 4)
                        link(dve.tensor_tensor(num[:, :, 0:N], num[:, :, 0:N], e_old, ALU.mult))
                        link(dve.tensor_tensor(den[:, :, 0:N], den[:, :, 0:N], e_old, ALU.mult))
                        link(dve.tensor_tensor(den[:, :, 0:N], den[:, :, 0:N], boost, ALU.add))
                        link(dve.tensor_tensor(boost, boost, v[:], ALU.mult))
                        link(dve.tensor_tensor(num[:, :, 0:N], num[:, :, 0:N], boost, ALU.add))
                        link(dve.reciprocal(keep[:], den[:, :, 0:N]))
                        link(dve.tensor_tensor(keep[:], keep[:], r[:], ALU.mult))
                        link(dve.tensor_tensor(keep[:], keep[:], num[:, :, 0:N], ALU.mult))
                dense(token_rows(keep, w.chunks("wo", KC), add_to_x))

        def capacity_experts():
            weights_here("l1f")
            w = weights("l1f")
            E, F, CAP = 8, 1024, 2 * N // 8
            FCH = F // P
            assert CAP == P
            with ExitStack() as own:
                logits = sb("logits", [P, NT, E], where=own)
                combine = sb("combine", [P, E * NT], where=own)
                picked = sb("picked", [P, NT, E], where=own)
                rank = sb("rank", [P, NT, E], where=own)
                place = sb("place", [P, NT, E, P], where=own)
                shareT = sb("shareT", [P, E, N], where=own)
                taken = sb("taken", [P, KC, E * P], where=own)
                y = sb("y", [P, E, D], where=own)
                dense(token_rows(xT, w.chunks("router", KC), lambda t: copy_to(logits[:, t, :]), width=E))
                route(logits[:], E, combine, "all", picked=picked[:])
                dense([([(w("ones"), picked[:, u, :]) for u in range(t)] + [(w("earlier"), picked[:, t, :])],
                        P, E, "dve", copy_to(rank[:, t, :])) for t in range(NT)])

                def one_hot(scalar):
                    steps = []
                    for t in range(NT):
                        for e in range(E):
                            steps.append((t, e, scalar(t, e)))
                    with signals(nc, "placed") as (placed,), nc.Block() as block:
                        @block.vector
                        def _(dve):
                            for t, e, s in steps:
                                dve.tensor_scalar(place[:, t, e, :], iota[:], rank[:, t, e:e + 1], s,
                                                  ALU.is_equal, ALU.mult).then_inc(placed, 1)
                            dve.wait_ge(placed, len(steps))
                one_hot(lambda t, e: picked[:, t, e:e + 1])
                dense([([(xn[:, t, c * P:(c + 1) * P],
                          place[:, t, 4 * g:4 * g + 4, :].rearrange("p e s -> p (e s)")) for t in range(NT)],
                        P, BANK, either(g), copy_to(taken[:, c, g * BANK:(g + 1) * BANK]))
                       for c in range(KC) for g in range(2)])
                one_hot(lambda t, e: combine[:, e * NT + t:e * NT + t + 1])
                dense([((None, [place[:, t, e, :] for t in range(NT)]), P, N, either(e), copy_to(shareT[:, e, :]))
                       for e in range(E)])

                names = ("w1_landed0", "w1_landed1", "w2_landed0", "w2_landed1", "raw_ready", "hidden_ready",
                         "y_ready", "y_kept")
                with ExitStack() as inner, signals(nc, *names) as \
                        (w1_landed0, w1_landed1, w2_landed0, w2_landed1, raw_ready, hidden_ready, y_ready, y_kept):
                    w1_landed, w2_landed = (w1_landed0, w1_landed1), (w2_landed0, w2_landed1)
                    w1 = sb("w1", [P, 2, KC, F], where=inner)
                    w2 = sb("w2", [P, 2, FCH, D], where=inner)
                    hid = sb("hid", [P, 2, FCH, P], where=inner)
                    with nc.Block() as block:
                        @block.sync
                        def _(sp):
                            for e in range(E):
                                i = e % 2
                                if e >= 2:
                                    sp.wait_ge(raw_ready, 2 * (e - 1))
                                sp.dma_start(w1[:, i], dram["l1f_w1"][e].rearrange("p (k f) -> p k f", k=KC))\
                                    .then_inc(w1_landed[i], 16)
                                if e >= 2:
                                    sp.wait_ge(y_ready, e - 1)
                                sp.dma_start(w2[:, i], dram["l1f_w2"][e].rearrange("p (k f) -> p k f", k=FCH))\
                                    .then_inc(w2_landed[i], 16)

                        @block.tensor
                        def _(pe):
                            def first_product(e):
                                i = e % 2
                                pe.wait_ge(w1_landed[i], 16 * (e // 2 + 1))
                                for g in range(2):
                                    if e >= 2:
                                        pe.wait_ge(hidden_ready, 2 * (e - 2) + g + 1)
                                    for m in range(4 * g, 4 * g + 4):
                                        for c in range(KC):
                                            last = pe.matmul(ps[:, 2 * i + g, (m % 4) * P:(m % 4 + 1) * P],
                                                             w1[:, i, c, m * P:(m + 1) * P],
                                                             taken[:, c, e * P:(e + 1) * P],
                                                             start=(c == 0), stop=(c == KC - 1))
                                    last.then_inc(raw_ready, 1)

                            def second_product(e):
                                i = e % 2
                                pe.wait_ge(w2_landed[i], 16 * (e // 2 + 1))
                                pe.wait_ge(hidden_ready, 2 * (e + 1))
                                if e >= 2:
                                    pe.wait_ge(y_kept, e - 1)
                                for m in range(FCH):
                                    last = pe.matmul(ps[:, 4 + i, 0:D], hid[:, i, m, :], w2[:, i, m, :],
                                                     start=(m == 0), stop=(m == FCH - 1))
                                last.then_inc(y_ready, 1)

                            first_product(0)
                            for e in range(E):
                                if e + 1 < E:
                                    first_product(e + 1)
                                second_product(e)

                        @block.scalar
                        def _(act):
                            for e in range(E):
                                i = e % 2
                                for g in range(2):
                                    act.wait_ge(raw_ready, 2 * e + g + 1)
                                    if e >= 2:
                                        act.wait_ge(y_ready, e - 1)
                                    nc.scalar.activation(hid[:, i, 4 * g:4 * g + 4, :],
                                                         ps[:, 2 * i + g, :].rearrange("p (m s) -> p m s", s=P),
                                                         ACT.Gelu_apprx_tanh).then_inc(hidden_ready, 1)

                        @block.vector
                        def _(dve):
                            for e in range(E):
                                dve.wait_ge(y_ready, e + 1)
                                dve.tensor_copy(y[:, e, :], ps[:, 4 + e % 2, 0:D]).then_inc(y_kept, 1)
                dense([([(shareT[:, e, t * P:(t + 1) * P], y[:, e, :]) for e in range(E)] + [(ones[0:1, :], w("bias", 1))],
                        P, D, "dve", add_to_x(t)) for t in range(NT)])

        def gated_experts(name, routed, total, hidden, kind, bias=False):
            weights_here(name)
            w = weights(name)
            with ExitStack() as own:
                combine = sb("combine", [P, total * NT], where=own)
                width = routed + (kind == "share")
                logits = sb("logits", [P, NT, width], where=own)
                dense(token_rows(xT, w.chunks("router", KC), lambda t: copy_to(logits[:, t, :]), width=width))
                route(logits[:, :, 0:routed], routed, combine, kind)
                shared = combine[:, routed * NT:total * NT].rearrange("p (e t) -> p e t", t=NT)
                with signals(nc, "chain", "gate_ready") as (chain, gate_ready), nc.Block() as block:
                    if kind == "share":
                        @block.scalar
                        def _(act):
                            nc.scalar.activation(std[:], logits[:, :, routed], ACT.Sigmoid).then_inc(gate_ready, 1)

                    @block.vector
                    def _(dve):
                        link = Chain(dve, chain)
                        if kind == "share":
                            dve.wait_ge(gate_ready, 1)
                            link(dve.tensor_copy(shared, std[:].unsqueeze(1).broadcast_to([P, total - routed, NT])))
                        else:
                            link(dve.memset(shared, 1.0))
                experts(dram[name + "_guide"], dram[name + "_down"], total, hidden, combine, bias)

        if LAYERS >= 1:
            held, inner, mid = two_attentions()
            pending = [inner, mid]
        else:
            held, pending = ExitStack(), []
        if LAYERS >= 2:
            normalise(x, xn, [(xT, None, None)], add=pending)
            weights_used = weights("l0a")
            inner_attention("l0a", True, True, "bo", lambda t: plus(mid[:, t, :], xn[:, t, :]))
            normalise(mid, inner, affine=(weights_used("gamma"), weights_used("beta")))
            pending = [inner]
        with held:
            if LAYERS == 2 or LAYERS == 1:
                normalise(x, xn, add=pending)
            if LAYERS >= 3:
                normalise(x, xn, [(xT, None, None)], add=pending)
        if LAYERS >= 3:
            gated_experts("l0f", 8, 10, 352, "pair")
        if LAYERS >= 4:
            normalise(x, xn, [(xT, None, None)])
            one_head_cross()
        if LAYERS >= 5:
            normalise(x, xn, [(xT, None, None)])
            recurrence()
        if LAYERS >= 6:
            normalise(x, xn, [(xT, None, None)])
            capacity_experts()
        if LAYERS >= 7:
            normalise(x, xn, [(xT, None, None)])
            many_head_cross("l2x", 64, 64 ** -0.5, True)
        if LAYERS >= 8:
            normalise(x, xn, [(xT, None, None)])
            inner_attention("l2a", True, False, "bu", add_to_x)
        if LAYERS >= 9:
            normalise(x, xn, [(xT, None, None)])
            gated_experts("l2f", 8, 9, 256, "all", bias=True)
        if LAYERS >= 10:
            normalise(x, xn, [(xT, None, None)])
            many_head_cross("l3x", HP, (D // H) ** -0.5, False)
        if LAYERS >= 11:
            normalise(x, xn, [(xT, None, None)])
            inner_attention("l3a", False, True, "bd", add_to_x)
        if LAYERS >= 12:
            normalise(x, xn, [(xT, None, None)])
            gated_experts("l3f", 16, 22, 128, "share")

        with signals(nc, "out_stored") as (out_stored,), nc.Block() as block:
            @block.sync
            def _(sp):
                sp.dma_start(out.rearrange("(t p) d -> p t d", p=P), x[:]).then_inc(out_stored, 16)
                sp.wait_ge(out_stored, 16)


def chunked(w):
    k = w.shape[0] // P
    return w.reshape(k, P, -1).transpose(1, 0, 2).reshape(P, -1)


def columns(v):
    return v.reshape(-1, P).T


def row(v):
    out = np.zeros((P, v.size), np.float32)
    out[0] = v.reshape(-1)
    return out


def spread(v):
    return np.broadcast_to(v.reshape(1, -1), (P, v.size))


def pad_heads(w):
    out = np.zeros(w.shape[:-1] + (H, HP), np.float32)
    out[..., 0:D // H] = w.reshape(w.shape[:-1] + (H, D // H))
    return out.reshape(w.shape[:-1] + (H * HP,))


def pad_rows(w):
    return np.ascontiguousarray(pad_heads(w.T).T)


def swapped(w):
    return w.reshape(w.shape[:-1] + (-1, 2))[..., ::-1].reshape(w.shape)


def rotary_tables(per_head):
    half = D // H // 2 if per_head else D // 2
    theta = (np.float32(1.0) / np.float32(10000.0) ** (np.arange(half, dtype=np.float32) / np.float32(half)))
    angle = np.arange(S, dtype=np.float32)[:, None] * theta.astype(np.float32)[None, :]
    pair = np.arange(D) // 2 % half
    sign = np.where(np.arange(D) % 2, 1.0, -1.0).astype(np.float32)
    tables = []
    for t in (np.cos(angle)[:, pair], np.sin(angle)[:, pair] * sign):
        t = chunked(np.ascontiguousarray(pad_heads(t.astype(np.float32)).T))
        tables.append(t[:, 0:S] if per_head else t)
    return tables


def lay_out(a):
    packs = {}

    def heads_last(w):
        return w.transpose(1, 0, 2).reshape(w.shape[1], -1)

    for name, pre in (("a1", "L0_xattn_a1_"), ("a2", "L0_xattn_a2_")):
        g = lambda k: a[pre + k]
        packs[name] = dict(
            wq=chunked(heads_last(g("wq"))), li1_w=chunked(g("li1_w")), li1_b=row(g("li1_b")),
            **{k: columns(g(k)) for k in ("lnx_g", "lnx_b", "lny_g", "lny_b")})
        packs[name + "_mlp"] = dict(
            li2_w=chunked(g("li2_w")), li3_w=chunked(g("li3_w")), li3_b=row(g("li3_b")), li2_b=columns(g("li2_b")),
            ln3_g=columns(g("ln3_g")), ln3_b=columns(g("ln3_b")))
    at = np.arange(S)
    packs["a1"].update(wk=chunked(heads_last(a["L0_xattn_a1_wk"])), wv=chunked(heads_last(a["L0_xattn_a1_wv"])),
                       ln1_g=spread(a["L0_xattn_ln1_g"]), ln1_b=spread(a["L0_xattn_ln1_b"]),
                       later=np.tile((at[None, :] > at[:, None]).astype(np.float32), (2, 1)))
    packs["a2"].update(wkT=chunked(a["L0_xattn_a2_wk"].transpose(0, 2, 1).reshape(H * HP, CD)),
                       wv=heads_last(a["L0_xattn_a2_wv"]),
                       ln2_g=spread(a["L0_xattn_ln2_g"]), ln2_b=spread(a["L0_xattn_ln2_b"]))
    cos, sin = rotary_tables(True)
    wqkv, bqkv = a["L0_attn_Wqkv"], a["L0_attn_bqkv"]
    packs["l0a"] = dict(wv=chunked(pad_heads(wqkv[:, 2 * D:])), bv=row(pad_heads(bqkv[2 * D:])),
                        wo=chunked(pad_rows(a["L0_attn_Wo"])),
                        bo=row(a["L0_attn_bo"]), gamma=spread(a["L0_attn_gamma"]), beta=spread(a["L0_attn_beta"]),
                        cos=cos, sin=sin)
    cos, sin = rotary_tables(False)
    packs["l2a"] = dict(wv=chunked(pad_heads(a["L2_attn_Wv"].T)), wo=chunked(pad_rows(a["L2_attn_Wu"].T)), bu=row(a["L2_attn_bu"]),
                        cos=cos, sin=sin)
    for n, m, b in (("q", wqkv[:, 0:D], bqkv[0:D]), ("k", wqkv[:, D:2 * D], bqkv[D:2 * D])):
        packs["l0a"].update({"w" + n: chunked(pad_heads(m)), f"w{n}_swapped": chunked(pad_heads(swapped(m))),
                             "b" + n: columns(pad_heads(b)), f"b{n}_swapped": columns(pad_heads(swapped(b)))})
        m = a["L2_attn_W" + n].T
        packs["l2a"].update({"w" + n: chunked(pad_heads(m)), f"w{n}_swapped": chunked(pad_heads(swapped(m)))})
    packs["l0f"] = dict(router=chunked(a["L0_ffn_Wg"]))
    packs["l1x"] = dict(wq=chunked(a["L1_xattn_Wq"]), wkT=chunked(a["L1_xattn_Wk"].T), wv=a["L1_xattn_Wv"],
                        bq=columns(a["L1_xattn_bq"]), bk=columns(a["L1_xattn_bk"]), bv=row(a["L1_xattn_bv"]))
    packs["l1a"] = dict(**{"w" + n: chunked(a["L1_attn_W" + n].T) for n in "kvro"},
                        decay=columns(a["L1_attn_time_decay"]), first=columns(a["L1_attn_time_first"]),
                        mix=np.concatenate([columns(a["L1_attn_time_mix_" + n]) for n in "kvr"], 1))
    p = np.arange(P)
    packs["l1f"] = dict(router=chunked(a["L1_ffn_w_router"]), bias=row(a["L1_ffn_bias"]),
                        ones=np.ones((P, P), np.float32), earlier=(p[:, None] < p[None, :]).astype(np.float32))
    packs["l2x"] = dict(wq=chunked(a["L2_xattn_Wq"]), wkT=chunked(a["L2_xattn_Wk"].T), wv=a["L2_xattn_Wv"],
                        wo=chunked(a["L2_xattn_Wo"]), bo=row(a["L2_xattn_bo"]))
    packs["l2f"] = dict(router=chunked(a["L2_ffn_gate_w"].T))
    packs["l3x"] = dict(wq=chunked(pad_heads(a["L3_xattn_Wq"].T)),
                        wkT=chunked(pad_rows(a["L3_xattn_Wkv"][0:D])),
                        wv=pad_heads(a["L3_xattn_Wkv"][D:].T),
                        wo=chunked(pad_rows(a["L3_xattn_Wo"].T)))
    packs["l3a"] = dict(wq=chunked(pad_heads(a["L3_attn_Wq"])), wk=chunked(pad_heads(a["L3_attn_Wk"])),
                        bq=columns(pad_heads(a["L3_attn_bq"])), bk=columns(pad_heads(a["L3_attn_bk"])),
                        wv=chunked(pad_heads(a["L3_attn_Wv"])), bv=row(pad_heads(a["L3_attn_bv"])),
                        wo=chunked(pad_rows(a["L3_attn_Wd"])),
                        bd=row(a["L3_attn_bd"]))
    packs["l3f"] = dict(router=chunked(np.concatenate([a["L3_ffn_gate_w"].T, a["L3_ffn_shared_gate_w"].T], 1)))
    return packs


def guides(gate, up):
    return np.stack([np.concatenate([chunked(g), chunked(u)], 1) for g, u in zip(gate, up)])


def downs(down):
    e, f, d = down.shape
    pad = np.zeros((e, -(-f // P) * P, d), np.float32)
    pad[:, 0:f] = down
    return np.stack([chunked(w) for w in pad])


def expert_arrays(a):
    out = {}
    halves = lambda w: w.reshape(D, 2, -1).transpose(1, 0, 2)
    out["l0f_guide"] = guides(np.concatenate([a["L0_ffn_W1"], halves(a["L0_ffn_Ws1"])]),
                              np.concatenate([a["L0_ffn_W2"], halves(a["L0_ffn_Ws2"])]))
    out["l0f_down"] = downs(np.concatenate([a["L0_ffn_W3"], a["L0_ffn_Ws3"].reshape(2, -1, D)]))
    out["l1f_w1"] = np.stack([chunked(w) for w in a["L1_ffn_w1"]])
    out["l1f_w2"] = np.stack([chunked(w) for w in a["L1_ffn_w2"]])
    g = lambda k: np.concatenate([a["L2_ffn_" + k], a["L2_ffn_s" + k][None]])
    out["l2f_guide"] = np.concatenate([guides(g("w1"), g("w3")), np.stack([columns(b) for b in g("b1")]),
                                       np.stack([columns(b) for b in g("b3")])], 2)
    out["l2f_down"] = np.concatenate([downs(g("w2")), np.stack([row(b) for b in g("b2")])], 2)
    gu = a["L3_ffn_w_gate_up"]
    wide = lambda w: np.concatenate([w, np.zeros((6 * P - w.shape[0], D), np.float32)]).reshape(6, P, D)
    out["l3f_guide"] = guides(
        np.concatenate([gu[:, :, 0:P], wide(a["L3_ffn_shared_w_gate"]).transpose(0, 2, 1)]),
        np.concatenate([gu[:, :, P:], wide(a["L3_ffn_shared_w_up"]).transpose(0, 2, 1)]))
    out["l3f_down"] = downs(np.concatenate([a["L3_ffn_w_down"], wide(a["L3_ffn_shared_w_down"].T)]))
    return out


def kernel(**inputs):
    import concourse.bacc as bacc
    from concourse.bass_utils import run_bass_kernel_spmd

    a = {n: np.asarray(v) for n, v in inputs.items()}
    arrays, fields = {"x": a["x"].reshape(N, D)}, {}
    for name, parts in lay_out(a).items():
        at, place = 0, {}
        for part, v in parts.items():
            place[part] = (at, v.shape[1])
            at += v.shape[1]
        fields[name] = (place, at)
        arrays[name] = np.concatenate(list(parts.values()), 1)
    arrays.update(expert_arrays(a))
    ctx = a["ctx_512"]
    padded = np.zeros((B, KPAD, CD), np.float32)
    padded[:, 0:KEYS] = ctx
    arrays["ctx"] = padded.reshape(B, KCH, P, CD).transpose(0, 2, 1, 3).reshape(B, P, KPAD)
    arrays["ctxT"] = padded[:, 0:KEVEN].transpose(0, 2, 1)
    arrays = {n: np.ascontiguousarray(v) for n, v in arrays.items()}

    nc = bacc.Bacc("TRN2", target_bir_lowering=False, num_devices=1)
    dram = {n: nc.dram_tensor(n + "_in", v.shape, mybir.dt.from_np(v.dtype), kind="ExternalInput").ap()
            for n, v in arrays.items()}
    out = nc.dram_tensor("out", (N, D), F32, kind="ExternalOutput").ap()
    dram["z"] = nc.dram_tensor("z", (B, P, KPAD), F32, kind="Internal").ap()
    dram["zT"] = nc.dram_tensor("zT", (B, P, KEVEN), F32, kind="Internal").ap()
    perceiver_kernel(nc, dram, fields, out)
    r = run_bass_kernel_spmd(nc, [{n + "_in": v for n, v in arrays.items()}], core_ids=[0])
    return r.results[0]["out"].reshape(B, S, D)
```
